# Optimizing a Trainium2 kernel written in Bass

```python
import numpy as np
import jax
import jax.numpy as jnp

def _softmax(x, axis=-1):
    return jax.nn.softmax(x, axis=axis)

def _gelu(x):
    return jax.nn.gelu(x, approximate=True)

def _silu(x):
    return jax.nn.silu(x)

def _sigmoid(x):
    return jax.nn.sigmoid(x)

def _layernorm(x, axis=-1, eps=1e-05):
    m = jnp.mean(x, axis=axis, keepdims=True)
    v = jnp.var(x, axis=axis, keepdims=True)
    return (x - m) / jnp.sqrt(v + eps)

def _scatter_add(tgt, idx, src, axis=0):
    return tgt.at[idx].add(src)

def _segment_sum(src, seg, n):
    return jax.ops.segment_sum(src, seg, n)
kernel_name = 'mk_gnn_resnorm_d4_gnn_r8_7703ea'

def setup_inputs(seed: int=0):
    np.random.seed(seed)
    _w = jnp.asarray

    def _rec_inputs():
        import jax
        import jax.numpy as jnp
        _gk = jax.random.key(seed)
        x = -8.776e-05 + 1 * jax.random.normal(jax.random.fold_in(_gk, 1), (1250, 512), jnp.float32)
        src = jax.random.randint(jax.random.fold_in(_gk, 2), (20000,), 0, 1250, jnp.int32)
        dst = jnp.minimum((1250 * jax.random.uniform(jax.random.fold_in(_gk, 3), (20000,)) ** 2.0).astype(jnp.int32), 9999)
        _o = jnp.argsort(dst, stable=True)
        src = src[_o]
        dst = dst[_o]
        edge_attr_4 = 0.00171547 + 0.999346 * jax.random.normal(jax.random.fold_in(_gk, 11), (20000, 4), jnp.float32)
        edge_attr_8 = 0.000126197 + 0.999763 * jax.random.normal(jax.random.fold_in(_gk, 12), (20000, 8), jnp.float32)
        edge_type_2 = jax.random.randint(jax.random.fold_in(_gk, 14), (20000,), 0, 2, jnp.int32)
        edge_weight = jax.random.uniform(jax.random.fold_in(_gk, 15), (20000,), jnp.float32, 0.0, 0.999998)
        return (x, src, dst, edge_attr_4, edge_attr_8, edge_type_2, edge_weight)
    x, src, dst, edge_attr_4, edge_attr_8, edge_type_2, edge_weight = _rec_inputs()

    def _L0_gnn_setup():
        import jax, jax.numpy as jnp
        import numpy as np
        MUL = 128
        N_NODES = 1250
        N_EDGES = 20000
        R_BASIS = 8
        HIDDEN = 64
        W_NUMEL = 4 * MUL
        SQRT3 = 3.0 ** 0.5
        SILU_2MOM = 1.679177
        AVG_NUM_NEIGHBORS = 10.0

        def _lin_irreps(x0, x1, W0, W1):
            y0 = x0 @ W0 / jnp.sqrt(jnp.float32(W0.shape[0]))
            y1 = jnp.einsum('num,uv->nvm', x1, W1) / jnp.sqrt(jnp.float32(W1.shape[0]))
            return (y0, y1)

        def _forward(node_feats, edge_attrs, edge_feats, edge_index, W_up0, W_up1, W_mlp1, W_mlp2, W_mlp3, W_mlp4, W_out0, W_out1):
            num_nodes = node_feats.shape[0]
            sender, receiver = (edge_index[0], edge_index[1])
            x0 = node_feats[:, :MUL]
            x1 = node_feats[:, MUL:].reshape(num_nodes, MUL, 3)
            x0, x1 = _lin_irreps(x0, x1, W_up0, W_up1)
            h = edge_feats
            for W in (W_mlp1, W_mlp2, W_mlp3):
                h = SILU_2MOM * jax.nn.silu(h @ W / jnp.sqrt(jnp.float32(W.shape[0])))
            tpw = h @ W_mlp4 / jnp.sqrt(jnp.float32(W_mlp4.shape[0]))
            w1, w2, w3, w4 = jnp.split(tpw, 4, axis=-1)
            s0 = x0[sender]
            s1 = x1[sender]
            y0 = edge_attrs[:, 0:1]
            y1 = edge_attrs[:, 1:4]
            p1 = w1 * s0 * y0
            p2 = (w2 * s0)[:, :, None] * y1[:, None, :]
            p3 = w3[:, :, None] * s1 * y0[:, None, :]
            p4 = w4 * jnp.einsum('eum,em->eu', s1, y1) / SQRT3
            m0 = jnp.concatenate([p1, p4], axis=-1)
            m1 = jnp.concatenate([p2, p3], axis=1)
            msg0 = jax.ops.segment_sum(m0, receiver, num_segments=num_nodes)
            msg1 = jax.ops.segment_sum(m1, receiver, num_segments=num_nodes)
            o0, o1 = _lin_irreps(msg0, msg1, W_out0, W_out1)
            out = jnp.concatenate([o0, o1.reshape(num_nodes, 3 * MUL)], axis=-1)
            return out / AVG_NUM_NEIGHBORS
        key = jax.random.key(seed)
        ks = jax.random.split(key, 12)
        rn = lambda k, s: jax.random.normal(k, s, dtype=jnp.float32)
        return {'node_feats': rn(ks[0], (N_NODES, 4 * MUL)), 'edge_attrs': rn(ks[1], (N_EDGES, 4)), 'edge_feats': rn(ks[2], (N_EDGES, R_BASIS)), 'edge_index': jax.random.randint(ks[3], (2, N_EDGES), 0, N_NODES), 'W_up0': rn(ks[4], (MUL, MUL)), 'W_up1': rn(ks[5], (MUL, MUL)), 'W_mlp1': rn(ks[6], (R_BASIS, HIDDEN)), 'W_mlp2': rn(ks[7], (HIDDEN, HIDDEN)), 'W_mlp3': rn(ks[8], (HIDDEN, HIDDEN)), 'W_mlp4': rn(ks[9], (HIDDEN, W_NUMEL)), 'W_out0': rn(ks[10], (2 * MUL, MUL)), 'W_out1': rn(ks[11], (2 * MUL, MUL))}
    _L0_gnn_all = _L0_gnn_setup()
    _L0_gnn_in = {k: v for k, v in _L0_gnn_all.items() if k in ('W_up0', 'W_up1', 'W_mlp1', 'W_mlp2', 'W_mlp3', 'W_mlp4', 'W_out0', 'W_out1')}
    del _L0_gnn_all

    def _L1_gnn_setup():
        import jax, jax.numpy as jnp
        import numpy as np
        N = 12500
        E = 100000
        IN_FEATS = 512
        N_HIDDEN = 128
        key = jax.random.key(seed)
        k1, k2, k3, k4, k5, k6 = jax.random.split(key, 6)
        inputs = jax.random.normal(k1, (N, IN_FEATS), dtype=jnp.float32)
        edge_index = jax.random.randint(k2, (2, E), 0, N, dtype=jnp.int64)
        edge_attr = jax.random.uniform(k3, (E,), dtype=jnp.float32)
        s_gcn = jnp.sqrt(6.0 / (IN_FEATS + N_HIDDEN)).astype(jnp.float32)
        W_gcn = jax.random.uniform(k4, (IN_FEATS, N_HIDDEN), dtype=jnp.float32, minval=-s_gcn, maxval=s_gcn)
        b_gcn = jnp.zeros((N_HIDDEN,), dtype=jnp.float32)
        s_fc = jnp.sqrt(6.0 / (N_HIDDEN + IN_FEATS)).astype(jnp.float32)
        W_fc = jax.random.uniform(k5, (IN_FEATS, N_HIDDEN), dtype=jnp.float32, minval=-s_fc, maxval=s_fc)
        b_fc = jax.random.uniform(k6, (IN_FEATS,), dtype=jnp.float32, minval=-1.0 / np.sqrt(N_HIDDEN), maxval=1.0 / np.sqrt(N_HIDDEN))
        return {'inputs': inputs, 'edge_index': edge_index, 'edge_attr': edge_attr, 'W_gcn': W_gcn, 'b_gcn': b_gcn, 'W_fc': W_fc, 'b_fc': b_fc}
    _L1_gnn_all = _L1_gnn_setup()
    _L1_gnn_in = {k: v for k, v in _L1_gnn_all.items() if k in ('W_gcn', 'b_gcn', 'W_fc', 'b_fc')}
    del _L1_gnn_all

    def _L2_gnn_setup():
        import jax, jax.numpy as jnp
        import numpy as np
        key = jax.random.key(seed)
        ks = jax.random.split(key, 8)
        n_nodes, n_edges, in_dim, out_dim = (6250, 50000, 512, 512)
        x = jax.random.normal(ks[0], (n_nodes, in_dim), dtype=jnp.float32)
        edge_index = jax.random.randint(ks[1], (2, n_edges), 0, n_nodes, dtype=jnp.int64)
        edge_weight = jax.random.uniform(ks[2], (n_edges,), dtype=jnp.float32)
        s = 1.0 / np.sqrt(in_dim)
        W_self = jax.random.uniform(ks[3], (out_dim, in_dim), minval=-s, maxval=s, dtype=jnp.float32)
        b_self = jax.random.uniform(ks[4], (out_dim,), minval=-s, maxval=s, dtype=jnp.float32)
        W_neigh = jax.random.uniform(ks[5], (out_dim, in_dim), minval=-s, maxval=s, dtype=jnp.float32)
        b_neigh = jax.random.uniform(ks[6], (out_dim,), minval=-s, maxval=s, dtype=jnp.float32)
        return {'x': x, 'edge_index': edge_index, 'edge_weight': edge_weight, 'W_self': W_self, 'b_self': b_self, 'W_neigh': W_neigh, 'b_neigh': b_neigh}
    _L2_gnn_all = _L2_gnn_setup()
    _L2_gnn_in = {k: v for k, v in _L2_gnn_all.items() if k in ('W_self', 'b_self', 'W_neigh', 'b_neigh')}
    del _L2_gnn_all

    def _L3_gnn_setup():
        import jax, jax.numpy as jnp
        import numpy as np
        NUM_RELATIONS = 2
        NUM_BASES = 30
        HIDDEN = 512
        N_NODES = 1250
        N_EDGES = 20000

        def rgcn_gate_layer(x, row, col, edge_type, basis, att, gate_w, root, bias):
            H = x.shape[1]
            w = jnp.einsum('rb,bio->rio', att, basis)
            x_j = x[col]
            msgs = []
            for r in range(NUM_RELATIONS):
                gate = jax.nn.sigmoid(x_j @ gate_w[r, :, 0])
                msgs.append(gate[:, None] * x_j @ w[r])
            msg = jnp.where((edge_type == 0)[:, None], msgs[0], msgs[1])
            agg = jax.ops.segment_sum(msg, row, num_segments=x.shape[0])
            return agg + x @ root + bias
        key = jax.random.key(seed)
        ks = jax.random.split(key, 16)
        H, R, B = (HIDDEN, NUM_RELATIONS, NUM_BASES)
        bound = 1.0 / np.sqrt(B * H)
        u = lambda k, shape: jax.random.uniform(k, shape, jnp.float32, -bound, bound)
        inp = {'x': jax.random.normal(ks[0], (N_NODES, H), jnp.float32), 'edge_index': jax.random.randint(ks[1], (2, N_EDGES), 0, N_NODES, jnp.int32), 'edge_type': jax.random.randint(ks[2], (N_EDGES,), 0, R, jnp.int32), 'basis1': u(ks[3], (B, H, H)), 'att1': u(ks[4], (R, B)), 'gate_w1': u(ks[5], (R, H, 1)), 'root1': u(ks[6], (H, H)), 'bias1': u(ks[7], (H,)), 'basis2': u(ks[8], (B, H, H)), 'att2': u(ks[9], (R, B)), 'gate_w2': u(ks[10], (R, H, 1)), 'root2': u(ks[11], (H, H)), 'bias2': u(ks[12], (H,))}
        return inp
    _L3_gnn_all = _L3_gnn_setup()
    _L3_gnn_in = {k: v for k, v in _L3_gnn_all.items() if k in ('basis1', 'att1', 'gate_w1', 'root1', 'bias1', 'basis2', 'att2', 'gate_w2', 'root2', 'bias2')}
    del _L3_gnn_all
    return {'x': x, 'src': src, 'dst': dst, 'edge_attr_4': edge_attr_4, 'edge_attr_8': edge_attr_8, 'edge_type_2': edge_type_2, 'edge_weight': edge_weight, 'L0_gnn_W_up0': _L0_gnn_in['W_up0'], 'L0_gnn_W_up1': _L0_gnn_in['W_up1'], 'L0_gnn_W_mlp1': _L0_gnn_in['W_mlp1'], 'L0_gnn_W_mlp2': _L0_gnn_in['W_mlp2'], 'L0_gnn_W_mlp3': _L0_gnn_in['W_mlp3'], 'L0_gnn_W_mlp4': _L0_gnn_in['W_mlp4'], 'L0_gnn_W_out0': _L0_gnn_in['W_out0'], 'L0_gnn_W_out1': _L0_gnn_in['W_out1'], 'L1_gnn_W_gcn': _L1_gnn_in['W_gcn'], 'L1_gnn_b_gcn': _L1_gnn_in['b_gcn'], 'L1_gnn_W_fc': _L1_gnn_in['W_fc'], 'L1_gnn_b_fc': _L1_gnn_in['b_fc'], 'L2_gnn_W_self': _L2_gnn_in['W_self'], 'L2_gnn_b_self': _L2_gnn_in['b_self'], 'L2_gnn_W_neigh': _L2_gnn_in['W_neigh'], 'L2_gnn_b_neigh': _L2_gnn_in['b_neigh'], 'L3_gnn_basis1': _L3_gnn_in['basis1'], 'L3_gnn_att1': _L3_gnn_in['att1'], 'L3_gnn_gate_w1': _L3_gnn_in['gate_w1'], 'L3_gnn_root1': _L3_gnn_in['root1'], 'L3_gnn_bias1': _L3_gnn_in['bias1'], 'L3_gnn_basis2': _L3_gnn_in['basis2'], 'L3_gnn_att2': _L3_gnn_in['att2'], 'L3_gnn_gate_w2': _L3_gnn_in['gate_w2'], 'L3_gnn_root2': _L3_gnn_in['root2'], 'L3_gnn_bias2': _L3_gnn_in['bias2']}

def reference(x, src, dst, edge_attr_4, edge_attr_8, edge_type_2, edge_weight, L0_gnn_W_up0, L0_gnn_W_up1, L0_gnn_W_mlp1, L0_gnn_W_mlp2, L0_gnn_W_mlp3, L0_gnn_W_mlp4, L0_gnn_W_out0, L0_gnn_W_out1, L1_gnn_W_gcn, L1_gnn_b_gcn, L1_gnn_W_fc, L1_gnn_b_fc, L2_gnn_W_self, L2_gnn_b_self, L2_gnn_W_neigh, L2_gnn_b_neigh, L3_gnn_basis1, L3_gnn_att1, L3_gnn_gate_w1, L3_gnn_root1, L3_gnn_bias1, L3_gnn_basis2, L3_gnn_att2, L3_gnn_gate_w2, L3_gnn_root2, L3_gnn_bias2):
    import jax
    import jax.numpy as jnp

    def _L0_gnn_ref(node_feats, edge_attrs, edge_feats, edge_index, W_up0, W_up1, W_mlp1, W_mlp2, W_mlp3, W_mlp4, W_out0, W_out1):
        import jax, jax.numpy as jnp
        import numpy as np
        MUL = 128
        N_NODES = 1250
        N_EDGES = 20000
        R_BASIS = 8
        HIDDEN = 64
        W_NUMEL = 4 * MUL
        SQRT3 = 3.0 ** 0.5
        SILU_2MOM = 1.679177
        AVG_NUM_NEIGHBORS = 10.0

        def _lin_irreps(x0, x1, W0, W1):
            y0 = x0 @ W0 / jnp.sqrt(jnp.float32(W0.shape[0]))
            y1 = jnp.einsum('num,uv->nvm', x1, W1) / jnp.sqrt(jnp.float32(W1.shape[0]))
            return (y0, y1)

        def _forward(node_feats, edge_attrs, edge_feats, edge_index, W_up0, W_up1, W_mlp1, W_mlp2, W_mlp3, W_mlp4, W_out0, W_out1):
            num_nodes = node_feats.shape[0]
            sender, receiver = (edge_index[0], edge_index[1])
            x0 = node_feats[:, :MUL]
            x1 = node_feats[:, MUL:].reshape(num_nodes, MUL, 3)
            x0, x1 = _lin_irreps(x0, x1, W_up0, W_up1)
            h = edge_feats
            for W in (W_mlp1, W_mlp2, W_mlp3):
                h = SILU_2MOM * jax.nn.silu(h @ W / jnp.sqrt(jnp.float32(W.shape[0])))
            tpw = h @ W_mlp4 / jnp.sqrt(jnp.float32(W_mlp4.shape[0]))
            w1, w2, w3, w4 = jnp.split(tpw, 4, axis=-1)
            s0 = x0[sender]
            s1 = x1[sender]
            y0 = edge_attrs[:, 0:1]
            y1 = edge_attrs[:, 1:4]
            p1 = w1 * s0 * y0
            p2 = (w2 * s0)[:, :, None] * y1[:, None, :]
            p3 = w3[:, :, None] * s1 * y0[:, None, :]
            p4 = w4 * jnp.einsum('eum,em->eu', s1, y1) / SQRT3
            m0 = jnp.concatenate([p1, p4], axis=-1)
            m1 = jnp.concatenate([p2, p3], axis=1)
            msg0 = jax.ops.segment_sum(m0, receiver, num_segments=num_nodes)
            msg1 = jax.ops.segment_sum(m1, receiver, num_segments=num_nodes)
            o0, o1 = _lin_irreps(msg0, msg1, W_out0, W_out1)
            out = jnp.concatenate([o0, o1.reshape(num_nodes, 3 * MUL)], axis=-1)
            return out / AVG_NUM_NEIGHBORS
        return _forward(node_feats, edge_attrs, edge_feats, edge_index, W_up0, W_up1, W_mlp1, W_mlp2, W_mlp3, W_mlp4, W_out0, W_out1)

    def _L1_gnn_ref(inputs, edge_index, edge_attr, W_gcn, b_gcn, W_fc, b_fc):
        import jax, jax.numpy as jnp
        import numpy as np
        N = 12500
        E = 100000
        IN_FEATS = 512
        N_HIDDEN = 128
        x = inputs @ W_gcn
        src, dst = (edge_index[0], edge_index[1])
        msg = x[src] * edge_attr[:, None]
        h = jax.ops.segment_sum(msg, dst, num_segments=inputs.shape[0]) + b_gcn
        return h @ W_fc.T + b_fc

    def _L2_gnn_ref(x, edge_index, edge_weight, W_self, b_self, W_neigh, b_neigh):
        import jax, jax.numpy as jnp
        import numpy as np
        n_nodes = x.shape[0]
        row, col = (edge_index[0], edge_index[1])
        msg = x[row] * edge_weight[:, None]
        x_neigh = jax.ops.segment_sum(msg, col, num_segments=n_nodes)
        degree = jax.ops.segment_sum(edge_weight, col, num_segments=n_nodes)
        degree = jnp.maximum(degree, 1.0)
        x_neigh = x_neigh / degree[:, None]
        x_self = x @ W_self.T + b_self
        x_neigh = x_neigh @ W_neigh.T + b_neigh
        return x_self + x_neigh

    def _L3_gnn_ref(x, edge_index, edge_type, basis1, att1, gate_w1, root1, bias1, basis2, att2, gate_w2, root2, bias2):
        import jax, jax.numpy as jnp
        import numpy as np
        NUM_RELATIONS = 2
        NUM_BASES = 30
        HIDDEN = 512
        N_NODES = 1250
        N_EDGES = 20000

        def rgcn_gate_layer(x, row, col, edge_type, basis, att, gate_w, root, bias):
            H = x.shape[1]
            w = jnp.einsum('rb,bio->rio', att, basis)
            x_j = x[col]
            msgs = []
            for r in range(NUM_RELATIONS):
                gate = jax.nn.sigmoid(x_j @ gate_w[r, :, 0])
                msgs.append(gate[:, None] * x_j @ w[r])
            msg = jnp.where((edge_type == 0)[:, None], msgs[0], msgs[1])
            agg = jax.ops.segment_sum(msg, row, num_segments=x.shape[0])
            return agg + x @ root + bias
        row, col = (edge_index[0], edge_index[1])
        h = jax.nn.relu(rgcn_gate_layer(x, row, col, edge_type, basis1, att1, gate_w1, root1, bias1))
        out = rgcn_gate_layer(h, row, col, edge_type, basis2, att2, gate_w2, root2, bias2)
        return out
    edge_index = jnp.stack([src, dst])
    x = _layernorm(x + _L0_gnn_ref(x, edge_attr_4, edge_attr_8, edge_index, L0_gnn_W_up0, L0_gnn_W_up1, L0_gnn_W_mlp1, L0_gnn_W_mlp2, L0_gnn_W_mlp3, L0_gnn_W_mlp4, L0_gnn_W_out0, L0_gnn_W_out1), axis=-1)
    x = _layernorm(x + _L1_gnn_ref(x, edge_index, edge_weight, L1_gnn_W_gcn, L1_gnn_b_gcn, L1_gnn_W_fc, L1_gnn_b_fc), axis=-1)
    x = _layernorm(x + _L2_gnn_ref(x, edge_index, edge_weight, L2_gnn_W_self, L2_gnn_b_self, L2_gnn_W_neigh, L2_gnn_b_neigh), axis=-1)
    x = _layernorm(x + _L3_gnn_ref(x, edge_index, edge_type_2, L3_gnn_basis1, L3_gnn_att1, L3_gnn_gate_w1, L3_gnn_root1, L3_gnn_bias1, L3_gnn_basis2, L3_gnn_att2, L3_gnn_gate_w2, L3_gnn_root2, L3_gnn_bias2), axis=-1)
    return x

_drawn_inputs = setup_inputs


def setup_inputs(seed=0):
    import zlib

    import numpy as np

    out = dict(_drawn_inputs(seed))
    spreads = {'L1_gnn_b_gcn': (0.0, 0.1)}
    factors = {'L2_gnn_b_self': 2.669,
     'L3_gnn_basis1': 8.0,
     'L3_gnn_att1': 8.0,
     'L3_gnn_gate_w1': 8.0,
     'L3_gnn_root1': 8.0,
     'L3_gnn_bias1': 8.0,
     'L3_gnn_basis2': 8.0,
     'L3_gnn_att2': 8.0,
     'L3_gnn_gate_w2': 8.0,
     'L3_gnn_root2': 7.22,
     'L3_gnn_bias2': 8.0}
    for name, (base, spread) in spreads.items():
        noise = np.random.default_rng([zlib.crc32(name.encode()), seed]).standard_normal(out[name].shape)
        drawn = base * np.exp(spread * noise) if base else spread * noise
        out[name] = jnp.asarray(drawn.astype(out[name].dtype))
    for name, factor in factors.items():
        out[name] = (out[name] * factor).astype(out[name].dtype)
    return out
```

```python
import concourse.bass as bass
from concourse import mybir
from concourse.alu_op_type import AluOpType as ALU
from contextlib import ExitStack
import math

F32 = mybir.dt.float32
I32 = mybir.dt.int32
I16 = mybir.dt.int16
BF16 = mybir.dt.bfloat16
ACT = mybir.ActivationFunctionType
AX = mybir.AxisListType

NODES, D, EDGES = 1250, 512, 20000
MUL = 128
P = 125
NT = NODES // P
ET = EDGES // P
EH = ET // 2
W = 32
WPAD = NODES + W
BODY = 8
TURNS = ET // BODY
HID, RB = 64, 8
FC = D // 128
BASES, REL = 30, 2
SILU_2MOM = 1.679177
SPANS = [(0, 500), (500, 1000), (1000, 1250)]
IC = 8
ALIGN = 3


def gnn_program(nc, A, out):
    ctx = ExitStack()
    with ctx:
        def sem(name):
            return ctx.enter_context(nc.semaphore(name))

        WORDS = 53100
        arena = ctx.enter_context(nc.sbuf_tensor("arena", [128, WORDS], F32))
        bank = [ctx.enter_context(nc.psum_tensor(f"bank{k}", [128, 512], F32)) for k in range(8)]

        def at(off, words, rows=128, dt=F32):
            assert off + words <= WORDS, (off, words)
            v = arena[0:rows, off:off + words]
            return v if dt == F32 else v.bitcast(dt)

        class Region:
            def __init__(self, lo, hi):
                self.at, self.hi = lo, hi

            def take(self, words, rows=128, dt=F32):
                off = self.at
                self.at += words + (words & 1)
                assert self.at <= self.hi, (self.at, self.hi)
                return at(off, words, rows, dt)

        SMALL = 2200
        AWORDS = NT * WPAD
        R1, R2 = SMALL, SMALL + AWORDS
        R3 = SMALL + 2 * AWORDS
        small = Region(0, SMALL)
        ident = small.take(128)
        onesM = small.take(P, P)
        iota32 = small.take(W, P)
        tab = small.take(3 * ET, 1, I32).rearrange("p (q t) -> p q t", q=3)
        invdeg = small.take(NT, P)
        eps = small.take(1)
        stats = small.take(NT * 6, P).rearrange("p (n s) -> p n s", n=NT)
        mv = small.take(NT * 2, P).rearrange("p (n s) -> p n s", n=NT)
        vare = small.take(NT, P)
        sd = small.take(NT, P)
        rs = small.take(NT, P)
        nt1 = small.take(NT, P)
        nt2 = small.take(NT, P)
        bgcn = small.take(1)
        brow = small.take(D, 1)
        brow2 = small.take(D, 1)

        AT = at(R1, AWORDS, P).rearrange("p (c n) -> p c n", c=NT)
        CNT = at(R2, AWORDS, P, I16).rearrange("p (c n) -> p c n", c=NT)
        accT = at(R3, 8 * WPAD).rearrange("p (b n) -> p b n", b=8)
        edge = Region(R3 + 8 * WPAD, WORDS)
        rel = edge.take(ET, P)
        srcT = edge.take(ET, P)
        idx = edge.take(ET, 128, I32)
        yT = edge.take(4 * ET, P).rearrange("p (t m) -> p t m", m=4)
        valT = edge.take(5 * ET // 2, P, BF16).rearrange("p (t m) -> p t m", m=5)
        edge_mark = edge.at

        hD = nc.dram_tensor("h_scratch", (TURNS, 128, 4 * P), F32, kind="Internal").ap()
        upD = nc.dram_tensor("up_scratch", (NODES, D), F32, kind="Internal").ap()
        wD = nc.dram_tensor("w_scratch", (2, REL * 4, 128, D), F32, kind="Internal").ap()

        ph = Region(R1, R3)
        Lf = ph.take(2 * P * RB, EH).rearrange("p (b x) -> p b x", b=2)
        La = ph.take(2 * P * 4, EH).rearrange("p (b x) -> p b x", b=2)
        Li = ph.take(3 * 2 * P, EH, I32).rearrange("p (q b x) -> p q b x", q=3, b=2)
        Lq = ph.take(4 * 2 * P, EH).rearrange("p (q b x) -> p q b x", q=4, b=2)
        mnx = ph.take(2 * 2, EH).rearrange("p (q b) -> p q b", q=2)
        more = ph.take(2, EH)
        morei = ph.take(2, EH, I32)
        diag = ph.take(4 * EH, EH).rearrange("p (q b x) -> p q b x", q=2, b=2)
        FT = ph.take(ET * RB, P).rearrange("p (c s h j) -> p c s h j", s=4, h=2, j=RB)
        misc = ph.take(4 * ET, P).rearrange("p (q t) -> p q t", q=4)
        base = ph.take(ET, P)
        cum = ph.take(ET, 1)
        kf = ph.take(ET, 1)
        onesr = ph.take(ET, 1)
        wr1 = ph.take(ET, P)
        wr2 = ph.take(ET, P)
        W1b = ph.take(128)
        W2b = ph.take(128)
        W3b = ph.take(128)
        fT = ph.take(4 * 4 * P).rearrange("p (q x) -> p q x", q=4)
        hA = ph.take(4 * 4 * P).rearrange("p (q x) -> p q x", q=4)
        hB = ph.take(4 * 4 * P).rearrange("p (q x) -> p q x", q=4)
        hC = ph.take(4 * 4 * P).rearrange("p (q x) -> p q x", q=4)

        e_ld = sem("e_ld"); e_cst = sem("e_cst"); e_dve = sem("e_dve"); e_tr = sem("e_tr")
        e_bc = sem("e_bc"); e_q = sem("e_q")
        quantities = [(Lf, j, RB) for j in range(RB)] + [(La, m, 4) for m in range(4)] + [(Lq, q, 1) for q in range(4)]

        with nc.Block() as block:
            @block.sync
            def _(sp):
                sp.dma_start(ident, A["ident"]).then_inc(e_ld, 16)
                for q, name in enumerate(("src", "dst", "edge_type_2")):
                    sp.dma_start(Li[:, q], A[name].rearrange("(b p x) -> p b x", b=2, p=EH)).then_inc(e_ld, 16)
                sp.dma_start(Lq[:, 3], A["edge_weight"].rearrange("(b p x) -> p b x", b=2, p=EH)).then_inc(e_ld, 16)
                sp.dma_start(Lf, A["edge_attr_8"].rearrange("(b p x) j -> p b (x j)", b=2, p=EH)).then_inc(e_ld, 16)
                sp.dma_start(La, A["edge_attr_4"].rearrange("(b p x) j -> p b (x j)", b=2, p=EH)).then_inc(e_ld, 16)

            @block.gpsimd
            def _(pool):
                pool.memset(onesM, 1.0).then_inc(e_cst, 1)
                pool.memset(onesr, 1.0).then_inc(e_cst, 1)
                pool.memset(eps, 1e-5).then_inc(e_cst, 1)
                pool.memset(idx, 0).then_inc(e_cst, 1)
                pool.iota(iota32, pattern=[[1, W]], base=0, channel_multiplier=0,
                          allow_small_or_imprecise_dtypes=True).then_inc(e_cst, 1)

            @block.vector
            def _(dve):
                n = [0]

                def link(ins):
                    n[0] += 1
                    ins.then_inc(e_dve, 1)
                    dve.wait_ge(e_dve, n[0])
                dve.wait_ge(e_ld, 7 * 16)
                dve.wait_ge(e_cst, 5)
                link(dve.tensor_copy(Lq[:, 0:3], Li))
                link(dve.tensor_reduce(mnx[:, 0], Lq[:, 1], AX.X, ALU.min))
                link(dve.tensor_reduce(mnx[:, 1], Lq[:, 1], AX.X, ALU.max))
                link(dve.tensor_tensor(more, mnx[:, 1], mnx[:, 0], ALU.subtract))
                link(dve.tensor_copy(morei, more))
                link(dve.tensor_scalar(morei, morei, 5, None, ALU.arith_shift_right))
                link(dve.tensor_copy(more, morei))
                for b in range(2):
                    link(dve.tensor_scalar(diag[:, 0, b], ident[0:EH, 0:EH], mnx[:, 0, b:b + 1], None, ALU.mult))
                    link(dve.tensor_scalar(diag[:, 1, b], ident[0:EH, 0:EH], more[:, b:b + 1], None, ALU.mult))
                dve.sem_inc(e_q, 1)
                for k in range(6):
                    dve.wait_ge(e_tr, k + 1)
                    b, g = k // 3, k % 3
                    ts = slice(b * EH, (b + 1) * EH)
                    for s, (_, j, step) in enumerate(quantities[6 * g:6 * g + 6]):
                        src = bank[k][0:P, s * EH:(s + 1) * EH]
                        if step == RB:
                            dst = FT[:, b * TURNS // 2:(b + 1) * TURNS // 2, :, :, j].rearrange("p c s h -> p c h s")
                            src = src.rearrange("p (c h s) -> p c h s", h=2, s=4)
                        elif step == 4:
                            dst = yT[:, ts, j]
                        else:
                            dst = misc[:, j, ts]
                        link(dve.tensor_copy(dst, src))
                dve.wait_ge(e_bc, 1)
                link(dve.tensor_copy(base, bank[6][0:P, 0:ET]))
                link(dve.tensor_tensor(rel, misc[:, 1], base, ALU.subtract))
                link(dve.tensor_copy(srcT, misc[:, 0]))
                link(dve.tensor_copy(idx[0:P], misc[:, 0]))
                link(dve.tensor_copy(tab[:, 0], base[0:1]))
                link(dve.tensor_copy(kf, bank[6][0:1, ET:2 * ET]))
                link(dve.tensor_copy(tab[:, 1], kf))
                link(dve.tensor_tensor_scan(cum, onesr, kf, 0.0, ALU.mult, ALU.add))
                link(dve.tensor_tensor(cum, cum, kf, ALU.subtract))
                link(dve.tensor_copy(tab[:, 2], cum))
                link(dve.tensor_copy(valT[:, :, 2], misc[:, 3]))
                link(dve.tensor_tensor(wr1, misc[:, 3], valT[:, :, 2], ALU.subtract))
                link(dve.tensor_copy(valT[:, :, 0], wr1))
                link(dve.tensor_tensor(wr2, wr1, valT[:, :, 0], ALU.subtract))
                link(dve.tensor_copy(valT[:, :, 1], wr2))
                link(dve.tensor_scalar(valT[:, :, 3], misc[:, 2], 0.0, None, ALU.is_equal))
                link(dve.tensor_scalar(valT[:, :, 4], misc[:, 2], 0.0, None, ALU.not_equal))

            @block.tensor
            def _(pe):
                pe.wait_ge(e_q, 1)
                pe.wait_ge(e_dve, 11)
                for k in range(6):
                    b, g = k // 3, k % 3
                    for s, (Lx, j, step) in enumerate(quantities[6 * g:6 * g + 6]):
                        if step == 1:
                            in_ = Lx[:, j, b, :]
                        else:
                            in_ = Lx[:, b, :].rearrange("p (x j) -> p j x", j=step)[:, j, :]
                        last = pe.transpose(bank[k][0:P, s * EH:(s + 1) * EH], in_, ident[0:EH, 0:EH])
                    last.then_inc(e_tr, 1)
                for q in range(2):
                    for b in range(2):
                        last = pe.matmul(bank[6][0:P, q * ET + b * EH:q * ET + (b + 1) * EH],
                                         onesM[0:EH, :], diag[:, q, b], start=True, stop=True)
                last.then_inc(e_bc, 1)

        m_ld = sem("m_ld"); m_z = sem("m_z"); m_t = sem("m_t"); m_f = sem("m_f"); m_mm = sem("m_mm"); m_h = sem("m_h")
        m_st = [sem(f"m_st{q}") for q in range(4)]
        GROUPS = TURNS // 4
        layer_in = [fT, hA, hB]
        layer_out = [hA, hB, hC]
        layer_w = [W1b, W2b, W3b]
        scales = [1.0 / math.sqrt(RB), SILU_2MOM / math.sqrt(HID), SILU_2MOM / math.sqrt(HID)]
        with nc.Block() as block:
            @block.sync
            def _(sp):
                sp.wait_ge(m_z, 3)
                for half in range(2):
                    k, c = slice(half * RB, (half + 1) * RB), slice(half * HID, (half + 1) * HID)
                    sp.dma_start(W1b[k, c], A["L0_gnn_W_mlp1"]).then_inc(m_ld, 16)
                    sp.dma_start(W2b[c, c], A["L0_gnn_W_mlp2"]).then_inc(m_ld, 16)
                    sp.dma_start(W3b[c, c], A["L0_gnn_W_mlp3"]).then_inc(m_ld, 16)
                for g in range(GROUPS):
                    for q in range(4):
                        sp.wait_ge(m_h, g * 12 + 8 + q + 1)
                        sp.dma_start(hD[g * 4 + q], hC[:, q]).then_inc(m_st[q], 16)
                for q in range(4):
                    sp.wait_ge(m_st[q], 16 * GROUPS)

            @block.gpsimd
            def _(pool):
                for w in layer_w:
                    pool.memset(w, 0.0).then_inc(m_z, 1)

            @block.vector
            def _(dve):
                for g in range(GROUPS):
                    for q in range(4):
                        dve.wait_ge(m_t, g * 4 + q + 1)
                        if g:
                            dve.wait_ge(m_mm, (g - 1) * 12 + q + 1)
                        dve.tensor_copy(fT[0:2 * RB, q], bank[q][0:2 * RB, 0:4 * P]).then_inc(m_f, 1)

            @block.tensor
            def _(pe):
                pe.wait_ge(m_ld, 6 * 16)
                for g in range(GROUPS):
                    for q in range(4):
                        c = g * 4 + q
                        if g:
                            pe.wait_ge(m_f, (g - 1) * 4 + q + 1)
                        for s in range(4):
                            last = pe.transpose(bank[q][0:2 * RB, s * P:(s + 1) * P],
                                                FT[:, c, s].rearrange("p h j -> p (h j)"), ident[0:P, 0:P])
                        last.then_inc(m_t, 1)
                    for layer in range(3):
                        for q in range(4):
                            if layer == 0:
                                pe.wait_ge(m_f, g * 4 + q + 1)
                                if g:
                                    pe.wait_ge(m_h, (g - 1) * 12 + 8 + q + 1)
                                k = 2 * RB
                            else:
                                pe.wait_ge(m_h, g * 12 + (layer - 1) * 4 + q + 1)
                                k = 128
                            pe.matmul(bank[4 + q][:, 0:4 * P], layer_w[layer][0:k], layer_in[layer][0:k, q],
                                      start=True, stop=True).then_inc(m_mm, 1)

            @block.scalar
            def _(act):
                for g in range(GROUPS):
                    for layer in range(3):
                        for q in range(4):
                            act.wait_ge(m_mm, g * 12 + layer * 4 + q + 1)
                            if layer == 2 and g:
                                act.wait_ge(m_st[q], 16 * g)
                            act.activation(layer_out[layer][:, q], bank[4 + q][:, 0:4 * P], ACT.Silu,
                                           scale=scales[layer]).then_inc(m_h, 1)

        ph = Region(R1, R3)
        bas = [ph.take(IC * D, 4 * BASES) for _ in range(3)]
        mask = ph.take(8, 4 * BASES)
        attp = ph.take(4, 4 * BASES)
        attL = ph.take(2 * 32, 4 * BASES).rearrange("p (l m) -> p l m", l=2)
        stage = [ph.take(IC // 4 * D).rearrange("p (k o) -> p k o", o=D) for _ in range(2)]
        NB = 128 // IC
        b_ld = [sem(f"b_ld{k}") for k in range(3)]
        b_c = sem("b_c"); b_z = sem("b_z"); b_at = sem("b_at"); b_mm = sem("b_mm"); b_ev = sem("b_ev")
        b_st = [sem("b_st0"), sem("b_st1")]
        with nc.Block() as block:
            @block.sync
            def _(sp):
                sp.dma_start(mask, A["mask4"]).then_inc(b_c, 16)
                sp.dma_start(attp[:, 0:2], A["att1_rep"]).then_inc(b_c, 16)
                sp.dma_start(attp[:, 2:4], A["att2_rep"]).then_inc(b_c, 16)
                for u in range(2 * NB):
                    if u >= 3:
                        sp.wait_ge(b_mm, (u - 2) * (IC // 4))
                    layer, c = u // NB, u % NB
                    v = A[f"L3_gnn_basis{layer + 1}"].rearrange("b (q i) o -> (b q) (i o)", q=4)
                    sp.dma_start(bas[u % 3], v[:, c * IC * D:(c + 1) * IC * D]).then_inc(b_ld[u % 3], 16)

            @block.vector
            def _(dve):
                dve.memset(attL, 0.0).then_inc(b_z, 1)
                dve.wait_ge(b_z, 1)
                dve.wait_ge(b_c, 48)
                for layer in range(2):
                    for r in range(REL):
                        dve.tensor_scalar(attL[:, layer, 4 * r:4 * r + 4], mask[:, 4 * r:4 * r + 4],
                                          attp[:, 2 * layer + r:2 * layer + r + 1], None, ALU.mult).then_inc(b_at, 1)

            @block.tensor
            def _(pe):
                pe.wait_ge(b_at, 4)
                for u in range(2 * NB):
                    pe.wait_ge(b_ld[u % 3], 16 * (u // 3 + 1))
                    for k in range(IC // 4):
                        g = u * (IC // 4) + k
                        if g >= 4:
                            pe.wait_ge(b_ev, g - 3)
                        for s in range(4):
                            last = pe.matmul(bank[g % 4][32 * s:32 * s + 32, :], attL[:, u // NB],
                                             bas[u % 3][:, (4 * k + s) * D:(4 * k + s + 1) * D], start=True, stop=True)
                        last.then_inc(b_mm, 1)

            @block.scalar
            def _(act):
                for u in range(2 * NB):
                    layer, c = u // NB, u % NB
                    for k in range(IC // 4):
                        g = u * (IC // 4) + k
                        if u >= 2 and k == 0:
                            act.wait_ge(b_st[u % 2], 64 * (u // 2))
                        act.wait_ge(b_mm, g + 1)
                        act.activation(stage[u % 2][:, k], bank[g % 4][:, :], ACT.Copy).then_inc(b_ev, 1)
                    act.wait_ge(b_ev, (u + 1) * (IC // 4))
                    for s in range(4):
                        act.dma_start(wD[layer].rearrange("m (k s) o -> s m k o", s=4)[s, :, c * (IC // 4):(c + 1) * (IC // 4)],
                                      stage[u % 2][32 * s:32 * s + 8]).then_inc(b_st[u % 2], 16)
                for k in range(2):
                    act.wait_ge(b_st[k], 64 * NB)

        def transpose_nodes(tag, xs, xT, cols):
            t_pe, t_ev = sem(tag + "_tr"), sem(tag + "_ev")
            with nc.Block() as block:
                @block.tensor
                def _(pe):
                    for n in range(NT):
                        if n >= 2:
                            pe.wait_ge(t_ev, n - 1)
                        for c in range(FC):
                            last = pe.transpose(bank[n % 2][:, c * P:(c + 1) * P], cols(xs[:, n], c), ident[0:P, 0:P])
                        last.then_inc(t_pe, 1)

                @block.vector
                def _(dve):
                    for n in range(NT):
                        dve.wait_ge(t_pe, n + 1)
                        dve.tensor_copy(xT[:, :, n * P:(n + 1) * P],
                                        bank[n % 2][:, 0:FC * P].rearrange("p (c x) -> p c x", c=FC)).then_inc(t_ev, 1)

        def plain_cols(x, c):
            return x[:, c * 128:(c + 1) * 128]

        def norm_nodes(tag, xs):
            d, a = sem(tag + "_d"), sem(tag + "_a")
            with nc.Block() as block:
                @block.vector
                def _(dve):
                    k = [0]

                    def link(ins):
                        k[0] += 1
                        ins.then_inc(d, 1)
                        dve.wait_ge(d, k[0])
                    for n in range(NT):
                        dve.bn_stats(stats[:, n], xs[:, n]).then_inc(d, 1)
                    k[0] = NT
                    dve.wait_ge(d, NT)
                    for n in range(NT):
                        dve.bn_aggr(mv[:, n], stats[:, n]).then_inc(d, 1)
                    k[0] = 2 * NT
                    dve.wait_ge(d, 2 * NT)
                    link(dve.tensor_scalar(vare, mv[:, :, 1], 1e-5, None, ALU.add))
                    dve.wait_ge(a, 1)
                    link(dve.reciprocal(rs, sd))
                    link(dve.tensor_tensor(nt1, rs, rs, ALU.mult))
                    link(dve.tensor_tensor(nt2, nt1, vare, ALU.mult))
                    link(dve.tensor_scalar(nt1, nt2, -0.5, 1.5, ALU.mult, ALU.add))
                    link(dve.tensor_tensor(nt2, rs, nt1, ALU.mult))
                    for n in range(NT):
                        dve.tensor_scalar(xs[:, n], xs[:, n], mv[:, n, 0:1], nt2[:, n:n + 1],
                                          ALU.subtract, ALU.mult).then_inc(d, 1)

                @block.scalar
                def _(act):
                    act.wait_ge(d, 2 * NT + 1)
                    act.activation(sd, vare, ACT.Sqrt).then_inc(a, 1)

        ph = Region(R1, R3)
        xs0 = ph.take(NT * D, P).rearrange("p (n f) -> p n f", n=NT)
        xT0 = ph.take(FC * NODES).rearrange("p (c n) -> p c n", c=FC)
        wup = ph.take(2 * 128).rearrange("p (q n) -> p q n", q=2)
        upS = [ph.take(D, P) for _ in range(2)]
        u_ld = sem("u_ld"); u_mm = sem("u_mm"); u_ev = sem("u_ev")
        u_st = [sem("u_st0"), sem("u_st1")]
        with nc.Block() as block:
            @block.sync
            def _(sp):
                sp.dma_start(xs0, A["x"].rearrange("(n p) f -> p n f", p=P)).then_inc(u_ld, 16)
                sp.dma_start(wup[:, 0], A["L0_gnn_W_up0"]).then_inc(u_ld, 16)
                sp.dma_start(wup[:, 1], A["L0_gnn_W_up1"]).then_inc(u_ld, 16)
                sp.wait_ge(u_ld, 48)

        def irrep_cols(x, c):
            return x[:, 0:MUL] if c == 0 else x[:, MUL:].rearrange("p (u m) -> p m u", m=3)[:, c - 1]
        transpose_nodes("t0", xs0, xT0, irrep_cols)
        with nc.Block() as block:
            @block.tensor
            def _(pe):
                for n in range(NT):
                    if n >= 2:
                        pe.wait_ge(u_ev, n - 1)
                    for c in range(FC):
                        last = pe.matmul(bank[n % 2][0:P, c * 128:(c + 1) * 128], xT0[:, c, n * P:(n + 1) * P],
                                         wup[:, min(c, 1)], start=True, stop=True)
                    last.then_inc(u_mm, 1)

            @block.scalar
            def _(act):
                for n in range(NT):
                    act.wait_ge(u_mm, n + 1)
                    if n >= 2:
                        act.wait_ge(u_st[n % 2], 16 * (n // 2))
                    act.activation(upS[n % 2], bank[n % 2][0:P, :], ACT.Copy, scale=1.0 / math.sqrt(MUL)).then_inc(u_ev, 1)

            @block.sync
            def _(sp):
                for n in range(NT):
                    sp.wait_ge(u_ev, n + 1)
                    sp.dma_start(upD[n * P:(n + 1) * P, :], upS[n % 2]).then_inc(u_st[n % 2], 16)
                for k in range(2):
                    sp.wait_ge(u_st[k], 16 * (NT // 2))

        edge.at = edge_mark
        G = [edge.take(D) for _ in range(BODY)]
        hS = edge.take(4 * P).rearrange("p (s e) -> p s e", s=4)
        W4 = edge.take(4 * MUL)
        M = [edge.take(8 * MUL, P).rearrange("p (b u) -> p b u", b=8) for _ in range(2)]
        Ss = [edge.take(NODES // 2, P, BF16) for _ in range(2)]
        iotaN = edge.take(NODES // 2, P, I16)
        eq = [edge.take(W, P) for _ in range(2)]
        Sy = [edge.take(4 * W, P).rearrange("p (m w) -> p m w", m=4) for _ in range(2)]
        Sw = [edge.take(5 * W // 2, P, BF16) for _ in range(2)]
        ring = edge.take(BODY, 128, I32)
        relx = edge.take(2, P)
        wsteps = edge.take(NODES // W + 1, P)

        z = sem("z"); w4_ld = sem("w4_ld")
        h_ld = [sem(f"h_ld{j}") for j in range(BODY)]
        gathered = [sem(f"gathered{j}") for j in range(BODY)]
        tpw_ready = sem("tpw_ready")
        prod_done = sem("prod_done")
        send_ready = sem("send_ready")
        recv_ready = sem("recv_ready")
        visit_done = sem("visit_done")
        acc_done = sem("acc_done")
        eq_done = sem("eq_done"); passed = sem("passed"); ring_done = sem("ring_done")
        x_eq = sem("x_eq"); x_rel = sem("x_rel")
        x_ready = sem("x_ready"); x_done = sem("x_done")
        x_acc = sem("x_acc")
        TP, MSG, BLD = (6, 7), (0, 1), (2, 4)

        with nc.Block() as block:
            @block.sync
            def _(sp):
                for half in range(2):
                    sp.dma_start(W4[half * HID:(half + 1) * HID], A["L0_gnn_W_mlp4"]).then_inc(w4_ld, 16)

                def load(turn, j):
                    half = slice(j // 4 * HID, (j // 4 + 1) * HID)
                    src = hD[turn] if isinstance(turn, int) else hD[bass.ds(turn, 1)].rearrange("a p x -> (a p) x")
                    sp.dma_start(hS[half, j % 4], src[half, j % 4 * P:(j % 4 + 1) * P]).then_inc(h_ld[j], 16)
                for j in range(BODY):
                    load(0, j)
                with sp.Fori(0, TURNS - 1) as i:
                    for j in range(BODY):
                        sp.wait_ge(tpw_ready, i * BODY + j + 1)
                        load(i + 1, j)

            @block.gpsimd
            def _(pool):
                pool.iota(iotaN, pattern=[[1, NODES]], base=0, channel_multiplier=0,
                          allow_small_or_imprecise_dtypes=True).then_inc(z, 1)
                pool.iota(wsteps, pattern=[[-W, NODES // W + 1]], base=-W, channel_multiplier=0,
                          allow_small_or_imprecise_dtypes=True).then_inc(z, 1)
                for j in range(BODY):
                    pool.indirect_dma_start(out=G[j], out_offset=None, in_=upD,
                                            in_offset=bass.IndirectOffsetOnAxis(idx[:, j:j + 1], 0)).then_inc(gathered[j], 16)

                def onehots(p, t, ready, eqs, n):
                    pool.wait_ge(eqs, n)
                    pool.sem_inc(passed, 1)
                    e = eq[p]
                    col = slice(t, t + 1) if isinstance(t, int) else bass.ds(t, 1)
                    y = yT[:, col].rearrange("p a m -> p (a m)")
                    v = valT[:, col].rearrange("p a m -> p (a m)")
                    pool.tensor_tensor(Sy[p], e.unsqueeze(1).to_broadcast([P, 4, W]),
                                       y.unsqueeze(2).to_broadcast([P, 4, W]), ALU.mult).then_inc(ready, 1)
                    pool.tensor_tensor(Sw[p][:, 0:3 * W].rearrange("p (m w) -> p m w", m=3),
                                       e.unsqueeze(1).to_broadcast([P, 3, W]),
                                       v[:, 0:3].unsqueeze(2).to_broadcast([P, 3, W]), ALU.mult).then_inc(ready, 1)
                    pool.tensor_tensor(Sw[p][:, 3 * W:5 * W].rearrange("p (w r) -> p w r", r=2),
                                       e.unsqueeze(2).to_broadcast([P, W, 2]),
                                       v[:, 3:5].unsqueeze(1).to_broadcast([P, W, 2]), ALU.mult).then_inc(ready, 1)

                def turn(i, last):
                    for j in range(BODY):
                        t, p = i * BODY + j, j % 2
                        col = slice(t, t + 1) if last else bass.ds(t, 1)
                        onehots(p, t, recv_ready, eq_done, t + 1)
                        further = pool.value_load(tab[:, 1, col], min_val=0, max_val=NODES // W)
                        seen = pool.value_load(tab[:, 2, col], min_val=0, max_val=ET * (NODES // W))
                        with pool.If(further > 0):
                            with pool.Fori(0, further) as k:
                                onehots(p, t, x_ready, x_eq, seen + k + 1)
                        if not last:
                            pool.wait_ge(prod_done, t + 2)
                            pool.sem_inc(passed, 1)
                            pool.tensor_copy(ring[:, j:j + 1], idx[:, bass.ds(t + BODY, 1)]).then_inc(ring_done, 1)
                            pool.wait_ge(ring_done, t + 1)
                            pool.sem_inc(passed, 1)
                            pool.indirect_dma_start(out=G[j], out_offset=None, in_=upD,
                                                    in_offset=bass.IndirectOffsetOnAxis(ring[:, j:j + 1], 0)).then_inc(gathered[j], 16)
                with pool.Fori(0, TURNS - 1) as i:
                    turn(i, False)
                turn(TURNS - 1, True)

            @block.vector
            def _(dve):
                dve.sem_inc(prod_done, 1)
                dve.sem_inc(acc_done, 2)
                dve.sem_inc(x_acc, 1)
                dve.memset(AT, 0.0).then_inc(z, 1)
                dve.memset(CNT, 0).then_inc(z, 1)
                dve.memset(accT, 0.0).then_inc(z, 1)
                dve.wait_ge(z, 5)

                def products(turn, j):
                    t, p, g = turn * BODY + j, j % 2, G[j][0:P]
                    dve.wait_ge(gathered[j], turn * 16 + 16)
                    dve.wait_ge(tpw_ready, t + 1)
                    tp = bank[TP[p]][0:P, :].rearrange("p (b u) -> p b u", b=4)
                    dve.tensor_tensor(M[p][:, 0:2], tp[:, 0:2],
                                      g[:, 0:MUL].unsqueeze(1).to_broadcast([P, 2, MUL]), ALU.mult)
                    dve.tensor_tensor(M[p][:, 2:8].rearrange("p (b m) u -> p b m u", b=2),
                                      tp[:, 2:4].unsqueeze(2).to_broadcast([P, 2, 3, MUL]),
                                      g[:, MUL:].rearrange("p (m u) -> p m u", m=3).unsqueeze(1).to_broadcast([P, 2, 3, MUL]),
                                      ALU.mult).then_inc(prod_done, 1)
                    col = slice(t, t + 1) if isinstance(t, int) else bass.ds(t, 1)
                    dve.tensor_scalar(eq[p], iota32, rel[:, col], None, ALU.is_equal).then_inc(eq_done, 1)
                    dve.tensor_scalar(Ss[p], iotaN, srcT[:, col], None, ALU.is_equal).then_inc(send_ready, 1)

                def accumulate(p, at_node, done):
                    w = bass.ds(at_node, W)
                    dve.tensor_tensor(accT[:, :, w], accT[:, :, w],
                                      bank[MSG[p]][:, 0:8 * W].rearrange("p (b w) -> p b w", b=8), ALU.add)
                    for h in range(2):
                        ps = bank[BLD[p] + h][0:P, 0:15 * W].rearrange("p (c x) -> p c x", c=5)
                        cs = slice(5 * h, 5 * h + 5)
                        a, c = AT[:, cs, w], CNT[:, cs, bass.ds(at_node * 2, 2 * W)]
                        dve.tensor_tensor(a, a, ps[:, :, 0:W], ALU.add)
                        last = dve.tensor_tensor(c, c, ps[:, :, W:3 * W], ALU.add)
                    last.then_inc(done, 1)

                def settle(turn, j):
                    t, p = turn * BODY + j, j % 2
                    col = slice(t, t + 1) if isinstance(t, int) else bass.ds(t, 1)
                    start = dve.value_load(tab[:, 0, col], min_val=0, max_val=NODES - 1)
                    dve.wait_ge(visit_done, t + 3)
                    dve.wait_ge(acc_done, t + 2)
                    accumulate(p, start, acc_done)
                    further = dve.value_load(tab[:, 1, col], min_val=0, max_val=NODES // W)
                    seen = dve.value_load(tab[:, 2, col], min_val=0, max_val=ET * (NODES // W))
                    with dve.If(further > 0):
                        with dve.Fori(0, further) as k:
                            dve.wait_ge(acc_done, t + 3)
                            dve.wait_ge(x_acc, seen + k + 1)
                            dve.tensor_tensor(relx[:, 0:1], rel[:, col], wsteps[:, bass.ds(k, 1)], ALU.add).then_inc(x_rel, 1)
                            dve.wait_ge(x_rel, seen + k + 1)
                            dve.tensor_scalar(eq[p], iota32, relx[:, 0:1], None, ALU.is_equal).then_inc(x_eq, 1)
                            dve.wait_ge(x_done, seen + k + 1)
                            node = nc.s_assert_within(start + (k + 1) * W, 0, NODES - 1,
                                skip_runtime_bounds_check_because="the last window starts at or before the largest receiver")
                            accumulate(p, node, x_acc)

                products(0, 0)
                with dve.Fori(0, TURNS - 1) as i:
                    for j in range(BODY):
                        products(i + (j + 1) // BODY, (j + 1) % BODY)
                        settle(i, j)
                for j in range(BODY):
                    if j + 1 < BODY:
                        products(TURNS - 1, j + 1)
                    settle(TURNS - 1, j)

            @block.tensor
            def _(pe):
                pe.sem_inc(visit_done, 2)
                pe.wait_ge(w4_ld, 32)

                def weights(turn, j):
                    half = slice(j // 4 * HID, (j // 4 + 1) * HID)
                    pe.wait_ge(h_ld[j], turn * 16 + 16)
                    pe.matmul(bank[TP[j % 2]][0:P, :], hS[half, j % 4], W4[half, :], start=True, stop=True).then_inc(tpw_ready, 1)

                def visit(p, done):
                    msg, m = bank[MSG[p]], M[p]
                    pe.matmul(msg[:, 0:W], m[:, 0], Sy[p][:, 0], start=True, stop=True)
                    pe.matmul(msg[:, W:4 * W], m[:, 1], Sy[p][:, 1:4].rearrange("p m w -> p (m w)"), start=True, stop=True)
                    for k in range(3):
                        pe.matmul(msg[:, (4 + k) * W:(5 + k) * W], m[:, 2 + k], Sy[p][:, 0], start=True, stop=True)
                    for k in range(3):
                        pe.matmul(msg[:, 7 * W:8 * W], m[:, 5 + k], Sy[p][:, 1 + k], start=(k == 0), stop=(k == 2))
                    for c in range(NT):
                        b, o = bank[BLD[p] + c // 5], c % 5 * 3 * W
                        s = Ss[p][:, c * P:(c + 1) * P]
                        pe.matmul(b[0:P, o:o + 3 * W], s, Sw[p][:, 2 * W:5 * W], start=True, stop=False)
                        pe.matmul(b[0:P, o:o + W], s, Sw[p][:, 0:W], start=False, stop=False)
                        last = pe.matmul(b[0:P, o:o + W], s, Sw[p][:, W:2 * W], start=False, stop=True)
                    last.then_inc(done, 1)

                def turn(i, last):
                    for j in range(BODY):
                        t = i * BODY + j
                        if not (last and j == BODY - 1):
                            pe.wait_ge(prod_done, t + 1)
                            weights(i + (j + 1) // BODY, (j + 1) % BODY)
                        pe.wait_ge(prod_done, t + 2)
                        pe.wait_ge(send_ready, t + 1)
                        pe.wait_ge(recv_ready, t * 3 + 3)
                        pe.wait_ge(acc_done, t + 1)
                        visit(j % 2, visit_done)
                        col = slice(t, t + 1) if last else bass.ds(t, 1)
                        further = pe.value_load(tab[:, 1, col], min_val=0, max_val=NODES // W)
                        seen = pe.value_load(tab[:, 2, col], min_val=0, max_val=ET * (NODES // W))
                        with pe.If(further > 0):
                            with pe.Fori(0, further) as k:
                                pe.wait_ge(x_ready, (seen + k) * 3 + 3)
                                visit(j % 2, x_done)
                weights(0, 0)
                with pe.Fori(0, TURNS - 1) as i:
                    turn(i, False)
                turn(TURNS - 1, True)

        xs = at(R3 + 8 * WPAD, NT * D, P).rearrange("p (n f) -> p n f", n=NT)
        ph = Region(R3 + 8 * WPAD + NT * D, WORDS)
        wout = ph.take(4 * 128).rearrange("p (q n) -> p q n", q=4)
        o_ld = sem("o_ld"); o_w = sem("o_w"); o_mm = sem("o_mm"); o_ev = sem("o_ev")
        with nc.Block() as block:
            @block.sync
            def _(sp):
                sp.dma_start(xs, A["x"].rearrange("(n p) f -> p n f", p=P)).then_inc(o_ld, 16)
                sp.dma_start(wout[:, 0:2], A["L0_gnn_W_out0"].rearrange("(q p) n -> p q n", q=2)).then_inc(o_ld, 16)
                sp.dma_start(wout[:, 2:4], A["L0_gnn_W_out1"].rearrange("(q p) n -> p q n", q=2)).then_inc(o_ld, 16)

            @block.tensor
            def _(pe):
                pe.wait_ge(o_w, 1)
                for n in range(NT):
                    if n >= 2:
                        pe.wait_ge(o_ev, 2 * (n - 1))
                    ns = slice(n * P, (n + 1) * P)
                    for q in range(4):
                        first, second = (0, 7) if q == 0 else (q, 3 + q)
                        o = bank[n % 2][0:P, q * 128:(q + 1) * 128]
                        pe.matmul(o, accT[:, first, ns], wout[:, 0 if q == 0 else 2], start=True, stop=False)
                        last = pe.matmul(o, accT[:, second, ns], wout[:, 1 if q == 0 else 3], start=False, stop=True)
                    last.then_inc(o_mm, 1)

            @block.vector
            def _(dve):
                dve.wait_ge(o_ld, 48)
                dve.tensor_scalar(wout[:, 1], wout[:, 1], 1.0 / math.sqrt(3.0), None, ALU.mult).then_inc(o_w, 1)
                c = SILU_2MOM / math.sqrt(HID) / math.sqrt(2 * MUL) / 10.0
                for n in range(NT):
                    dve.wait_ge(o_mm, n + 1)
                    b = bank[n % 2][0:P, :]
                    dve.scalar_tensor_tensor(xs[:, n, 0:MUL], b[:, 0:MUL], c, xs[:, n, 0:MUL], ALU.mult, ALU.add).then_inc(o_ev, 1)
                    v = xs[:, n, MUL:].rearrange("p (u m) -> p m u", m=3)
                    dve.scalar_tensor_tensor(v, b[:, MUL:].rearrange("p (m u) -> p m u", m=3), c, v,
                                             ALU.mult, ALU.add).then_inc(o_ev, 1)
        norm_nodes("n0", xs)

        xT = at(R3, FC * NODES).rearrange("p (c n) -> p c n", c=FC)
        xnT = at(R3 + FC * NODES, FC * NODES).rearrange("p (c n) -> p c n", c=FC)
        transpose_nodes("t1", xs, xT, plain_cols)
        ph = Region(R3 + 8 * WPAD + NT * D, WORDS)
        wg = ph.take(FC * 128).rearrange("p (c n) -> p c n", c=FC)
        wf = ph.take(FC * 128).rearrange("p (c n) -> p c n", c=FC)
        wfT = ph.take(D)
        xw = ph.take(NT * 128, P).rearrange("p (n f) -> p n f", n=NT)
        hT = ph.take(NODES)
        g_ld = sem("g_ld"); g_wt = sem("g_wt"); g_mm = sem("g_mm"); g_ev = sem("g_ev"); g_dg = sem("g_dg")
        g_hm = sem("g_hm"); g_he = sem("g_he"); g_o = sem("g_o"); g_x = sem("g_x"); g_d2 = sem("g_d2")
        with nc.Block() as block:
            @block.sync
            def _(sp):
                sp.dma_start(wg, A["L1_gnn_W_gcn"].rearrange("(c p) n -> p c n", c=FC)).then_inc(g_ld, 16)
                sp.dma_start(wf, A["L1_gnn_W_fc"].rearrange("(c p) n -> p c n", c=FC)).then_inc(g_ld, 16)
                sp.dma_start(bgcn, A["L1_gnn_b_gcn"].rearrange("(p a) -> p a", a=1)).then_inc(g_ld, 16)
                sp.dma_start(brow, A["L1_gnn_b_fc"].rearrange("(a n) -> a n", a=1)).then_inc(g_ld, 16)

            @block.tensor
            def _(pe):
                pe.wait_ge(g_ld, 64)
                for c in range(FC):
                    last = pe.transpose(bank[7][:, c * 128:(c + 1) * 128], wf[:, c], ident)
                last.then_inc(g_wt, 1)
                for n in range(NT):
                    if n >= 2:
                        pe.wait_ge(g_ev, n - 1)
                    for c in range(FC):
                        last = pe.matmul(bank[n % 2][0:P, 0:128], xT[:, c, n * P:(n + 1) * P], wg[:, c],
                                         start=(c == 0), stop=(c == FC - 1))
                    last.then_inc(g_mm, 1)
                for n in range(NT):
                    for s in range(NT):
                        last = pe.matmul(bank[6][0:P, n:n + 1], AT[:, s, n * P:(n + 1) * P], onesM[:, 0:1],
                                         start=(s == 0), stop=(s == NT - 1))
                last.then_inc(g_dg, 1)
                pe.wait_ge(g_ev, NT)
                for k, (lo, hi) in enumerate(SPANS):
                    for s in range(NT):
                        last = pe.matmul(bank[2 + k][:, 0:hi - lo], xw[:, s], AT[:, s, lo:hi],
                                         start=(s == 0), stop=(s == NT - 1))
                    last.then_inc(g_hm, 1)
                pe.wait_ge(g_he, 3)
                pe.wait_ge(g_wt, 2)
                for n in range(NT):
                    if n >= 2:
                        pe.wait_ge(g_x, n - 1)
                    pe.matmul(bank[n % 2][0:P, :], hT[:, n * P:(n + 1) * P], wfT, start=True, stop=False)
                    pe.matmul(bank[n % 2][0:P, :], onesM[0:1, :], brow, start=False, stop=True).then_inc(g_o, 1)

            @block.scalar
            def _(act):
                act.wait_ge(g_wt, 1)
                act.activation(wfT, bank[7][:, :], ACT.Copy).then_inc(g_wt, 1)
                for k, (lo, hi) in enumerate(SPANS):
                    act.wait_ge(g_hm, k + 1)
                    act.activation(hT[:, lo:hi], bank[2 + k][:, 0:hi - lo], ACT.Identity, bias=bgcn).then_inc(g_he, 1)

            @block.vector
            def _(dve):
                for n in range(NT):
                    dve.wait_ge(g_mm, n + 1)
                    dve.tensor_copy(xw[:, n], bank[n % 2][0:P, 0:128]).then_inc(g_ev, 1)
                dve.wait_ge(g_dg, 1)
                dve.tensor_scalar(invdeg, bank[6][0:P, 0:NT], 1.0, None, ALU.max).then_inc(g_d2, 1)
                dve.wait_ge(g_d2, 1)
                dve.reciprocal(nt1, invdeg).then_inc(g_d2, 1)
                dve.wait_ge(g_d2, 2)
                dve.tensor_copy(invdeg, nt1).then_inc(g_d2, 1)
                for n in range(NT):
                    dve.wait_ge(g_o, n + 1)
                    dve.tensor_tensor(xs[:, n], bank[n % 2][0:P, :], xs[:, n], ALU.add).then_inc(g_x, 1)
        norm_nodes("n1", xs)

        transpose_nodes("t2", xs, xT, plain_cols)
        ph = Region(R3 + 8 * WPAD + NT * D, WORDS)
        raw = ph.take(FC * D).rearrange("p (c n) -> p c n", c=FC)
        wT = [ph.take(FC * D).rearrange("p (c n) -> p c n", c=FC) for _ in range(2)]
        s_ld = sem("s_ld"); s_tr = sem("s_tr"); s_te = sem("s_te"); s_nm = sem("s_nm"); s_ne = sem("s_ne")
        s_o = sem("s_o"); s_x = sem("s_x"); s_y = sem("s_y")
        with nc.Block() as block:
            @block.sync
            def _(sp):
                sp.dma_start(brow, A["L2_gnn_b_self"].rearrange("(a n) -> a n", a=1)).then_inc(s_ld, 16)
                sp.dma_start(brow2, A["L2_gnn_b_neigh"].rearrange("(a n) -> a n", a=1)).then_inc(s_ld, 16)
                sp.dma_start(raw, A["L2_gnn_W_neigh"].rearrange("(c p) n -> p c n", c=FC)).then_inc(s_ld, 16)
                sp.wait_ge(s_tr, FC)
                sp.dma_start(raw, A["L2_gnn_W_self"].rearrange("(c p) n -> p c n", c=FC)).then_inc(s_ld, 16)

            @block.tensor
            def _(pe):
                for w in range(2):
                    pe.wait_ge(s_ld, 48 + 16 * w)
                    for ic in range(FC):
                        k = w * FC + ic
                        if k >= 2:
                            pe.wait_ge(s_te, k - 1)
                        for oc in range(FC):
                            last = pe.transpose(bank[k % 2][:, oc * 128:(oc + 1) * 128],
                                                raw[:, oc, ic * 128:(ic + 1) * 128], ident)
                        last.then_inc(s_tr, 1)
                for g in range(FC * 3):
                    c, (lo, hi) = g // 3, SPANS[g % 3]
                    if g >= 4:
                        pe.wait_ge(s_ne, g - 3)
                    for s in range(NT):
                        last = pe.matmul(bank[4 + g % 4][:, 0:hi - lo], xs[:, s, c * 128:(c + 1) * 128], AT[:, s, lo:hi],
                                         start=(s == 0), stop=(s == NT - 1))
                    last.then_inc(s_nm, 1)
                pe.wait_ge(s_te, 2 * FC)
                pe.wait_ge(s_ne, FC * 3)
                for n in range(NT):
                    if n >= 2:
                        pe.wait_ge(s_y, n - 1)
                    a, b = bank[n % 2][0:P, :], bank[2 + n % 2][0:P, :]
                    for c in range(FC):
                        pe.matmul(a, xnT[:, c, n * P:(n + 1) * P], wT[0][:, c], start=(c == 0), stop=(c == FC - 1))
                    for c in range(FC):
                        pe.matmul(b, xT[:, c, n * P:(n + 1) * P], wT[1][:, c], start=(c == 0), stop=False)
                    pe.matmul(b, onesM[0:1, :], brow, start=False, stop=False)
                    pe.matmul(b, onesM[0:1, :], brow2, start=False, stop=True).then_inc(s_o, 1)

            @block.scalar
            def _(act):
                for k in range(2 * FC):
                    act.wait_ge(s_tr, k + 1)
                    act.activation(wT[k // FC][:, k % FC], bank[k % 2][:, :], ACT.Copy).then_inc(s_te, 1)

            @block.vector
            def _(dve):
                for g in range(FC * 3):
                    c, (lo, hi) = g // 3, SPANS[g % 3]
                    dve.wait_ge(s_nm, g + 1)
                    dve.tensor_copy(xnT[:, c, lo:hi], bank[4 + g % 4][:, 0:hi - lo]).then_inc(s_ne, 1)
                for n in range(NT):
                    dve.wait_ge(s_o, n + 1)
                    dve.scalar_tensor_tensor(xs[:, n], bank[n % 2][0:P, :], invdeg[:, n:n + 1], xs[:, n],
                                             ALU.mult, ALU.add).then_inc(s_x, 1)
                    dve.wait_ge(s_x, n + 1)
                    dve.tensor_tensor(xs[:, n], xs[:, n], bank[2 + n % 2][0:P, :], ALU.add).then_inc(s_y, 1)
        norm_nodes("n2", xs)

        x3 = at(R3, NT * D, P).rearrange("p (n f) -> p n f", n=NT)
        R4 = R3 + NT * D
        BT = [at(R1, NT * NODES, P).rearrange("p (c n) -> p c n", c=NT),
              at(R4, NT * NODES, P).rearrange("p (c n) -> p c n", c=NT)]
        R5 = R4 + NT * NODES
        m_x3 = sem("m_x3")
        with nc.Block() as block:
            @block.vector
            def _(dve):
                for n in range(NT):
                    dve.tensor_copy(x3[:, n], xs[:, n]).then_inc(m_x3, 1)
        ph = Region(R5, WORDS)
        cf = [ph.take(2 * P, P).rearrange("p (n r) -> p n r", r=2) for _ in range(4)]
        c_cv = sem("c_cv"); c_tr = sem("c_tr"); c_ev = sem("c_ev")
        with nc.Block() as block:
            @block.scalar
            def _(act):
                for k in range(NT * NT):
                    s, d = k % NT, k // NT
                    if k >= 4:
                        act.wait_ge(c_tr, k - 3)
                    act.activation(cf[k % 4], CNT[:, s, 2 * d * P:2 * (d + 1) * P].rearrange("p (n r) -> p n r", r=2),
                                   ACT.Copy).then_inc(c_cv, 1)

            @block.tensor
            def _(pe):
                for k in range(NT * NT):
                    pe.wait_ge(c_cv, k + 1)
                    if k >= 8:
                        pe.wait_ge(c_ev, k - 7)
                    for r in range(REL):
                        last = pe.transpose(bank[k % 8][0:P, r * P:(r + 1) * P], cf[k % 4][:, :, r], ident[0:P, 0:P])
                    last.then_inc(c_tr, 1)

            @block.vector
            def _(dve):
                for k in range(NT * NT):
                    s, d = k % NT, k // NT
                    dve.wait_ge(c_tr, k + 1)
                    dve.tensor_copy(BT[0][:, d, s * P:(s + 1) * P], bank[k % 8][0:P, 0:P])
                    dve.tensor_copy(BT[1][:, d, s * P:(s + 1) * P], bank[k % 8][0:P, P:2 * P]).then_inc(c_ev, 1)

        Z = [at(R2 + r * NT * D, NT * D, P).rearrange("p (n f) -> p n f", n=NT) for r in range(REL)]
        ph = Region(R5, WORDS)
        wr = ph.take(FC * D).rearrange("p (c n) -> p c n", c=FC)
        gw = ph.take(FC * REL).rearrange("p (c r) -> p c r", c=FC)
        gate = ph.take(NT * REL, P).rearrange("p (n r) -> p n r", n=NT)
        r_lo = Region(R2 + REL * NT * D, R3)
        wr2_ = r_lo.take(FC * D).rearrange("p (c n) -> p c n", c=FC)
        xT3 = ph.take(FC * NODES).rearrange("p (c n) -> p c n", c=FC)
        wbuf = [wr, wr2_]
        x3D = nc.dram_tensor("x3_scratch", (P, NT * D), F32, kind="Internal").ap()
        x_sv = sem("x_sv")
        x3flat = at(R3, NT * D, P)
        with nc.Block() as block:
            @block.sync
            def _(sp):
                sp.dma_start(x3D, x3flat).then_inc(x_sv, 16)
                sp.wait_ge(x_sv, 16)
        for layer in range(2):
            tag = f"r{layer}"
            transpose_nodes("t3" + tag, x3, xT3, plain_cols)
            q_ld = [sem(tag + "_ld0"), sem(tag + "_ld1")]
            q_c = sem(tag + "_c"); q_g = sem(tag + "_g"); q_gs = sem(tag + "_gs")
            q_z = sem(tag + "_z"); q_ze = sem(tag + "_ze"); q_o = sem(tag + "_o"); q_e = sem(tag + "_e")
            with nc.Block() as block:
                @block.sync
                def _(sp):
                    sp.dma_start(gw, A[f"gate_w{layer + 1}"]).then_inc(q_c, 16)
                    sp.dma_start(brow, A[f"L3_gnn_bias{layer + 1}"].rearrange("(a n) -> a n", a=1)).then_inc(q_c, 16)
                    for r in range(REL):
                        sp.dma_start(wbuf[r], wD[layer, 4 * r:4 * r + 4].rearrange("q i o -> i q o")).then_inc(q_ld[r], 16)
                    if layer == 1:
                        sp.dma_start(x3flat, x3D).then_inc(x_sv, 16)
                    sp.wait_ge(q_z, NT)
                    sp.dma_start(wbuf[0], A[f"L3_gnn_root{layer + 1}"].rearrange("(c p) n -> p c n", c=FC)).then_inc(q_ld[0], 16)

                @block.tensor
                def _(pe):
                    pe.wait_ge(q_c, 32)
                    for n in range(NT):
                        for c in range(FC):
                            last = pe.matmul(bank[6][0:P, 2 * n:2 * n + 2], xT3[:, c, n * P:(n + 1) * P], gw[:, c],
                                             start=(c == 0), stop=(c == FC - 1))
                    last.then_inc(q_g, 1)
                    for k in range(REL * NT):
                        r, n = k // NT, k % NT
                        if n == 0:
                            pe.wait_ge(q_ld[r], 16)
                        if k >= 2:
                            pe.wait_ge(q_ze, k - 1)
                        for c in range(FC):
                            last = pe.matmul(bank[k % 2][0:P, :], xT3[:, c, n * P:(n + 1) * P], wbuf[r][:, c],
                                             start=(c == 0), stop=(c == FC - 1))
                        last.then_inc(q_z, 1)
                    pe.wait_ge(q_ld[0], 32)
                    pe.wait_ge(q_ze, REL * NT)
                    for n in range(NT):
                        ns = slice(n * P, (n + 1) * P)
                        o = bank[2 + n % 4][0:P, :]
                        if n >= 4:
                            pe.wait_ge(q_e, n - 3)
                        pe.matmul(o, onesM[0:1, :], brow, start=True, stop=False)
                        for c in range(FC):
                            pe.matmul(o, xT3[:, c, ns], wbuf[0][:, c], start=False, stop=False)
                        for k in range(REL * NT):
                            r, d = k // NT, k % NT
                            last = pe.matmul(o, BT[r][:, d, ns], Z[r][:, d], start=False, stop=(k == REL * NT - 1))
                        last.then_inc(q_o, 1)

                @block.scalar
                def _(act):
                    act.wait_ge(q_g, 1)
                    act.activation(gate.rearrange("p n r -> p (n r)"), bank[6][0:P, 0:REL * NT], ACT.Sigmoid).then_inc(q_gs, 1)

                @block.vector
                def _(dve):
                    dve.wait_ge(q_gs, 1)
                    for k in range(REL * NT):
                        r, n = k // NT, k % NT
                        dve.wait_ge(q_z, k + 1)
                        dve.tensor_scalar(Z[r][:, n], bank[k % 2][0:P, :], gate[:, n, r:r + 1], None, ALU.mult).then_inc(q_ze, 1)
                    for n in range(NT):
                        dve.wait_ge(q_o, n + 1)
                        o = bank[2 + n % 4][0:P, :]
                        if layer == 0:
                            dve.tensor_scalar(x3[:, n], o, 0.0, None, ALU.max).then_inc(q_e, 1)
                        else:
                            dve.wait_ge(x_sv, 32)
                            dve.tensor_tensor(x3[:, n], o, x3[:, n], ALU.add).then_inc(q_e, 1)
        norm_nodes("n3", x3)
        f_st = sem("f_st")
        with nc.Block() as block:
            @block.sync
            def _(sp):
                sp.dma_start(out.rearrange("(n p) f -> p n f", p=P), x3).then_inc(f_st, 16)
                sp.wait_ge(f_st, 16)


_NAMES = ["x", "src", "dst", "edge_attr_4", "edge_attr_8", "edge_type_2", "edge_weight",
          "L0_gnn_W_up0", "L0_gnn_W_up1", "L0_gnn_W_mlp1", "L0_gnn_W_mlp2", "L0_gnn_W_mlp3", "L0_gnn_W_mlp4",
          "L0_gnn_W_out0", "L0_gnn_W_out1", "L1_gnn_W_gcn", "L1_gnn_b_gcn", "L1_gnn_W_fc", "L1_gnn_b_fc",
          "L2_gnn_W_self", "L2_gnn_b_self", "L2_gnn_W_neigh", "L2_gnn_b_neigh",
          "L3_gnn_basis1", "L3_gnn_root1", "L3_gnn_bias1", "L3_gnn_basis2", "L3_gnn_root2", "L3_gnn_bias2"]


def kernel(**inputs):
    import numpy as np
    import concourse.bacc as bacc
    from concourse.bass_utils import run_bass_kernel_spmd

    nc = bacc.Bacc("TRN2", target_bir_lowering=False, num_devices=1)
    host = {name: np.ascontiguousarray(inputs[name]) for name in _NAMES}
    for k in (1, 2):
        host[f"att{k}_rep"] = np.ascontiguousarray(np.repeat(np.asarray(inputs[f"L3_gnn_att{k}"]).T, 4, axis=0))
        gate = np.asarray(inputs[f"L3_gnn_gate_w{k}"]).reshape(REL, FC, 128)
        host[f"gate_w{k}"] = np.ascontiguousarray(gate.transpose(2, 1, 0))
    host["ident"] = np.eye(128, dtype=np.float32)
    host["mask4"] = np.tile(np.tile(np.eye(4, dtype=np.float32), (BASES, 1)), (1, REL))
    aps = {}
    arrays = {}
    for name, a in host.items():
        arrays["in_" + name] = a
        aps[name] = nc.dram_tensor("in_" + name, a.shape, mybir.dt.from_np(a.dtype), kind="ExternalInput").ap()
    out = nc.dram_tensor("out_0", (NODES, D), F32, kind="ExternalOutput").ap()
    gnn_program(nc, aps, out)
    r = run_bass_kernel_spmd(nc, [arrays], core_ids=[0])
    return r.results[0]["out_0"]
```

```python
import concourse.bass as bass
from concourse import mybir
from concourse.alu_op_type import AluOpType as ALU
from contextlib import ExitStack
import math

F32 = mybir.dt.float32
I32 = mybir.dt.int32
I16 = mybir.dt.int16
BF16 = mybir.dt.bfloat16
ACT = mybir.ActivationFunctionType
AX = mybir.AxisListType

NODES, D, EDGES = 1250, 512, 20000
MUL = 128
P = 125
NP = 128
NT = -(-NODES // NP)
NALL = NT * NP
TAIL = NODES - (NT - 1) * NP
ET = EDGES // P
EH = ET // 2
W = 32
WPAD = NODES + W
BODY = 8
TURNS = ET // BODY
HID, RB = 64, 8
FC = D // 128
BASES, REL = 30, 2
SILU_2MOM = 1.679177
SPANS = [(0, 512), (512, 1024), (1024, 1280)]
IC = 8


def gnn_program(nc, A, out):
    ctx = ExitStack()
    with ctx:
        def sem(name):
            return ctx.enter_context(nc.semaphore(name))

        WORDS = 53100
        arena = ctx.enter_context(nc.sbuf_tensor("arena", [128, WORDS], F32))
        bank = [ctx.enter_context(nc.psum_tensor(f"bank{k}", [128, 512], F32)) for k in range(8)]

        def at(off, words, rows=128, dt=F32):
            assert off + words <= WORDS, (off, words)
            v = arena[0:rows, off:off + words]
            return v if dt == F32 else v.bitcast(dt)

        class Region:
            def __init__(self, lo, hi):
                self.at, self.hi = lo, hi

            def take(self, words, rows=128, dt=F32):
                off = self.at
                self.at += words + (words & 1)
                assert self.at <= self.hi, (self.at, self.hi)
                return at(off, words, rows, dt)

        SMALL = 2200
        AWORDS = NT * WPAD
        R1, R2 = SMALL, SMALL + AWORDS
        R3 = SMALL + 2 * AWORDS
        small = Region(0, SMALL)
        ident = small.take(128)
        onesM = small.take(128)
        iota32 = small.take(W, P)
        tab = small.take(3 * ET, 1, I32).rearrange("p (q t) -> p q t", q=3)
        turns_more = small.take(TURNS, 1, I32)
        invdeg = small.take(NT)
        eps = small.take(1)
        stats = small.take(NT * 6).rearrange("p (n s) -> p n s", n=NT)
        mv = small.take(NT * 2).rearrange("p (n s) -> p n s", n=NT)
        vare = small.take(NT)
        sd = small.take(NT)
        rs = small.take(NT)
        nt1 = small.take(NT)
        nt2 = small.take(NT)
        bgcn = small.take(1)
        brow = small.take(D, 1)
        brow2 = small.take(D, 1)

        AT = at(R1, AWORDS).rearrange("p (c n) -> p c n", c=NT)
        CNT = at(R2, AWORDS, 128, I16).rearrange("p (c n) -> p c n", c=NT)
        accT = at(R3, 8 * WPAD).rearrange("p (b n) -> p b n", b=8)
        edge = Region(R3 + 8 * WPAD, WORDS)
        rel = edge.take(ET, P)
        srcT = edge.take(ET, P)
        idx = edge.take(ET, 128, I32)
        yT = edge.take(4 * ET, P).rearrange("p (t m) -> p t m", m=4)
        valT = edge.take(5 * ET // 2, P, BF16).rearrange("p (t m) -> p t m", m=5)
        edge_mark = edge.at

        hD = nc.dram_tensor("h_scratch", (TURNS, 128, 4 * P), F32, kind="Internal").ap()
        upD = nc.dram_tensor("up_scratch", (NODES, D), F32, kind="Internal").ap()
        wD = nc.dram_tensor("w_scratch", (2, REL * 4, 128, D), F32, kind="Internal").ap()

        ph = Region(R1, R3)
        Lf = ph.take(2 * P * RB, EH).rearrange("p (b x) -> p b x", b=2)
        La = ph.take(2 * P * 4, EH).rearrange("p (b x) -> p b x", b=2)
        Li = ph.take(3 * 2 * P, EH, I32).rearrange("p (q b x) -> p q b x", q=3, b=2)
        Lq = ph.take(4 * 2 * P, EH).rearrange("p (q b x) -> p q b x", q=4, b=2)
        mnx = ph.take(2 * 2, EH).rearrange("p (q b) -> p q b", q=2)
        more = ph.take(2, EH)
        morei = ph.take(2, EH, I32)
        diag = ph.take(4 * EH, EH).rearrange("p (q b x) -> p q b x", q=2, b=2)
        FT = ph.take(ET * RB, P).rearrange("p (c s h j) -> p c s h j", s=4, h=2, j=RB)
        misc = ph.take(4 * ET, P).rearrange("p (q t) -> p q t", q=4)
        base = ph.take(ET, P)
        cum = ph.take(ET, 1)
        kf = ph.take(ET, 1)
        kt = ph.take(TURNS, 1)
        onesr = ph.take(ET, 1)
        wr1 = ph.take(ET, P)
        wr2 = ph.take(ET, P)
        W1b = ph.take(128)
        W2b = ph.take(128)
        W3b = ph.take(128)
        fT = ph.take(4 * 4 * P).rearrange("p (q x) -> p q x", q=4)
        hA = ph.take(4 * 4 * P).rearrange("p (q x) -> p q x", q=4)
        hB = ph.take(4 * 4 * P).rearrange("p (q x) -> p q x", q=4)
        hC = ph.take(4 * 4 * P).rearrange("p (q x) -> p q x", q=4)

        e_ld = sem("e_ld"); e_cst = sem("e_cst"); e_dve = sem("e_dve"); e_tr = sem("e_tr")
        e_bc = sem("e_bc"); e_q = sem("e_q")
        quantities = [(Lf, j, RB) for j in range(RB)] + [(La, m, 4) for m in range(4)] + [(Lq, q, 1) for q in range(4)]

        with nc.Block() as block:
            @block.sync
            def _(sp):
                sp.dma_start(ident, A["ident"]).then_inc(e_ld, 16)
                for q, name in enumerate(("src", "dst", "edge_type_2")):
                    sp.dma_start(Li[:, q], A[name].rearrange("(b p x) -> p b x", b=2, p=EH)).then_inc(e_ld, 16)
                sp.dma_start(Lq[:, 3], A["edge_weight"].rearrange("(b p x) -> p b x", b=2, p=EH)).then_inc(e_ld, 16)
                sp.dma_start(Lf, A["edge_attr_8"].rearrange("(b p x) j -> p b (x j)", b=2, p=EH)).then_inc(e_ld, 16)
                sp.dma_start(La, A["edge_attr_4"].rearrange("(b p x) j -> p b (x j)", b=2, p=EH)).then_inc(e_ld, 16)

            @block.gpsimd
            def _(pool):
                pool.memset(onesM, 1.0).then_inc(e_cst, 1)
                pool.memset(onesr, 1.0).then_inc(e_cst, 1)
                pool.memset(eps, 1e-5).then_inc(e_cst, 1)
                pool.memset(idx, 0).then_inc(e_cst, 1)
                pool.iota(iota32, pattern=[[1, W]], base=0, channel_multiplier=0,
                          allow_small_or_imprecise_dtypes=True).then_inc(e_cst, 1)

            @block.vector
            def _(dve):
                n = [0]

                def link(ins):
                    n[0] += 1
                    ins.then_inc(e_dve, 1)
                    dve.wait_ge(e_dve, n[0])
                dve.wait_ge(e_ld, 7 * 16)
                dve.wait_ge(e_cst, 5)
                link(dve.tensor_copy(Lq[:, 0:3], Li))
                link(dve.tensor_reduce(mnx[:, 0], Lq[:, 1], AX.X, ALU.min))
                link(dve.tensor_reduce(mnx[:, 1], Lq[:, 1], AX.X, ALU.max))
                link(dve.tensor_tensor(more, mnx[:, 1], mnx[:, 0], ALU.subtract))
                link(dve.tensor_copy(morei, more))
                link(dve.tensor_scalar(morei, morei, 5, None, ALU.arith_shift_right))
                link(dve.tensor_copy(more, morei))
                for b in range(2):
                    link(dve.tensor_scalar(diag[:, 0, b], ident[0:EH, 0:EH], mnx[:, 0, b:b + 1], None, ALU.mult))
                    link(dve.tensor_scalar(diag[:, 1, b], ident[0:EH, 0:EH], more[:, b:b + 1], None, ALU.mult))
                dve.sem_inc(e_q, 1)
                for k in range(6):
                    dve.wait_ge(e_tr, k + 1)
                    b, g = k // 3, k % 3
                    ts = slice(b * EH, (b + 1) * EH)
                    for s, (_, j, step) in enumerate(quantities[6 * g:6 * g + 6]):
                        src = bank[k][0:P, s * EH:(s + 1) * EH]
                        if step == RB:
                            dst = FT[:, b * TURNS // 2:(b + 1) * TURNS // 2, :, :, j].rearrange("p c s h -> p c h s")
                            src = src.rearrange("p (c h s) -> p c h s", h=2, s=4)
                        elif step == 4:
                            dst = yT[:, ts, j]
                        else:
                            dst = misc[:, j, ts]
                        link(dve.tensor_copy(dst, src))
                dve.wait_ge(e_bc, 1)
                link(dve.tensor_copy(base, bank[6][0:P, 0:ET]))
                link(dve.tensor_tensor(rel, misc[:, 1], base, ALU.subtract))
                link(dve.tensor_copy(srcT, misc[:, 0]))
                link(dve.tensor_copy(idx[0:P], misc[:, 0]))
                link(dve.tensor_copy(tab[:, 0], base[0:1]))
                link(dve.tensor_copy(kf, bank[6][0:1, ET:2 * ET]))
                link(dve.tensor_copy(tab[:, 1], kf))
                link(dve.tensor_reduce(kt, kf.rearrange("p (i j) -> p i j", j=BODY), AX.X, ALU.add))
                link(dve.tensor_copy(turns_more, kt))
                link(dve.tensor_tensor_scan(cum, onesr, kf, 0.0, ALU.mult, ALU.add))
                link(dve.tensor_tensor(cum, cum, kf, ALU.subtract))
                link(dve.tensor_copy(tab[:, 2], cum))
                link(dve.tensor_copy(valT[:, :, 2], misc[:, 3]))
                link(dve.tensor_tensor(wr1, misc[:, 3], valT[:, :, 2], ALU.subtract))
                link(dve.tensor_copy(valT[:, :, 0], wr1))
                link(dve.tensor_tensor(wr2, wr1, valT[:, :, 0], ALU.subtract))
                link(dve.tensor_copy(valT[:, :, 1], wr2))
                link(dve.tensor_scalar(valT[:, :, 3], misc[:, 2], 0.0, None, ALU.is_equal))
                link(dve.tensor_scalar(valT[:, :, 4], misc[:, 2], 0.0, None, ALU.not_equal))

            @block.tensor
            def _(pe):
                pe.wait_ge(e_q, 1)
                pe.wait_ge(e_dve, 11)
                for k in range(6):
                    b, g = k // 3, k % 3
                    for s, (Lx, j, step) in enumerate(quantities[6 * g:6 * g + 6]):
                        if step == 1:
                            in_ = Lx[:, j, b, :]
                        else:
                            in_ = Lx[:, b, :].rearrange("p (x j) -> p j x", j=step)[:, j, :]
                        last = pe.transpose(bank[k][0:P, s * EH:(s + 1) * EH], in_, ident[0:EH, 0:EH])
                    last.then_inc(e_tr, 1)
                for q in range(2):
                    for b in range(2):
                        last = pe.matmul(bank[6][0:P, q * ET + b * EH:q * ET + (b + 1) * EH],
                                         onesM[0:EH, 0:P], diag[:, q, b], start=True, stop=True)
                last.then_inc(e_bc, 1)

        m_ld = sem("m_ld"); m_z = sem("m_z"); m_t = sem("m_t"); m_f = sem("m_f"); m_mm = sem("m_mm"); m_h = sem("m_h")
        m_st = [sem(f"m_st{q}") for q in range(4)]
        GROUPS = TURNS // 4
        layer_in = [fT, hA, hB]
        layer_out = [hA, hB, hC]
        layer_w = [W1b, W2b, W3b]
        scales = [1.0 / math.sqrt(RB), SILU_2MOM / math.sqrt(HID), SILU_2MOM / math.sqrt(HID)]
        with nc.Block() as block:
            @block.sync
            def _(sp):
                sp.wait_ge(m_z, 3)
                for half in range(2):
                    k, c = slice(half * RB, (half + 1) * RB), slice(half * HID, (half + 1) * HID)
                    sp.dma_start(W1b[k, c], A["L0_gnn_W_mlp1"]).then_inc(m_ld, 16)
                    sp.dma_start(W2b[c, c], A["L0_gnn_W_mlp2"]).then_inc(m_ld, 16)
                    sp.dma_start(W3b[c, c], A["L0_gnn_W_mlp3"]).then_inc(m_ld, 16)
                for g in range(GROUPS):
                    for q in range(4):
                        sp.wait_ge(m_h, g * 12 + 8 + q + 1)
                        sp.dma_start(hD[g * 4 + q], hC[:, q]).then_inc(m_st[q], 16)
                for q in range(4):
                    sp.wait_ge(m_st[q], 16 * GROUPS)

            @block.gpsimd
            def _(pool):
                for w in layer_w:
                    pool.memset(w, 0.0).then_inc(m_z, 1)

            @block.vector
            def _(dve):
                for g in range(GROUPS):
                    for q in range(4):
                        dve.wait_ge(m_t, g * 4 + q + 1)
                        if g:
                            dve.wait_ge(m_mm, (g - 1) * 12 + q + 1)
                        dve.tensor_copy(fT[0:2 * RB, q], bank[q][0:2 * RB, 0:4 * P]).then_inc(m_f, 1)

            @block.tensor
            def _(pe):
                pe.wait_ge(m_ld, 6 * 16)
                for g in range(GROUPS):
                    for q in range(4):
                        c = g * 4 + q
                        if g:
                            pe.wait_ge(m_f, (g - 1) * 4 + q + 1)
                        for s in range(4):
                            last = pe.transpose(bank[q][0:2 * RB, s * P:(s + 1) * P],
                                                FT[:, c, s].rearrange("p h j -> p (h j)"), ident[0:P, 0:P])
                        last.then_inc(m_t, 1)
                    for layer in range(3):
                        for q in range(4):
                            if layer == 0:
                                pe.wait_ge(m_f, g * 4 + q + 1)
                                if g:
                                    pe.wait_ge(m_h, (g - 1) * 12 + 8 + q + 1)
                                k = 2 * RB
                            else:
                                pe.wait_ge(m_h, g * 12 + (layer - 1) * 4 + q + 1)
                                k = 128
                            pe.matmul(bank[4 + q][:, 0:4 * P], layer_w[layer][0:k], layer_in[layer][0:k, q],
                                      start=True, stop=True).then_inc(m_mm, 1)

            @block.scalar
            def _(act):
                for g in range(GROUPS):
                    for layer in range(3):
                        for q in range(4):
                            act.wait_ge(m_mm, g * 12 + layer * 4 + q + 1)
                            if layer == 2 and g:
                                act.wait_ge(m_st[q], 16 * g)
                            act.activation(layer_out[layer][:, q], bank[4 + q][:, 0:4 * P], ACT.Silu,
                                           scale=scales[layer]).then_inc(m_h, 1)

        ph = Region(R1, R3)
        bas = [ph.take(IC * D, 4 * BASES) for _ in range(3)]
        mask = ph.take(8, 4 * BASES)
        attp = ph.take(4, 4 * BASES)
        attL = ph.take(2 * 32, 4 * BASES).rearrange("p (l m) -> p l m", l=2)
        stage = [ph.take(IC // 4 * D).rearrange("p (k o) -> p k o", o=D) for _ in range(2)]
        NB = 128 // IC
        b_ld = [sem(f"b_ld{k}") for k in range(3)]
        b_c = sem("b_c"); b_z = sem("b_z"); b_at = sem("b_at"); b_mm = sem("b_mm"); b_ev = sem("b_ev")
        b_st = [sem("b_st0"), sem("b_st1")]
        with nc.Block() as block:
            @block.sync
            def _(sp):
                sp.dma_start(mask, A["mask4"]).then_inc(b_c, 16)
                sp.dma_start(attp[:, 0:2], A["att1_rep"]).then_inc(b_c, 16)
                sp.dma_start(attp[:, 2:4], A["att2_rep"]).then_inc(b_c, 16)
                for u in range(2 * NB):
                    if u >= 3:
                        sp.wait_ge(b_mm, (u - 2) * (IC // 4))
                    layer, c = u // NB, u % NB
                    v = A[f"L3_gnn_basis{layer + 1}"].rearrange("b (q i) o -> (b q) (i o)", q=4)
                    sp.dma_start(bas[u % 3], v[:, c * IC * D:(c + 1) * IC * D]).then_inc(b_ld[u % 3], 16)

            @block.vector
            def _(dve):
                dve.memset(attL, 0.0).then_inc(b_z, 1)
                dve.wait_ge(b_z, 1)
                dve.wait_ge(b_c, 48)
                for layer in range(2):
                    for r in range(REL):
                        dve.tensor_scalar(attL[:, layer, 4 * r:4 * r + 4], mask[:, 4 * r:4 * r + 4],
                                          attp[:, 2 * layer + r:2 * layer + r + 1], None, ALU.mult).then_inc(b_at, 1)

            @block.tensor
            def _(pe):
                pe.wait_ge(b_at, 4)
                for u in range(2 * NB):
                    pe.wait_ge(b_ld[u % 3], 16 * (u // 3 + 1))
                    for k in range(IC // 4):
                        g = u * (IC // 4) + k
                        if g >= 4:
                            pe.wait_ge(b_ev, g - 3)
                        for s in range(4):
                            last = pe.matmul(bank[g % 4][32 * s:32 * s + 32, :], attL[:, u // NB],
                                             bas[u % 3][:, (4 * k + s) * D:(4 * k + s + 1) * D], start=True, stop=True)
                        last.then_inc(b_mm, 1)

            @block.scalar
            def _(act):
                for u in range(2 * NB):
                    layer, c = u // NB, u % NB
                    for k in range(IC // 4):
                        g = u * (IC // 4) + k
                        if u >= 2 and k == 0:
                            act.wait_ge(b_st[u % 2], 64 * (u // 2))
                        act.wait_ge(b_mm, g + 1)
                        act.activation(stage[u % 2][:, k], bank[g % 4][:, :], ACT.Copy).then_inc(b_ev, 1)
                    act.wait_ge(b_ev, (u + 1) * (IC // 4))
                    for s in range(4):
                        act.dma_start(wD[layer].rearrange("m (k s) o -> s m k o", s=4)[s, :, c * (IC // 4):(c + 1) * (IC // 4)],
                                      stage[u % 2][32 * s:32 * s + 8]).then_inc(b_st[u % 2], 16)
                for k in range(2):
                    act.wait_ge(b_st[k], 64 * NB)

        def transpose_nodes(tag, xs, xT, cols):
            t_pe, t_ev = sem(tag + "_tr"), sem(tag + "_ev")
            with nc.Block() as block:
                @block.tensor
                def _(pe):
                    for n in range(NT):
                        if n >= 2:
                            pe.wait_ge(t_ev, n - 1)
                        for c in range(FC):
                            last = pe.transpose(bank[n % 2][:, c * NP:(c + 1) * NP], cols(xs[:, n], c), ident)
                        last.then_inc(t_pe, 1)

                @block.vector
                def _(dve):
                    for n in range(NT):
                        dve.wait_ge(t_pe, n + 1)
                        dve.tensor_copy(xT[:, :, n * NP:(n + 1) * NP],
                                        bank[n % 2][:, 0:FC * NP].rearrange("p (c x) -> p c x", c=FC)).then_inc(t_ev, 1)

        def load_nodes(sp, xs, cleared, loaded):
            whole = (NT - 1) * NP
            sp.dma_start(xs[:, 0:NT - 1], A["x"][0:whole].rearrange("(n p) f -> p n f", p=NP)).then_inc(loaded, 16)
            sp.wait_ge(cleared, 1)
            sp.dma_start(xs[0:TAIL, NT - 1], A["x"][whole:NODES]).then_inc(loaded, 16)

        def plain_cols(x, c):
            return x[:, c * 128:(c + 1) * 128]

        def norm_nodes(tag, xs):
            d, a = sem(tag + "_d"), sem(tag + "_a")
            with nc.Block() as block:
                @block.vector
                def _(dve):
                    k = [0]

                    def link(ins):
                        k[0] += 1
                        ins.then_inc(d, 1)
                        dve.wait_ge(d, k[0])
                    for n in range(NT):
                        dve.bn_stats(stats[:, n], xs[:, n]).then_inc(d, 1)
                    k[0] = NT
                    dve.wait_ge(d, NT)
                    for n in range(NT):
                        dve.bn_aggr(mv[:, n], stats[:, n]).then_inc(d, 1)
                    k[0] = 2 * NT
                    dve.wait_ge(d, 2 * NT)
                    link(dve.tensor_scalar(vare, mv[:, :, 1], 1e-5, None, ALU.add))
                    dve.wait_ge(a, 1)
                    link(dve.reciprocal(rs, sd))
                    link(dve.tensor_tensor(nt1, rs, rs, ALU.mult))
                    link(dve.tensor_tensor(nt2, nt1, vare, ALU.mult))
                    link(dve.tensor_scalar(nt1, nt2, -0.5, 1.5, ALU.mult, ALU.add))
                    link(dve.tensor_tensor(nt2, rs, nt1, ALU.mult))
                    for n in range(NT):
                        dve.tensor_scalar(xs[:, n], xs[:, n], mv[:, n, 0:1], nt2[:, n:n + 1],
                                          ALU.subtract, ALU.mult).then_inc(d, 1)

                @block.scalar
                def _(act):
                    act.wait_ge(d, 2 * NT + 1)
                    act.activation(sd, vare, ACT.Sqrt).then_inc(a, 1)

        ph = Region(R1, R3)
        xs0 = ph.take(NT * D).rearrange("p (n f) -> p n f", n=NT)
        xT0 = ph.take(FC * NALL).rearrange("p (c n) -> p c n", c=FC)
        wup = ph.take(2 * 128).rearrange("p (q n) -> p q n", q=2)
        upS = [ph.take(D) for _ in range(2)]
        u_z = sem("u_z"); u_ld = sem("u_ld"); u_mm = sem("u_mm"); u_ev = sem("u_ev")
        u_st = [sem("u_st0"), sem("u_st1")]
        with nc.Block() as block:
            @block.sync
            def _(sp):
                load_nodes(sp, xs0, u_z, u_ld)
                sp.dma_start(wup[:, 0], A["L0_gnn_W_up0"]).then_inc(u_ld, 16)
                sp.dma_start(wup[:, 1], A["L0_gnn_W_up1"]).then_inc(u_ld, 16)
                sp.wait_ge(u_ld, 64)

            @block.gpsimd
            def _(pool):
                pool.memset(xs0[:, NT - 1], 0.0).then_inc(u_z, 1)

        def irrep_cols(x, c):
            return x[:, 0:MUL] if c == 0 else x[:, MUL:].rearrange("p (u m) -> p m u", m=3)[:, c - 1]
        transpose_nodes("t0", xs0, xT0, irrep_cols)
        with nc.Block() as block:
            @block.tensor
            def _(pe):
                for n in range(NT):
                    if n >= 2:
                        pe.wait_ge(u_ev, n - 1)
                    for c in range(FC):
                        last = pe.matmul(bank[n % 2][:, c * 128:(c + 1) * 128], xT0[:, c, n * NP:(n + 1) * NP],
                                         wup[:, min(c, 1)], start=True, stop=True)
                    last.then_inc(u_mm, 1)

            @block.scalar
            def _(act):
                for n in range(NT):
                    act.wait_ge(u_mm, n + 1)
                    if n >= 2:
                        act.wait_ge(u_st[n % 2], 16 * (n // 2))
                    act.activation(upS[n % 2], bank[n % 2][:, :], ACT.Copy, scale=1.0 / math.sqrt(MUL)).then_inc(u_ev, 1)

            @block.sync
            def _(sp):
                for n in range(NT):
                    sp.wait_ge(u_ev, n + 1)
                    rows = min(NP, NODES - n * NP)
                    sp.dma_start(upD[n * NP:n * NP + rows, :], upS[n % 2][0:rows]).then_inc(u_st[n % 2], 16)
                for k in range(2):
                    sp.wait_ge(u_st[k], 16 * (NT // 2))

        edge.at = edge_mark
        G = [edge.take(D) for _ in range(BODY)]
        hS = edge.take(4 * P).rearrange("p (s e) -> p s e", s=4)
        W4 = edge.take(4 * MUL)
        M = [edge.take(8 * MUL, P).rearrange("p (b u) -> p b u", b=8) for _ in range(2)]
        Ss = [edge.take(NALL // 2, P, BF16) for _ in range(2)]
        iotaN = edge.take(NALL // 2, P, I16)
        eq = [edge.take(W, P) for _ in range(2)]
        Sy = [edge.take(4 * W, P).rearrange("p (m w) -> p m w", m=4) for _ in range(2)]
        Sw = [edge.take(5 * W // 2, P, BF16) for _ in range(2)]
        ring = edge.take(BODY, 128, I32)
        relx = edge.take(2, P)
        wsteps = edge.take(NODES // W + 1, P)

        z = sem("z"); w4_ld = sem("w4_ld")
        h_ld = [sem(f"h_ld{j}") for j in range(BODY)]
        gathered = [sem(f"gathered{j}") for j in range(BODY)]
        tpw_ready = sem("tpw_ready")
        prod_done = sem("prod_done")
        send_ready = sem("send_ready")
        recv_ready = sem("recv_ready")
        visit_done = sem("visit_done")
        acc_done = sem("acc_done")
        eq_done = sem("eq_done"); passed = sem("passed"); ring_done = sem("ring_done")
        x_eq = sem("x_eq"); x_rel = sem("x_rel")
        x_ready = sem("x_ready"); x_done = sem("x_done")
        x_acc = sem("x_acc")
        TP, MSG, BLD = (6, 7), (0, 1), (2, 4)

        def either(eng, i, turn):
            col = slice(i, i + 1) if isinstance(i, int) else bass.ds(i, 1)
            some = eng.value_load(turns_more[:, col], min_val=0, max_val=BODY * (NODES // W))
            with eng.If(some > 0):
                turn(True)
            with eng.Else():
                turn(False)

        def tile_numbers(eng, t):
            col = slice(t, t + 1) if isinstance(t, int) else bass.ds(t, 1)
            further = eng.value_load(tab[:, 1, col], min_val=0, max_val=NODES // W)
            seen = eng.value_load(tab[:, 2, col], min_val=0, max_val=ET * (NODES // W))
            return further, seen

        with nc.Block() as block:
            @block.sync
            def _(sp):
                for half in range(2):
                    sp.dma_start(W4[half * HID:(half + 1) * HID], A["L0_gnn_W_mlp4"]).then_inc(w4_ld, 16)

                def load(turn, j):
                    half = slice(j // 4 * HID, (j // 4 + 1) * HID)
                    src = hD[turn] if isinstance(turn, int) else hD[bass.ds(turn, 1)].rearrange("a p x -> (a p) x")
                    sp.dma_start(hS[half, j % 4], src[half, j % 4 * P:(j % 4 + 1) * P]).then_inc(h_ld[j], 16)
                for j in range(BODY):
                    load(0, j)
                with sp.Fori(0, TURNS - 1) as i:
                    for j in range(BODY):
                        sp.wait_ge(tpw_ready, i * BODY + j + 1)
                        load(i + 1, j)

            @block.gpsimd
            def _(pool):
                pool.iota(iotaN, pattern=[[1, NALL]], base=0, channel_multiplier=0,
                          allow_small_or_imprecise_dtypes=True).then_inc(z, 1)
                pool.iota(wsteps, pattern=[[-W, NODES // W + 1]], base=-W, channel_multiplier=0,
                          allow_small_or_imprecise_dtypes=True).then_inc(z, 1)
                for j in range(BODY):
                    pool.indirect_dma_start(out=G[j], out_offset=None, in_=upD,
                                            in_offset=bass.IndirectOffsetOnAxis(idx[:, j:j + 1], 0)).then_inc(gathered[j], 16)

                def onehots(p, t, ready, eqs, n):
                    pool.wait_ge(eqs, n)
                    pool.sem_inc(passed, 1)
                    e = eq[p]
                    col = slice(t, t + 1) if isinstance(t, int) else bass.ds(t, 1)
                    y = yT[:, col].rearrange("p a m -> p (a m)")
                    v = valT[:, col].rearrange("p a m -> p (a m)")
                    pool.tensor_tensor(Sy[p], e.unsqueeze(1).to_broadcast([P, 4, W]),
                                       y.unsqueeze(2).to_broadcast([P, 4, W]), ALU.mult).then_inc(ready, 1)
                    pool.tensor_tensor(Sw[p][:, 0:3 * W].rearrange("p (m w) -> p m w", m=3),
                                       e.unsqueeze(1).to_broadcast([P, 3, W]),
                                       v[:, 0:3].unsqueeze(2).to_broadcast([P, 3, W]), ALU.mult).then_inc(ready, 1)
                    pool.tensor_tensor(Sw[p][:, 3 * W:5 * W].rearrange("p (w r) -> p w r", r=2),
                                       e.unsqueeze(2).to_broadcast([P, W, 2]),
                                       v[:, 3:5].unsqueeze(1).to_broadcast([P, W, 2]), ALU.mult).then_inc(ready, 1)

                def turn(i, last, look):
                    for j in range(BODY):
                        t, p = i * BODY + j, j % 2
                        onehots(p, t, recv_ready, eq_done, t + 1)
                        if look:
                            further, seen = tile_numbers(pool, t)
                            with pool.If(further > 0):
                                with pool.Fori(0, further) as k:
                                    onehots(p, t, x_ready, x_eq, seen + k + 1)
                        if not last:
                            pool.wait_ge(prod_done, t + 2)
                            pool.sem_inc(passed, 1)
                            pool.tensor_copy(ring[:, j:j + 1], idx[:, bass.ds(t + BODY, 1)]).then_inc(ring_done, 1)
                            pool.wait_ge(ring_done, t + 1)
                            pool.sem_inc(passed, 1)
                            pool.indirect_dma_start(out=G[j], out_offset=None, in_=upD,
                                                    in_offset=bass.IndirectOffsetOnAxis(ring[:, j:j + 1], 0)).then_inc(gathered[j], 16)
                with pool.Fori(0, TURNS - 1) as i:
                    either(pool, i, lambda look: turn(i, False, look))
                either(pool, TURNS - 1, lambda look: turn(TURNS - 1, True, look))

            @block.vector
            def _(dve):
                dve.sem_inc(prod_done, 1)
                dve.sem_inc(acc_done, 2)
                dve.sem_inc(x_acc, 1)
                dve.memset(AT, 0.0).then_inc(z, 1)
                dve.memset(CNT, 0).then_inc(z, 1)
                dve.memset(accT, 0.0).then_inc(z, 1)
                dve.wait_ge(z, 5)

                def products(turn, j):
                    t, p, g = turn * BODY + j, j % 2, G[j][0:P]
                    col = slice(t, t + 1) if isinstance(t, int) else bass.ds(t, 1)
                    dve.tensor_scalar(eq[p], iota32, rel[:, col], None, ALU.is_equal).then_inc(eq_done, 1)
                    dve.wait_ge(gathered[j], turn * 16 + 16)
                    dve.wait_ge(tpw_ready, t + 1)
                    tp = bank[TP[p]][0:P, :].rearrange("p (b u) -> p b u", b=4)
                    dve.tensor_tensor(M[p][:, 0:2], tp[:, 0:2],
                                      g[:, 0:MUL].unsqueeze(1).to_broadcast([P, 2, MUL]), ALU.mult)
                    dve.tensor_tensor(M[p][:, 2:8].rearrange("p (b m) u -> p b m u", b=2),
                                      tp[:, 2:4].unsqueeze(2).to_broadcast([P, 2, 3, MUL]),
                                      g[:, MUL:].rearrange("p (m u) -> p m u", m=3).unsqueeze(1).to_broadcast([P, 2, 3, MUL]),
                                      ALU.mult).then_inc(prod_done, 1)
                    dve.tensor_scalar(Ss[p], iotaN, srcT[:, col], None, ALU.is_equal).then_inc(send_ready, 1)

                def accumulate(p, at_node, done):
                    w = bass.ds(at_node, W)
                    dve.tensor_tensor(accT[:, :, w], accT[:, :, w],
                                      bank[MSG[p]][:, 0:8 * W].rearrange("p (b w) -> p b w", b=8), ALU.add)
                    for h in range(2):
                        ps = bank[BLD[p] + h][:, 0:15 * W].rearrange("p (c x) -> p c x", c=5)
                        cs = slice(5 * h, 5 * h + 5)
                        a, c = AT[:, cs, w], CNT[:, cs, bass.ds(at_node * 2, 2 * W)]
                        dve.tensor_tensor(a, a, ps[:, :, 0:W], ALU.add)
                        last = dve.tensor_tensor(c, c, ps[:, :, W:3 * W], ALU.add)
                    last.then_inc(done, 1)

                def settle(i, j, look):
                    t, p = i * BODY + j, j % 2
                    col = slice(t, t + 1) if isinstance(t, int) else bass.ds(t, 1)
                    start = dve.value_load(tab[:, 0, col], min_val=0, max_val=NODES - 1)
                    if look:
                        further, seen = tile_numbers(dve, t)
                    dve.wait_ge(visit_done, t + 3)
                    dve.wait_ge(acc_done, t + 2)
                    if look:
                        dve.wait_ge(x_acc, seen + 1)
                    accumulate(p, start, acc_done)
                    if look:
                        with dve.If(further > 0):
                            with dve.Fori(0, further) as k:
                                dve.wait_ge(acc_done, t + 3)
                                dve.wait_ge(x_acc, seen + k + 1)
                                dve.tensor_tensor(relx[:, 0:1], rel[:, col], wsteps[:, bass.ds(k, 1)], ALU.add).then_inc(x_rel, 1)
                                dve.wait_ge(x_rel, seen + k + 1)
                                dve.tensor_scalar(eq[p], iota32, relx[:, 0:1], None, ALU.is_equal).then_inc(x_eq, 1)
                                dve.wait_ge(x_done, seen + k + 1)
                                node = nc.s_assert_within(
                                    start + (k + 1) * W, 0, NODES - 1,
                                    skip_runtime_bounds_check_because="the last window starts at or before the largest receiver")
                                accumulate(p, node, x_acc)

                def turn(i, last, look):
                    if not look:
                        _, seen = tile_numbers(dve, i * BODY)
                        dve.wait_ge(x_acc, seen + 1)
                    for j in range(BODY):
                        if not (last and j == BODY - 1):
                            products(i + (j + 1) // BODY, (j + 1) % BODY)
                        settle(i, j, look)

                products(0, 0)
                with dve.Fori(0, TURNS - 1) as i:
                    either(dve, i, lambda look: turn(i, False, look))
                either(dve, TURNS - 1, lambda look: turn(TURNS - 1, True, look))

            @block.tensor
            def _(pe):
                pe.sem_inc(visit_done, 2)
                pe.wait_ge(w4_ld, 32)

                def weights(turn, j):
                    half = slice(j // 4 * HID, (j // 4 + 1) * HID)
                    pe.wait_ge(h_ld[j], turn * 16 + 16)
                    pe.matmul(bank[TP[j % 2]][0:P, :], hS[half, j % 4], W4[half, :], start=True, stop=True).then_inc(tpw_ready, 1)

                def visit(p, done):
                    msg, m = bank[MSG[p]], M[p]
                    sy = Sy[p].rearrange("p m w -> p (m w)")
                    pe.matmul(msg[:, 0:4 * W], m[:, 0], sy, start=True, stop=True)
                    pe.matmul(msg[:, W:4 * W], m[:, 1], sy[:, W:], start=True, stop=True)
                    for k in range(3):
                        pe.matmul(msg[:, (4 + k) * W:(8 + k) * W], m[:, 2 + k], sy, start=True, stop=True)
                    for k in range(3):
                        pe.matmul(msg[:, 7 * W:(10 - k) * W], m[:, 5 + k], sy[:, (1 + k) * W:], start=(k == 0), stop=(k == 2))
                    for c in range(NT):
                        b, o = bank[BLD[p] + c // 5], c % 5 * 3 * W
                        s = Ss[p][:, c * NP:(c + 1) * NP]
                        pe.matmul(b[:, o:o + 3 * W], s, Sw[p][:, 2 * W:5 * W], start=True, stop=False)
                        pe.matmul(b[:, o:o + W], s, Sw[p][:, 0:W], start=False, stop=False)
                        last = pe.matmul(b[:, o:o + W], s, Sw[p][:, W:2 * W], start=False, stop=True)
                    last.then_inc(done, 1)

                def turn(i, last, look):
                    for j in range(BODY):
                        t = i * BODY + j
                        if not (last and j == BODY - 1):
                            pe.wait_ge(prod_done, t + 1)
                            weights(i + (j + 1) // BODY, (j + 1) % BODY)
                        pe.wait_ge(prod_done, t + 2)
                        pe.wait_ge(send_ready, t + 1)
                        pe.wait_ge(recv_ready, t * 3 + 3)
                        pe.wait_ge(acc_done, t + 1)
                        visit(j % 2, visit_done)
                        if look:
                            further, seen = tile_numbers(pe, t)
                            with pe.If(further > 0):
                                with pe.Fori(0, further) as k:
                                    pe.wait_ge(x_ready, (seen + k) * 3 + 3)
                                    visit(j % 2, x_done)
                weights(0, 0)
                with pe.Fori(0, TURNS - 1) as i:
                    either(pe, i, lambda look: turn(i, False, look))
                either(pe, TURNS - 1, lambda look: turn(TURNS - 1, True, look))

        xs = at(R3 + 8 * WPAD, NT * D).rearrange("p (n f) -> p n f", n=NT)
        ph = Region(R3 + 8 * WPAD + NT * D, WORDS)
        wout = ph.take(4 * 128).rearrange("p (q n) -> p q n", q=4)
        o_z = sem("o_z"); o_ld = sem("o_ld"); o_w = sem("o_w"); o_mm = sem("o_mm"); o_ev = sem("o_ev")
        with nc.Block() as block:
            @block.sync
            def _(sp):
                load_nodes(sp, xs, o_z, o_ld)
                sp.dma_start(wout[:, 0:2], A["L0_gnn_W_out0"].rearrange("(q p) n -> p q n", q=2)).then_inc(o_ld, 16)
                sp.dma_start(wout[:, 2:4], A["L0_gnn_W_out1"].rearrange("(q p) n -> p q n", q=2)).then_inc(o_ld, 16)

            @block.gpsimd
            def _(pool):
                pool.memset(xs[:, NT - 1], 0.0).then_inc(o_z, 1)

            @block.tensor
            def _(pe):
                pe.wait_ge(o_w, 1)
                for n in range(NT):
                    if n >= 2:
                        pe.wait_ge(o_ev, 2 * (n - 1))
                    ns = slice(n * NP, (n + 1) * NP)
                    for q in range(4):
                        first, second = (0, 7) if q == 0 else (q, 3 + q)
                        o = bank[n % 2][:, q * 128:(q + 1) * 128]
                        pe.matmul(o, accT[:, first, ns], wout[:, 0 if q == 0 else 2], start=True, stop=False)
                        last = pe.matmul(o, accT[:, second, ns], wout[:, 1 if q == 0 else 3], start=False, stop=True)
                    last.then_inc(o_mm, 1)

            @block.vector
            def _(dve):
                dve.wait_ge(o_ld, 64)
                dve.tensor_scalar(wout[:, 1], wout[:, 1], 1.0 / math.sqrt(3.0), None, ALU.mult).then_inc(o_w, 1)
                c = SILU_2MOM / math.sqrt(HID) / math.sqrt(2 * MUL) / 10.0
                for n in range(NT):
                    dve.wait_ge(o_mm, n + 1)
                    b = bank[n % 2][:, :]
                    dve.scalar_tensor_tensor(xs[:, n, 0:MUL], b[:, 0:MUL], c, xs[:, n, 0:MUL], ALU.mult, ALU.add).then_inc(o_ev, 1)
                    v = xs[:, n, MUL:].rearrange("p (u m) -> p m u", m=3)
                    dve.scalar_tensor_tensor(v, b[:, MUL:].rearrange("p (m u) -> p m u", m=3), c, v,
                                             ALU.mult, ALU.add).then_inc(o_ev, 1)
        norm_nodes("n0", xs)

        xT = at(R3, FC * NALL).rearrange("p (c n) -> p c n", c=FC)
        xnT = at(R3 + FC * NALL, FC * NALL).rearrange("p (c n) -> p c n", c=FC)
        transpose_nodes("t1", xs, xT, plain_cols)
        ph = Region(R3 + 8 * WPAD + NT * D, WORDS)
        wg = ph.take(FC * 128).rearrange("p (c n) -> p c n", c=FC)
        wf = ph.take(FC * 128).rearrange("p (c n) -> p c n", c=FC)
        wfT = ph.take(D)
        xw = ph.take(NT * 128).rearrange("p (n f) -> p n f", n=NT)
        hT = ph.take(NALL)
        g_ld = sem("g_ld"); g_wt = sem("g_wt"); g_mm = sem("g_mm"); g_ev = sem("g_ev"); g_dg = sem("g_dg")
        g_hm = sem("g_hm"); g_he = sem("g_he"); g_o = sem("g_o"); g_x = sem("g_x"); g_d2 = sem("g_d2")
        with nc.Block() as block:
            @block.sync
            def _(sp):
                sp.dma_start(wg, A["L1_gnn_W_gcn"].rearrange("(c p) n -> p c n", c=FC)).then_inc(g_ld, 16)
                sp.dma_start(wf, A["L1_gnn_W_fc"].rearrange("(c p) n -> p c n", c=FC)).then_inc(g_ld, 16)
                sp.dma_start(bgcn, A["L1_gnn_b_gcn"].rearrange("(p a) -> p a", a=1)).then_inc(g_ld, 16)
                sp.dma_start(brow, A["L1_gnn_b_fc"].rearrange("(a n) -> a n", a=1)).then_inc(g_ld, 16)

            @block.tensor
            def _(pe):
                pe.wait_ge(g_ld, 64)
                for c in range(FC):
                    last = pe.transpose(bank[7][:, c * 128:(c + 1) * 128], wf[:, c], ident)
                last.then_inc(g_wt, 1)
                for n in range(NT):
                    if n >= 2:
                        pe.wait_ge(g_ev, n - 1)
                    for c in range(FC):
                        last = pe.matmul(bank[n % 2][:, 0:128], xT[:, c, n * NP:(n + 1) * NP], wg[:, c],
                                         start=(c == 0), stop=(c == FC - 1))
                    last.then_inc(g_mm, 1)
                for n in range(NT):
                    for s in range(NT):
                        last = pe.matmul(bank[6][:, n:n + 1], AT[:, s, n * NP:(n + 1) * NP], onesM[:, 0:1],
                                         start=(s == 0), stop=(s == NT - 1))
                last.then_inc(g_dg, 1)
                pe.wait_ge(g_ev, NT)
                for k, (lo, hi) in enumerate(SPANS):
                    for s in range(NT):
                        last = pe.matmul(bank[2 + k][:, 0:hi - lo], xw[:, s], AT[:, s, lo:hi],
                                         start=(s == 0), stop=(s == NT - 1))
                    last.then_inc(g_hm, 1)
                pe.wait_ge(g_he, 3)
                pe.wait_ge(g_wt, 2)
                for n in range(NT):
                    if n >= 2:
                        pe.wait_ge(g_x, n - 1)
                    pe.matmul(bank[n % 2][:, :], hT[:, n * NP:(n + 1) * NP], wfT, start=True, stop=False)
                    pe.matmul(bank[n % 2][:, :], onesM[0:1, :], brow, start=False, stop=True).then_inc(g_o, 1)

            @block.scalar
            def _(act):
                act.wait_ge(g_wt, 1)
                act.activation(wfT, bank[7][:, :], ACT.Copy).then_inc(g_wt, 1)
                for k, (lo, hi) in enumerate(SPANS):
                    act.wait_ge(g_hm, k + 1)
                    act.activation(hT[:, lo:hi], bank[2 + k][:, 0:hi - lo], ACT.Identity, bias=bgcn).then_inc(g_he, 1)

            @block.vector
            def _(dve):
                for n in range(NT):
                    dve.wait_ge(g_mm, n + 1)
                    dve.tensor_copy(xw[:, n], bank[n % 2][:, 0:128]).then_inc(g_ev, 1)
                dve.wait_ge(g_dg, 1)
                dve.tensor_scalar(invdeg, bank[6][:, 0:NT], 1.0, None, ALU.max).then_inc(g_d2, 1)
                dve.wait_ge(g_d2, 1)
                dve.reciprocal(nt1, invdeg).then_inc(g_d2, 1)
                dve.wait_ge(g_d2, 2)
                dve.tensor_copy(invdeg, nt1).then_inc(g_d2, 1)
                for n in range(NT):
                    dve.wait_ge(g_o, n + 1)
                    dve.tensor_tensor(xs[:, n], bank[n % 2][:, :], xs[:, n], ALU.add).then_inc(g_x, 1)
        norm_nodes("n1", xs)

        transpose_nodes("t2", xs, xT, plain_cols)
        ph = Region(R3 + 8 * WPAD + NT * D, WORDS)
        raw = ph.take(FC * D).rearrange("p (c n) -> p c n", c=FC)
        wT = [ph.take(FC * D).rearrange("p (c n) -> p c n", c=FC) for _ in range(2)]
        s_ld = sem("s_ld"); s_tr = sem("s_tr"); s_te = sem("s_te"); s_nm = sem("s_nm"); s_ne = sem("s_ne")
        s_o = sem("s_o"); s_x = sem("s_x"); s_y = sem("s_y")
        with nc.Block() as block:
            @block.sync
            def _(sp):
                sp.dma_start(brow, A["L2_gnn_b_self"].rearrange("(a n) -> a n", a=1)).then_inc(s_ld, 16)
                sp.dma_start(brow2, A["L2_gnn_b_neigh"].rearrange("(a n) -> a n", a=1)).then_inc(s_ld, 16)
                sp.dma_start(raw, A["L2_gnn_W_neigh"].rearrange("(c p) n -> p c n", c=FC)).then_inc(s_ld, 16)
                sp.wait_ge(s_tr, FC)
                sp.dma_start(raw, A["L2_gnn_W_self"].rearrange("(c p) n -> p c n", c=FC)).then_inc(s_ld, 16)

            @block.tensor
            def _(pe):
                for w in range(2):
                    pe.wait_ge(s_ld, 48 + 16 * w)
                    for ic in range(FC):
                        k = w * FC + ic
                        if k >= 2:
                            pe.wait_ge(s_te, k - 1)
                        for oc in range(FC):
                            last = pe.transpose(bank[k % 2][:, oc * 128:(oc + 1) * 128],
                                                raw[:, oc, ic * 128:(ic + 1) * 128], ident)
                        last.then_inc(s_tr, 1)
                for g in range(FC * 3):
                    c, (lo, hi) = g // 3, SPANS[g % 3]
                    if g >= 4:
                        pe.wait_ge(s_ne, g - 3)
                    for s in range(NT):
                        last = pe.matmul(bank[4 + g % 4][:, 0:hi - lo], xs[:, s, c * 128:(c + 1) * 128], AT[:, s, lo:hi],
                                         start=(s == 0), stop=(s == NT - 1))
                    last.then_inc(s_nm, 1)
                pe.wait_ge(s_te, 2 * FC)
                pe.wait_ge(s_ne, FC * 3)
                for n in range(NT):
                    if n >= 2:
                        pe.wait_ge(s_y, n - 1)
                    a, b = bank[n % 2][:, :], bank[2 + n % 2][:, :]
                    for c in range(FC):
                        pe.matmul(a, xnT[:, c, n * NP:(n + 1) * NP], wT[0][:, c], start=(c == 0), stop=(c == FC - 1))
                    for c in range(FC):
                        pe.matmul(b, xT[:, c, n * NP:(n + 1) * NP], wT[1][:, c], start=(c == 0), stop=False)
                    pe.matmul(b, onesM[0:1, :], brow, start=False, stop=False)
                    pe.matmul(b, onesM[0:1, :], brow2, start=False, stop=True).then_inc(s_o, 1)

            @block.scalar
            def _(act):
                for k in range(2 * FC):
                    act.wait_ge(s_tr, k + 1)
                    act.activation(wT[k // FC][:, k % FC], bank[k % 2][:, :], ACT.Copy).then_inc(s_te, 1)

            @block.vector
            def _(dve):
                for g in range(FC * 3):
                    c, (lo, hi) = g // 3, SPANS[g % 3]
                    dve.wait_ge(s_nm, g + 1)
                    dve.tensor_copy(xnT[:, c, lo:hi], bank[4 + g % 4][:, 0:hi - lo]).then_inc(s_ne, 1)
                for n in range(NT):
                    dve.wait_ge(s_o, n + 1)
                    dve.scalar_tensor_tensor(xs[:, n], bank[n % 2][:, :], invdeg[:, n:n + 1], xs[:, n],
                                             ALU.mult, ALU.add).then_inc(s_x, 1)
                    dve.wait_ge(s_x, n + 1)
                    dve.tensor_tensor(xs[:, n], xs[:, n], bank[2 + n % 2][:, :], ALU.add).then_inc(s_y, 1)
        norm_nodes("n2", xs)

        x3 = at(R3, NT * D).rearrange("p (n f) -> p n f", n=NT)
        R4 = R3 + NT * D
        BT = [at(R1, NT * NALL).rearrange("p (c n) -> p c n", c=NT),
              at(R4, NT * NALL).rearrange("p (c n) -> p c n", c=NT)]
        R5 = R4 + NT * NALL
        m_x3 = sem("m_x3")
        with nc.Block() as block:
            @block.vector
            def _(dve):
                for n in range(NT):
                    dve.tensor_copy(x3[:, n], xs[:, n]).then_inc(m_x3, 1)
        ph = Region(R5, WORDS)
        cf = [ph.take(2 * NP).rearrange("p (n r) -> p n r", r=2) for _ in range(4)]
        c_cv = sem("c_cv"); c_tr = sem("c_tr"); c_ev = sem("c_ev")
        with nc.Block() as block:
            @block.scalar
            def _(act):
                for k in range(NT * NT):
                    s, d = k % NT, k // NT
                    if k >= 4:
                        act.wait_ge(c_tr, k - 3)
                    act.activation(cf[k % 4], CNT[:, s, 2 * d * NP:2 * (d + 1) * NP].rearrange("p (n r) -> p n r", r=2),
                                   ACT.Copy).then_inc(c_cv, 1)

            @block.tensor
            def _(pe):
                for k in range(NT * NT):
                    pe.wait_ge(c_cv, k + 1)
                    if k >= 8:
                        pe.wait_ge(c_ev, k - 7)
                    for r in range(REL):
                        last = pe.transpose(bank[k % 8][:, r * NP:(r + 1) * NP], cf[k % 4][:, :, r], ident)
                    last.then_inc(c_tr, 1)

            @block.vector
            def _(dve):
                for k in range(NT * NT):
                    s, d = k % NT, k // NT
                    dve.wait_ge(c_tr, k + 1)
                    dve.tensor_copy(BT[0][:, d, s * NP:(s + 1) * NP], bank[k % 8][:, 0:NP])
                    dve.tensor_copy(BT[1][:, d, s * NP:(s + 1) * NP], bank[k % 8][:, NP:2 * NP]).then_inc(c_ev, 1)

        Z = [at(R2 + r * NT * D, NT * D).rearrange("p (n f) -> p n f", n=NT) for r in range(REL)]
        ph = Region(R5, WORDS)
        wr = ph.take(FC * D).rearrange("p (c n) -> p c n", c=FC)
        gw = ph.take(FC * REL).rearrange("p (c r) -> p c r", c=FC)
        gate = ph.take(NT * REL).rearrange("p (n r) -> p n r", n=NT)
        r_lo = Region(R2 + REL * NT * D, R3)
        wr2_ = r_lo.take(FC * D).rearrange("p (c n) -> p c n", c=FC)
        xT3 = ph.take(FC * NALL).rearrange("p (c n) -> p c n", c=FC)
        wbuf = [wr, wr2_]
        x3D = nc.dram_tensor("x3_scratch", (128, NT * D), F32, kind="Internal").ap()
        x_sv = sem("x_sv")
        x3flat = at(R3, NT * D)
        with nc.Block() as block:
            @block.sync
            def _(sp):
                sp.dma_start(x3D, x3flat).then_inc(x_sv, 16)
                sp.wait_ge(x_sv, 16)
        for layer in range(2):
            tag = f"r{layer}"
            transpose_nodes("t3" + tag, x3, xT3, plain_cols)
            q_ld = [sem(tag + "_ld0"), sem(tag + "_ld1")]
            q_c = sem(tag + "_c"); q_g = sem(tag + "_g"); q_gs = sem(tag + "_gs")
            q_z = sem(tag + "_z"); q_ze = sem(tag + "_ze"); q_o = sem(tag + "_o"); q_e = sem(tag + "_e")
            with nc.Block() as block:
                @block.sync
                def _(sp):
                    sp.dma_start(gw, A[f"gate_w{layer + 1}"]).then_inc(q_c, 16)
                    sp.dma_start(brow, A[f"L3_gnn_bias{layer + 1}"].rearrange("(a n) -> a n", a=1)).then_inc(q_c, 16)
                    for r in range(REL):
                        sp.dma_start(wbuf[r], wD[layer, 4 * r:4 * r + 4].rearrange("q i o -> i q o")).then_inc(q_ld[r], 16)
                    if layer == 1:
                        sp.dma_start(x3flat, x3D).then_inc(x_sv, 16)
                    sp.wait_ge(q_z, NT)
                    sp.dma_start(wbuf[0], A[f"L3_gnn_root{layer + 1}"].rearrange("(c p) n -> p c n", c=FC)).then_inc(q_ld[0], 16)

                @block.tensor
                def _(pe):
                    pe.wait_ge(q_c, 32)
                    for n in range(NT):
                        for c in range(FC):
                            last = pe.matmul(bank[6][:, 2 * n:2 * n + 2], xT3[:, c, n * NP:(n + 1) * NP], gw[:, c],
                                             start=(c == 0), stop=(c == FC - 1))
                    last.then_inc(q_g, 1)
                    for k in range(REL * NT):
                        r, n = k // NT, k % NT
                        if n == 0:
                            pe.wait_ge(q_ld[r], 16)
                        if k >= 2:
                            pe.wait_ge(q_ze, k - 1)
                        for c in range(FC):
                            last = pe.matmul(bank[k % 2][:, :], xT3[:, c, n * NP:(n + 1) * NP], wbuf[r][:, c],
                                             start=(c == 0), stop=(c == FC - 1))
                        last.then_inc(q_z, 1)
                    pe.wait_ge(q_ld[0], 32)
                    pe.wait_ge(q_ze, REL * NT)
                    for n in range(NT):
                        ns = slice(n * NP, (n + 1) * NP)
                        o = bank[2 + n % 4][:, :]
                        if n >= 4:
                            pe.wait_ge(q_e, n - 3)
                        pe.matmul(o, onesM[0:1, :], brow, start=True, stop=False)
                        for c in range(FC):
                            pe.matmul(o, xT3[:, c, ns], wbuf[0][:, c], start=False, stop=False)
                        for k in range(REL * NT):
                            r, d = k // NT, k % NT
                            last = pe.matmul(o, BT[r][:, d, ns], Z[r][:, d], start=False, stop=(k == REL * NT - 1))
                        last.then_inc(q_o, 1)

                @block.scalar
                def _(act):
                    act.wait_ge(q_g, 1)
                    act.activation(gate.rearrange("p n r -> p (n r)"), bank[6][:, 0:REL * NT], ACT.Sigmoid).then_inc(q_gs, 1)

                @block.vector
                def _(dve):
                    dve.wait_ge(q_gs, 1)
                    for k in range(REL * NT):
                        r, n = k // NT, k % NT
                        dve.wait_ge(q_z, k + 1)
                        dve.tensor_scalar(Z[r][:, n], bank[k % 2][:, :], gate[:, n, r:r + 1], None, ALU.mult).then_inc(q_ze, 1)
                    for n in range(NT):
                        dve.wait_ge(q_o, n + 1)
                        o = bank[2 + n % 4][:, :]
                        if layer == 0:
                            dve.tensor_scalar(x3[:, n], o, 0.0, None, ALU.max).then_inc(q_e, 1)
                        else:
                            dve.wait_ge(x_sv, 32)
                            dve.tensor_tensor(x3[:, n], o, x3[:, n], ALU.add).then_inc(q_e, 1)
        norm_nodes("n3", x3)
        f_st = sem("f_st")
        with nc.Block() as block:
            @block.sync
            def _(sp):
                whole = (NT - 1) * NP
                sp.dma_start(out[0:whole].rearrange("(n p) f -> p n f", p=NP), x3[:, 0:NT - 1]).then_inc(f_st, 16)
                sp.dma_start(out[whole:NODES], x3[0:TAIL, NT - 1]).then_inc(f_st, 16)
                sp.wait_ge(f_st, 32)


_NAMES = ["x", "src", "dst", "edge_attr_4", "edge_attr_8", "edge_type_2", "edge_weight",
          "L0_gnn_W_up0", "L0_gnn_W_up1", "L0_gnn_W_mlp1", "L0_gnn_W_mlp2", "L0_gnn_W_mlp3", "L0_gnn_W_mlp4",
          "L0_gnn_W_out0", "L0_gnn_W_out1", "L1_gnn_W_gcn", "L1_gnn_b_gcn", "L1_gnn_W_fc", "L1_gnn_b_fc",
          "L2_gnn_W_self", "L2_gnn_b_self", "L2_gnn_W_neigh", "L2_gnn_b_neigh",
          "L3_gnn_basis1", "L3_gnn_root1", "L3_gnn_bias1", "L3_gnn_basis2", "L3_gnn_root2", "L3_gnn_bias2"]


def kernel(**inputs):
    import numpy as np
    import concourse.bacc as bacc
    from concourse.bass_utils import run_bass_kernel_spmd

    nc = bacc.Bacc("TRN2", target_bir_lowering=False, num_devices=1)
    host = {name: np.ascontiguousarray(inputs[name]) for name in _NAMES}
    for k in (1, 2):
        host[f"att{k}_rep"] = np.ascontiguousarray(np.repeat(np.asarray(inputs[f"L3_gnn_att{k}"]).T, 4, axis=0))
        gate = np.asarray(inputs[f"L3_gnn_gate_w{k}"]).reshape(REL, FC, 128)
        host[f"gate_w{k}"] = np.ascontiguousarray(gate.transpose(2, 1, 0))
    host["ident"] = np.eye(128, dtype=np.float32)
    host["mask4"] = np.tile(np.tile(np.eye(4, dtype=np.float32), (BASES, 1)), (1, REL))
    aps = {}
    arrays = {}
    for name, a in host.items():
        arrays["in_" + name] = a
        aps[name] = nc.dram_tensor("in_" + name, a.shape, mybir.dt.from_np(a.dtype), kind="ExternalInput").ap()
    out = nc.dram_tensor("out_0", (NODES, D), F32, kind="ExternalOutput").ap()
    gnn_program(nc, aps, out)
    r = run_bass_kernel_spmd(nc, [arrays], core_ids=[0])
    return r.results[0]["out_0"]
```

```python
import concourse.bass as bass
from concourse import mybir
from concourse.alu_op_type import AluOpType as ALU
from contextlib import ExitStack
import math

F32 = mybir.dt.float32
I32 = mybir.dt.int32
I16 = mybir.dt.int16
BF16 = mybir.dt.bfloat16
F32R = mybir.dt.float32r
ACT = mybir.ActivationFunctionType
AX = mybir.AxisListType

NODES, D, EDGES = 1250, 512, 20000
MUL = 128
P = 125
NP = 128
NT = -(-NODES // NP)
NALL = NT * NP
TAIL = NODES - (NT - 1) * NP
ET = EDGES // P
EH = ET // 2
W = 32
WPAD = NODES + W
SLOTS = 8
EIGHTS = ET // SLOTS
BODY = 2 * SLOTS
TURNS = ET // BODY
HID, RB = 64, 8
FC = D // 128
BASES, REL = 30, 2
SILU_2MOM = 1.679177
SPANS = [(0, 512), (512, 1024), (1024, 1280)]
IC = 8


def gnn_program(nc, A, out):
    ctx = ExitStack()
    with ctx:
        def sem(name):
            return ctx.enter_context(nc.semaphore(name))

        WORDS = 53200
        arena = ctx.enter_context(nc.sbuf_tensor("arena", [128, WORDS], F32))
        ARENA = nc.sbuf_base - 4 * WORDS
        bank = [ctx.enter_context(nc.psum_tensor(f"bank{k}", [128, 512], F32)) for k in range(8)]

        def at(off, words, rows=128, dt=F32):
            assert off + words <= WORDS, (off, words)
            v = arena[0:rows, off:off + words]
            return v if dt == F32 else v.bitcast(dt)

        class Region:
            def __init__(self, lo, hi):
                self.at, self.hi = lo, hi

            def take(self, words, rows=128, dt=F32):
                off = self.at
                self.at += words + (words & 1)
                assert self.at <= self.hi, (self.at, self.hi)
                return at(off, words, rows, dt)

        SMALL = 2200
        AWORDS = NT * WPAD
        R1, R2 = SMALL, SMALL + AWORDS
        R3 = SMALL + 2 * AWORDS
        small = Region(0, SMALL)
        ident = small.take(128)
        onesM = small.take(128)
        iota32 = small.take(W, P)
        tab = small.take(3 * ET, 1, I32).rearrange("p (q t) -> p q t", q=3)
        turns_more = small.take(TURNS, 1, I32)
        large = small.take(1, 1, I32)
        cmax = small.take(1)
        cmax1 = small.take(1, 1)
        invdeg = small.take(NT)
        zero = small.take(1)
        stats = small.take(NT * 6).rearrange("p (n s) -> p n s", n=NT)
        mv = small.take(NT * 2).rearrange("p (n s) -> p n s", n=NT)
        vare = small.take(NT)
        sd = small.take(NT)
        rs = small.take(NT)
        nt1 = small.take(NT)
        nt2 = small.take(NT)
        bgcn = small.take(1)
        brow = small.take(D, 1)
        brow2 = small.take(D, 1)
        attL = small.take(2 * 32, 4 * BASES).rearrange("p (l m) -> p l m", l=2)

        AT = at(R1, AWORDS).rearrange("p (c n) -> p c n", c=NT)
        CNT = at(R2, AWORDS, 128, I16).rearrange("p (c n) -> p c n", c=NT)
        accT = at(R3, 8 * WPAD).rearrange("p (b n) -> p b n", b=8)
        edge = Region(R3 + 8 * WPAD, WORDS)
        rel = edge.take(ET, P)
        srcT = edge.take(ET, P)
        idx = edge.take(ET, 128, I32)
        yT = edge.take(4 * ET, P).rearrange("p (t m) -> p t m", m=4)
        valT = edge.take(5 * ET // 2, P, BF16).rearrange("p (t m) -> p t m", m=5)
        edge_mark = edge.at

        hD = nc.dram_tensor("h_scratch", (EIGHTS, 128, 4 * P), F32, kind="Internal").ap()
        x3D = nc.dram_tensor("x3_scratch", (128, NT * D), F32, kind="Internal").ap()
        upD = nc.dram_tensor("up_scratch", (NODES, D), F32, kind="Internal").ap()
        wD = nc.dram_tensor("w_scratch", (2, REL * 4, 128, D), F32, kind="Internal").ap()

        def load_nodes(eng, xs, cleared, loaded):
            whole = (NT - 1) * NP
            eng.dma_start(xs[:, 0:NT - 1], A["x"][0:whole].rearrange("(n p) f -> p n f", p=NP)).then_inc(loaded, 16)
            eng.wait_ge(cleared, 1)
            eng.dma_start(xs[0:TAIL, NT - 1], A["x"][whole:NODES]).then_inc(loaded, 16)

        def plain_cols(x, c):
            return x[:, c * 128:(c + 1) * 128]

        x_sv = sem("x_sv")
        f_rows = sem("f_rows")
        f_stats = sem("f_stats"); f_mean = sem("f_mean"); f_var = sem("f_var"); f_root = sem("f_root")
        f_newton = sem("f_newton"); f_normed = sem("f_normed")
        f_turned = sem("f_turned")
        f_columns = sem("f_columns")

        def norm_vector(dve, layer, xs, rows):
            t, p = NT * layer, NT // 2 * layer
            for g in range(NT // 2 + 1):
                if g < NT // 2:
                    pair = (2 * g, 2 * g + 1)
                    for n in pair:
                        rows(n)
                    for n in pair:
                        dve.wait_ge(f_rows, t + n + 1)
                        dve.bn_stats(stats[:, n], xs[:, n]).then_inc(f_stats, 1)
                    for n in pair:
                        dve.wait_ge(f_stats, t + n + 1)
                        dve.bn_aggr(mv[:, n], stats[:, n]).then_inc(f_mean, 1)
                    dve.wait_ge(f_mean, t + 2 * g + 2)
                    dve.tensor_scalar(vare[:, 2 * g:2 * g + 2], mv[:, 2 * g:2 * g + 2, 1], 1e-5, None,
                                      ALU.add).then_inc(f_var, 1)
                if g:
                    pair = (2 * g - 2, 2 * g - 1)
                    q = slice(2 * g - 2, 2 * g)
                    dve.wait_ge(f_root, p + g)
                    dve.reciprocal(rs[:, q], sd[:, q]).then_inc(f_newton, 1)
                    dve.wait_ge(f_newton, 5 * (p + g) - 4)
                    dve.tensor_tensor(nt1[:, q], rs[:, q], rs[:, q], ALU.mult).then_inc(f_newton, 1)
                    dve.wait_ge(f_newton, 5 * (p + g) - 3)
                    dve.tensor_tensor(nt2[:, q], nt1[:, q], vare[:, q], ALU.mult).then_inc(f_newton, 1)
                    dve.wait_ge(f_newton, 5 * (p + g) - 2)
                    dve.tensor_scalar(nt1[:, q], nt2[:, q], -0.5, 1.5, ALU.mult, ALU.add).then_inc(f_newton, 1)
                    dve.wait_ge(f_newton, 5 * (p + g) - 1)
                    dve.tensor_tensor(nt2[:, q], rs[:, q], nt1[:, q], ALU.mult).then_inc(f_newton, 1)
                    dve.wait_ge(f_newton, 5 * (p + g))
                    for n in pair:
                        dve.tensor_scalar(xs[:, n], xs[:, n], mv[:, n, 0:1], nt2[:, n:n + 1],
                                          ALU.subtract, ALU.mult).then_inc(f_normed, 1)

        def norm_scalar(act, layer, xT=None, first=None):
            t, p = NT * layer, NT // 2 * layer
            for g in range(NT // 2 + 2):
                if g < NT // 2:
                    act.wait_ge(f_var, p + g + 1)
                    act.activation(sd[:, 2 * g:2 * g + 2], vare[:, 2 * g:2 * g + 2], ACT.Sqrt).then_inc(f_root, 1)
                if xT is not None and g >= 2:
                    for n in (2 * g - 4, 2 * g - 3):
                        act.wait_ge(f_turned, t + n + 1)
                        act.activation(xT[:, :, n * NP:(n + 1) * NP],
                                       bank[first + n % 2][:, :].rearrange("p (c x) -> p c x", c=FC),
                                       ACT.Copy).then_inc(f_columns, 1)

        def norm_tensor(pe, layer, xs, first, tile):
            t, p = NT * layer, NT // 2 * layer
            for g in range(NT // 2 + 2):
                if g < NT // 2:
                    tile(2 * g)
                    tile(2 * g + 1)
                if g >= 2:
                    for n in (2 * g - 4, 2 * g - 3):
                        pe.wait_ge(f_normed, t + n + 1)
                        if n >= 2:
                            pe.wait_ge(f_columns, t + n - 1)
                        for c in range(FC):
                            last = pe.transpose(bank[first + n % 2][:, c * NP:(c + 1) * NP], plain_cols(xs[:, n], c), ident)
                        last.then_inc(f_turned, 1)

        ph = Region(R1, R2)
        Lf = ph.take(2 * P * RB, EH).rearrange("p (b x) -> p b x", b=2)
        La = ph.take(2 * P * 4, EH).rearrange("p (b x) -> p b x", b=2)
        Li = ph.take(3 * 2 * P, EH, I32).rearrange("p (q b x) -> p q b x", q=3, b=2)
        Lq = ph.take(4 * 2 * P, EH).rearrange("p (q b x) -> p q b x", q=4, b=2)
        mnx = ph.take(2 * 2, EH).rearrange("p (q b) -> p q b", q=2)
        more = ph.take(2, EH)
        morei = ph.take(2, EH, I32)
        diag = ph.take(4 * EH, EH).rearrange("p (q b x) -> p q b x", q=2, b=2)
        misc = ph.take(4 * ET, P).rearrange("p (q t) -> p q t", q=4)
        base = ph.take(ET, P)
        cum = ph.take(ET, 1)
        kf = ph.take(ET, 1)
        kt = ph.take(TURNS, 1)
        onesr = ph.take(ET, 1)
        wr1 = ph.take(ET, P)
        wr2 = ph.take(ET, P)
        CLEARED = -(-(ph.at - R1) // WPAD)
        ph = Region(R1 + CLEARED * WPAD, R2)
        stage = [ph.take(IC // 4 * D).rearrange("p (k o) -> p k o", o=D) for _ in range(2)]
        ph = Region(R2, R3)
        xs0 = ph.take(NT * D).rearrange("p (n f) -> p n f", n=NT)
        xT0 = ph.take(FC * NALL).rearrange("p (c n) -> p c n", c=FC)
        wup = ph.take(2 * 128).rearrange("p (q n) -> p q n", q=2)
        upS = [ph.take(D) for _ in range(2)]
        mask = ph.take(8, 4 * BASES)
        attp = ph.take(4, 4 * BASES)
        ph = Region(R3, R3 + 8 * WPAD)
        FT = ph.take(ET * RB, P).rearrange("p (c s h j) -> p c s h j", s=4, h=2, j=RB)
        W1b = ph.take(128)
        W2b = ph.take(128)
        W3b = ph.take(128)
        fT = ph.take(4 * 4 * P).rearrange("p (q x) -> p q x", q=4)
        hA = ph.take(4 * 4 * P).rearrange("p (q x) -> p q x", q=4)
        hB = ph.take(4 * 4 * P).rearrange("p (q x) -> p q x", q=4)
        hC = ph.take(4 * 4 * P).rearrange("p (q x) -> p q x", q=4)
        ph = Region(edge_mark, WORDS)
        bas = [ph.take(IC * D, 4 * BASES) for _ in range(3)]

        e_ld = sem("e_ld"); e_cst = sem("e_cst"); e_dve = sem("e_dve"); e_tr = sem("e_tr")
        e_bc = sem("e_bc"); e_q = sem("e_q"); e_done = sem("e_done"); e_bcr = sem("e_bcr"); e_z = sem("e_z")
        m_ld = sem("m_ld"); m_z = sem("m_z"); m_t = sem("m_t"); m_f = sem("m_f"); m_mm = sem("m_mm"); m_h = sem("m_h")
        m_st = [sem(f"m_st{q}") for q in range(4)]
        b_ld = [sem(f"b_ld{k}") for k in range(3)]
        b_c = sem("b_c"); b_z = sem("b_z"); b_at = sem("b_at"); b_mm = sem("b_mm"); b_ev = sem("b_ev")
        b_st = [sem("b_st0"), sem("b_st1")]
        u_z = sem("u_z"); u_ld = sem("u_ld"); u_tr = sem("u_tr"); u_te = sem("u_te"); u_mm = sem("u_mm"); u_ev = sem("u_ev")
        u_st = [sem("u_st0"), sem("u_st1")]
        quantities = [(Lf, j, RB) for j in range(RB)] + [(La, m, 4) for m in range(4)] + [(Lq, q, 1) for q in range(4)]
        GROUPS = EIGHTS // 4
        layer_in = [fT, hA, hB]
        layer_out = [hA, hB, hC]
        layer_w = [W1b, W2b, W3b]
        scales = [1.0 / math.sqrt(RB), SILU_2MOM / math.sqrt(HID), SILU_2MOM / math.sqrt(HID)]
        NB = 128 // IC
        KB = IC // 4
        STEPS = NB * KB
        IN_MLP = 4 * GROUPS
        PER_NODE = (STEPS - IN_MLP) // (NT + 1)

        def irrep_cols(x, c):
            return x[:, 0:MUL] if c == 0 else x[:, MUL:].rearrange("p (u m) -> p m u", m=3)[:, c - 1]

        with nc.Block() as block:
            @block.sync
            def _(sp):
                sp.dma_start(ident, A["ident"]).then_inc(e_ld, 16)
                for q, name in enumerate(("src", "dst", "edge_type_2")):
                    sp.dma_start(Li[:, q], A[name].rearrange("(b p x) -> p b x", b=2, p=EH)).then_inc(e_ld, 16)
                sp.dma_start(Lq[:, 3], A["edge_weight"].rearrange("(b p x) -> p b x", b=2, p=EH)).then_inc(e_ld, 16)
                sp.dma_start(Lf, A["edge_attr_8"].rearrange("(b p x) j -> p b (x j)", b=2, p=EH)).then_inc(e_ld, 16)
                sp.dma_start(La, A["edge_attr_4"].rearrange("(b p x) j -> p b (x j)", b=2, p=EH)).then_inc(e_ld, 16)
                sp.dma_start(mask, A["mask4"]).then_inc(b_c, 16)
                sp.dma_start(attp[:, 0:2], A["att1_rep"]).then_inc(b_c, 16)
                sp.dma_start(attp[:, 2:4], A["att2_rep"]).then_inc(b_c, 16)

                def store(u):
                    sp.wait_ge(b_ev, (u + 1) * KB)
                    for s in range(4):
                        sp.dma_start(wD[0].rearrange("m (k s) o -> s m k o", s=4)[s, :, u * KB:(u + 1) * KB],
                                     stage[u % 2][32 * s:32 * s + 8]).then_inc(b_st[u % 2], 16)
                for u in range(NB):
                    if u >= 3:
                        sp.wait_ge(b_mm, (u - 2) * KB)
                    v = A["L3_gnn_basis1"].rearrange("b (q i) o -> (b q) (i o)", q=4)
                    sp.dma_start(bas[u % 3], v[:, u * IC * D:(u + 1) * IC * D]).then_inc(b_ld[u % 3], 16)
                    if u >= 3:
                        store(u - 3)
                for u in range(NB - 3, NB):
                    store(u)
                for k in range(2):
                    sp.wait_ge(b_st[k], 32 * NB)

            @block.gpsimd
            def _(pool):
                pool.memset(onesM, 1.0).then_inc(e_cst, 1)
                pool.memset(onesr, 1.0).then_inc(e_cst, 1)
                pool.memset(zero, 0.0).then_inc(e_cst, 1)
                pool.memset(idx, 0).then_inc(e_cst, 1)
                pool.iota(iota32, pattern=[[1, W]], base=0, channel_multiplier=0,
                          allow_small_or_imprecise_dtypes=True).then_inc(e_cst, 1)
                for w in layer_w:
                    pool.memset(w, 0.0).then_inc(m_z, 1)
                pool.memset(attL, 0.0).then_inc(b_z, 1)
                pool.memset(xs0[:, NT - 1], 0.0).then_inc(u_z, 1)
                pool.wait_ge(m_z, 3)
                for half in range(2):
                    k, c = slice(half * RB, (half + 1) * RB), slice(half * HID, (half + 1) * HID)
                    pool.dma_start(W1b[k, c], A["L0_gnn_W_mlp1"]).then_inc(m_ld, 16)
                    pool.dma_start(W2b[c, c], A["L0_gnn_W_mlp2"]).then_inc(m_ld, 16)
                    pool.dma_start(W3b[c, c], A["L0_gnn_W_mlp3"]).then_inc(m_ld, 16)
                load_nodes(pool, xs0, u_z, u_ld)
                pool.dma_start(wup[:, 0], A["L0_gnn_W_up0"]).then_inc(u_ld, 16)
                pool.dma_start(wup[:, 1], A["L0_gnn_W_up1"]).then_inc(u_ld, 16)
                pool.wait_ge(e_done, 1)
                pool.memset(AT[:, 0:CLEARED], 0.0).then_inc(e_z, 1)

            @block.vector
            def _(dve):
                n = [0]

                def link(ins):
                    n[0] += 1
                    ins.then_inc(e_dve, 1)
                    dve.wait_ge(e_dve, n[0])
                dve.wait_ge(e_ld, 7 * 16)
                dve.wait_ge(e_cst, 5)
                link(dve.tensor_copy(Lq[:, 0:3], Li))
                link(dve.tensor_reduce(mnx[:, 0], Lq[:, 1], AX.X, ALU.min))
                link(dve.tensor_reduce(mnx[:, 1], Lq[:, 1], AX.X, ALU.max))
                link(dve.tensor_tensor(more, mnx[:, 1], mnx[:, 0], ALU.subtract))
                link(dve.tensor_copy(morei, more))
                link(dve.tensor_scalar(morei, morei, 5, None, ALU.arith_shift_right))
                link(dve.tensor_copy(more, morei))
                for b in range(2):
                    link(dve.tensor_scalar(diag[:, 0, b], ident[0:EH, 0:EH], mnx[:, 0, b:b + 1], None, ALU.mult))
                    link(dve.tensor_scalar(diag[:, 1, b], ident[0:EH, 0:EH], more[:, b:b + 1], None, ALU.mult))
                dve.sem_inc(e_q, 1)
                for k in range(6):
                    dve.wait_ge(e_tr, k + 1)
                    b, g = k // 3, k % 3
                    ts = slice(b * EH, (b + 1) * EH)
                    for s, (_, j, step) in enumerate(quantities[6 * g:6 * g + 6]):
                        src = bank[k][0:P, s * EH:(s + 1) * EH]
                        if step == RB:
                            dst = FT[:, b * EIGHTS // 2:(b + 1) * EIGHTS // 2, :, :, j].rearrange("p c s h -> p c h s")
                            src = src.rearrange("p (c h s) -> p c h s", h=2, s=4)
                        elif step == 4:
                            dst = yT[:, ts, j]
                        else:
                            dst = misc[:, j, ts]
                        dve.tensor_copy(dst, src).then_inc(e_dve, 1)
                        n[0] += 1
                dve.wait_ge(e_dve, n[0])
                dve.wait_ge(e_bc, 1)
                dve.tensor_copy(kf, bank[6][0:1, ET:2 * ET]).then_inc(e_bcr, 1)
                dve.tensor_copy(base, bank[6][0:P, 0:ET]).then_inc(e_bcr, 1)
                dve.wait_ge(e_bcr, 2)
                dve.wait_ge(b_z, 1)
                dve.wait_ge(b_c, 48)
                for layer in range(2):
                    for r in range(REL):
                        dve.tensor_scalar(attL[:, layer, 4 * r:4 * r + 4], mask[:, 4 * r:4 * r + 4],
                                          attp[:, 2 * layer + r:2 * layer + r + 1], None, ALU.mult).then_inc(b_at, 1)

                link(dve.tensor_tensor(rel, misc[:, 1], base, ALU.subtract))
                link(dve.tensor_copy(srcT, misc[:, 0]))
                link(dve.tensor_copy(idx[0:P], misc[:, 0]))
                link(dve.tensor_copy(tab[:, 0], base[0:1]))
                link(dve.tensor_copy(tab[:, 1], kf))
                link(dve.tensor_reduce(kt, kf.rearrange("p (i j) -> p i j", j=BODY), AX.X, ALU.add))
                link(dve.tensor_copy(turns_more, kt))
                link(dve.tensor_tensor_scan(cum, onesr, kf, 0.0, ALU.mult, ALU.add))
                link(dve.tensor_tensor(cum, cum, kf, ALU.subtract))
                link(dve.tensor_copy(tab[:, 2], cum))
                link(dve.tensor_copy(valT[:, :, 2], misc[:, 3]))
                link(dve.tensor_tensor(wr1, misc[:, 3], valT[:, :, 2], ALU.subtract))
                link(dve.tensor_copy(valT[:, :, 0], wr1))
                link(dve.tensor_tensor(wr2, wr1, valT[:, :, 0], ALU.subtract))
                link(dve.tensor_copy(valT[:, :, 1], wr2))
                link(dve.tensor_scalar(valT[:, :, 3], misc[:, 2], 0.0, None, ALU.is_equal))
                link(dve.tensor_scalar(valT[:, :, 4], misc[:, 2], 0.0, None, ALU.not_equal))
                dve.sem_inc(e_done, 1)

                def bases(lo, hi):
                    for g in range(lo, hi):
                        u, k = g // KB, g % KB
                        if u >= 2 and k == 0:
                            dve.wait_ge(b_st[u % 2], 64 * (u // 2))
                        dve.wait_ge(b_mm, g + 1)
                        dve.tensor_copy(stage[u % 2][:, k], bank[6 + g % 2][:, :]).then_inc(b_ev, 1)

                for g in range(GROUPS):
                    for q in range(4):
                        c = g * 4 + q
                        dve.wait_ge(m_t, c + 1)
                        if g:
                            dve.wait_ge(m_mm, (g - 1) * 12 + q + 1)
                        dve.tensor_copy(fT[0:2 * RB, q], bank[q % 2][0:2 * RB, 0:4 * P]).then_inc(m_f, 1)
                    bases(4 * g, 4 * g + 4)
                for n in range(NT):
                    dve.wait_ge(u_tr, n + 1)
                    dve.tensor_copy(xT0[:, :, n * NP:(n + 1) * NP],
                                    bank[n % 2][:, 0:FC * NP].rearrange("p (c x) -> p c x", c=FC)).then_inc(u_te, 1)
                    bases(IN_MLP + n * PER_NODE, IN_MLP + (n + 1) * PER_NODE)
                bases(IN_MLP + NT * PER_NODE, STEPS)

            @block.tensor
            def _(pe):
                pe.wait_ge(e_q, 1)
                pe.wait_ge(e_dve, 11)
                for k in range(6):
                    b, g = k // 3, k % 3
                    for s, (Lx, j, step) in enumerate(quantities[6 * g:6 * g + 6]):
                        if step == 1:
                            in_ = Lx[:, j, b, :]
                        else:
                            in_ = Lx[:, b, :].rearrange("p (x j) -> p j x", j=step)[:, j, :]
                        last = pe.transpose(bank[k][0:P, s * EH:(s + 1) * EH], in_, ident[0:EH, 0:EH])
                    last.then_inc(e_tr, 1)
                for q in range(2):
                    for b in range(2):
                        last = pe.matmul(bank[6][0:P, q * ET + b * EH:q * ET + (b + 1) * EH],
                                         onesM[0:EH, 0:P], diag[:, q, b], start=True, stop=True)
                last.then_inc(e_bc, 1)
                pe.wait_ge(e_bcr, 2)

                def bases(lo, hi):
                    for g in range(lo, hi):
                        u, k = g // KB, g % KB
                        if k == 0:
                            pe.wait_ge(b_ld[u % 3], 16 * (u // 3 + 1))
                        if g >= 2:
                            pe.wait_ge(b_ev, g - 1)
                        for s in range(4):
                            last = pe.matmul(bank[6 + g % 2][32 * s:32 * s + 32, :], attL[:, 0],
                                             bas[u % 3][:, (4 * k + s) * D:(4 * k + s + 1) * D], start=True, stop=True)
                        last.then_inc(b_mm, 1)

                def mlp_layer(g, layer, q):
                    if layer == 0:
                        pe.wait_ge(m_f, g * 4 + q + 1)
                        if g:
                            pe.wait_ge(m_h, (g - 1) * 12 + 8 + q + 1)
                        k = 2 * RB
                    else:
                        pe.wait_ge(m_h, g * 12 + (layer - 1) * 4 + q + 1)
                        k = 128
                    pe.matmul(bank[2 + q][:, 0:4 * P], layer_w[layer][0:k], layer_in[layer][0:k, q],
                              start=True, stop=True).then_inc(m_mm, 1)

                pe.wait_ge(m_ld, 6 * 16)
                for g in range(GROUPS):
                    for q in range(4):
                        c = g * 4 + q
                        if c >= 2:
                            pe.wait_ge(m_f, c - 1)
                        for s in range(4):
                            last = pe.transpose(bank[q % 2][0:2 * RB, s * P:(s + 1) * P],
                                                FT[:, c, s].rearrange("p h j -> p (h j)"), ident[0:P, 0:P])
                        last.then_inc(m_t, 1)
                    if g == 0:
                        pe.wait_ge(b_at, 4)
                    bases(4 * g, 4 * g + 1)
                    for layer in range(3):
                        for q in range(4):
                            mlp_layer(g, layer, q)
                        bases(4 * g + 1 + layer, 4 * g + 2 + layer)
                pe.wait_ge(m_f, EIGHTS)
                pe.wait_ge(m_h, 12 * GROUPS)
                pe.wait_ge(u_ld, 64)

                def table(n):
                    if n >= 2:
                        pe.wait_ge(u_ev, n - 1)
                    pe.wait_ge(u_te, n + 1)
                    for c in range(FC):
                        last = pe.matmul(bank[2 + n % 2][:, c * 128:(c + 1) * 128], xT0[:, c, n * NP:(n + 1) * NP],
                                         wup[:, min(c, 1)], start=True, stop=True)
                    last.then_inc(u_mm, 1)
                for n in range(NT):
                    if n >= 2:
                        pe.wait_ge(u_te, n - 1)
                    for c in range(FC):
                        last = pe.transpose(bank[n % 2][:, c * NP:(c + 1) * NP], irrep_cols(xs0[:, n], c), ident)
                    last.then_inc(u_tr, 1)
                    if n:
                        table(n - 1)
                    bases(IN_MLP + n * PER_NODE, IN_MLP + (n + 1) * PER_NODE)
                table(NT - 1)
                bases(IN_MLP + NT * PER_NODE, STEPS)

            @block.scalar
            def _(act):
                for g in range(GROUPS):
                    for layer in range(3):
                        for q in range(4):
                            act.wait_ge(m_mm, g * 12 + layer * 4 + q + 1)
                            if layer == 2 and g:
                                act.wait_ge(m_st[q], 16 * g)
                            act.activation(layer_out[layer][:, q], bank[2 + q][:, 0:4 * P], ACT.Silu,
                                           scale=scales[layer]).then_inc(m_h, 1)
                    for q in range(4):
                        act.wait_ge(m_h, g * 12 + 8 + q + 1)
                        act.dma_start(hD[g * 4 + q], hC[:, q]).then_inc(m_st[q], 16)
                for n in range(NT):
                    act.wait_ge(u_mm, n + 1)
                    if n >= 2:
                        act.wait_ge(u_st[n % 2], 16 * (n // 2))
                    act.activation(upS[n % 2], bank[2 + n % 2][:, :], ACT.Copy, scale=1.0 / math.sqrt(MUL)).then_inc(u_ev, 1)
                    act.wait_ge(u_ev, n + 1)
                    rows = min(NP, NODES - n * NP)
                    act.dma_start(upD[n * NP:n * NP + rows, :], upS[n % 2][0:rows]).then_inc(u_st[n % 2], 16)
                for q in range(4):
                    act.wait_ge(m_st[q], 16 * GROUPS)
                for k in range(2):
                    act.wait_ge(u_st[k], 16 * (NT // 2))

        edge.at = edge_mark
        G = [edge.take(D) for _ in range(SLOTS)]
        hS = edge.take(4 * P).rearrange("p (s e) -> p s e", s=4)
        W4 = edge.take(4 * MUL)
        M = [edge.take(8 * MUL, P).rearrange("p (b u) -> p b u", b=8) for _ in range(2)]
        Ss = [edge.take(NALL // 2, P, BF16) for _ in range(2)]
        iotaN = edge.take(NALL // 2, P, I16)
        eq = [edge.take(W, P) for _ in range(2)]
        Sy = [edge.take(4 * W, P).rearrange("p (m w) -> p m w", m=4) for _ in range(2)]
        Sw = [edge.take(5 * W // 2, P, BF16) for _ in range(2)]
        ring = edge.take(SLOTS, 128, I32)
        relx = edge.take(2, P)
        wsteps = edge.take(NODES // W + 1, P)

        cnt_words = at(R2, AWORDS)
        CSPLIT = AWORDS * 3 // 4
        z = sem("z"); w4_ld = sem("w4_ld")
        h_ld = [sem(f"h_ld{j}") for j in range(SLOTS)]
        gathered = [sem(f"gathered{j}") for j in range(SLOTS)]
        tpw_ready = sem("tpw_ready")
        prod_done = sem("prod_done")
        send_ready = sem("send_ready")
        recv_ready = sem("recv_ready")
        visit_done = sem("visit_done")
        acc_done = sem("acc_done")
        eq_done = sem("eq_done"); passed = sem("passed"); ring_done = sem("ring_done")
        x_eq = sem("x_eq"); x_rel = sem("x_rel")
        x_ready = sem("x_ready"); x_done = sem("x_done")
        x_acc = sem("x_acc")
        TP, MSG, BLD = (6, 7), (0, 1), (2, 4)

        def either(eng, i, turn):
            col = slice(i, i + 1) if isinstance(i, int) else bass.ds(i, 1)
            some = eng.value_load(turns_more[:, col], min_val=0, max_val=BODY * (NODES // W))
            with eng.If(some > 0):
                turn(True)
            with eng.Else():
                turn(False)

        def tile_numbers(eng, t):
            col = slice(t, t + 1) if isinstance(t, int) else bass.ds(t, 1)
            further = eng.value_load(tab[:, 1, col], min_val=0, max_val=NODES // W)
            seen = eng.value_load(tab[:, 2, col], min_val=0, max_val=ET * (NODES // W))
            return further, seen

        with nc.Block() as block:
            @block.sync
            def _(sp):
                for half in range(2):
                    sp.dma_start(W4[half * HID:(half + 1) * HID], A["L0_gnn_W_mlp4"]).then_inc(w4_ld, 16)

                def load(eight, j):
                    half = slice(j // 4 * HID, (j // 4 + 1) * HID)
                    src = hD[eight] if isinstance(eight, int) else hD[bass.ds(eight, 1)].rearrange("a p x -> (a p) x")
                    sp.dma_start(hS[half, j % 4], src[half, j % 4 * P:(j % 4 + 1) * P]).then_inc(h_ld[j], 16)
                for j in range(SLOTS):
                    load(0, j)
                with sp.Fori(0, EIGHTS - 1) as i:
                    for j in range(SLOTS):
                        sp.wait_ge(tpw_ready, i * SLOTS + j + 1)
                        load(i + 1, j)

            @block.scalar
            def _(act):
                act.activation(cnt_words[:, CSPLIT:], zero.to_broadcast([128, AWORDS - CSPLIT]), ACT.Copy).then_inc(z, 1)
                act.activation(at(R3, 8 * WPAD), zero.to_broadcast([128, 8 * WPAD]), ACT.Copy).then_inc(z, 1)

            @block.gpsimd
            def _(pool):
                pool.iota(iotaN, pattern=[[1, NALL]], base=0, channel_multiplier=0,
                          allow_small_or_imprecise_dtypes=True).then_inc(z, 1)
                pool.iota(wsteps, pattern=[[-W, NODES // W + 1]], base=-W, channel_multiplier=0,
                          allow_small_or_imprecise_dtypes=True).then_inc(z, 1)
                for j in range(SLOTS):
                    pool.indirect_dma_start(out=G[j], out_offset=None, in_=upD,
                                            in_offset=bass.IndirectOffsetOnAxis(idx[:, j:j + 1], 0)).then_inc(gathered[j], 16)

                pool.memset(AT[:, CLEARED:], 0.0).then_inc(z, 1)

                def onehots(p, t, ready, eqs, n):
                    pool.wait_ge(eqs, n)
                    pool.sem_inc(passed, 1)
                    e = eq[p]
                    col = slice(t, t + 1) if isinstance(t, int) else bass.ds(t, 1)
                    y = yT[:, col].rearrange("p a m -> p (a m)")
                    v = valT[:, col].rearrange("p a m -> p (a m)")
                    pool.tensor_tensor(Sy[p], e.unsqueeze(1).to_broadcast([P, 4, W]),
                                       y.unsqueeze(2).to_broadcast([P, 4, W]), ALU.mult).then_inc(ready, 1)
                    pool.tensor_tensor(Sw[p][:, 0:3 * W].rearrange("p (m w) -> p m w", m=3),
                                       e.unsqueeze(1).to_broadcast([P, 3, W]),
                                       v[:, 0:3].unsqueeze(2).to_broadcast([P, 3, W]), ALU.mult).then_inc(ready, 1)
                    pool.tensor_tensor(Sw[p][:, 3 * W:5 * W].rearrange("p (w r) -> p w r", r=2),
                                       e.unsqueeze(2).to_broadcast([P, W, 2]),
                                       v[:, 3:5].unsqueeze(1).to_broadcast([P, W, 2]), ALU.mult).then_inc(ready, 1)

                def turn(i, last, look):
                    for j in range(BODY):
                        t, p = i * BODY + j, j % 2
                        onehots(p, t, recv_ready, eq_done, t + 1)
                        if look:
                            further, seen = tile_numbers(pool, t)
                            with pool.If(further > 0):
                                with pool.Fori(0, further) as k:
                                    onehots(p, t, x_ready, x_eq, seen + k + 1)
                        if not (last and j >= BODY - SLOTS):
                            q = j % SLOTS
                            pool.wait_ge(prod_done, t + 2)
                            pool.sem_inc(passed, 1)
                            pool.tensor_copy(ring[:, q:q + 1], idx[:, bass.ds(t + SLOTS, 1)]).then_inc(ring_done, 1)
                            pool.wait_ge(ring_done, t + 1)
                            pool.sem_inc(passed, 1)
                            pool.indirect_dma_start(out=G[q], out_offset=None, in_=upD,
                                                    in_offset=bass.IndirectOffsetOnAxis(ring[:, q:q + 1], 0)).then_inc(gathered[q], 16)
                with pool.Fori(0, TURNS - 1) as i:
                    either(pool, i, lambda look: turn(i, False, look))
                either(pool, TURNS - 1, lambda look: turn(TURNS - 1, True, look))

            @block.vector
            def _(dve):
                dve.sem_inc(prod_done, 1)
                dve.sem_inc(acc_done, 2)
                dve.sem_inc(x_acc, 1)
                dve.memset(cnt_words[:, 0:CSPLIT], 0.0).then_inc(z, 1)
                dve.wait_ge(z, 6)

                def products(turn, j):
                    t, p, g = turn * BODY + j, j % 2, G[j % SLOTS][0:P]
                    col = slice(t, t + 1) if isinstance(t, int) else bass.ds(t, 1)
                    dve.tensor_scalar(eq[p], iota32, rel[:, col], None, ALU.is_equal).then_inc(eq_done, 1)
                    dve.wait_ge(gathered[j % SLOTS], (turn * (BODY // SLOTS) + j // SLOTS) * 16 + 16)
                    dve.wait_ge(tpw_ready, t + 1)
                    tp = bank[TP[p]][0:P, :].rearrange("p (b u) -> p b u", b=4)
                    dve.tensor_tensor(M[p][:, 0:2], tp[:, 0:2],
                                      g[:, 0:MUL].unsqueeze(1).to_broadcast([P, 2, MUL]), ALU.mult)
                    dve.tensor_tensor(M[p][:, 2:8].rearrange("p (b m) u -> p b m u", b=2),
                                      tp[:, 2:4].unsqueeze(2).to_broadcast([P, 2, 3, MUL]),
                                      g[:, MUL:].rearrange("p (m u) -> p m u", m=3).unsqueeze(1).to_broadcast([P, 2, 3, MUL]),
                                      ALU.mult).then_inc(prod_done, 1)
                    dve.tensor_scalar(Ss[p], iotaN, srcT[:, col], None, ALU.is_equal).then_inc(send_ready, 1)

                def accumulate(p, at_node, done):
                    w = bass.ds(at_node, W)
                    dve.tensor_tensor(accT[:, :, w], accT[:, :, w],
                                      bank[MSG[p]][:, 0:8 * W].rearrange("p (b w) -> p b w", b=8), ALU.add)
                    for h in range(2):
                        ps = bank[BLD[p] + h][:, 0:15 * W].rearrange("p (c x) -> p c x", c=5)
                        cs = slice(5 * h, 5 * h + 5)
                        a, c = AT[:, cs, w], CNT[:, cs, bass.ds(at_node * 2, 2 * W)]
                        dve.tensor_tensor(a, a, ps[:, :, 0:W], ALU.add)
                        last = dve.tensor_tensor(c, c, ps[:, :, W:3 * W], ALU.add)
                    last.then_inc(done, 1)

                def settle(i, j, look):
                    t, p = i * BODY + j, j % 2
                    col = slice(t, t + 1) if isinstance(t, int) else bass.ds(t, 1)
                    start = dve.value_load(tab[:, 0, col], min_val=0, max_val=NODES - 1)
                    if look or j == 0:
                        further, seen = tile_numbers(dve, t)
                    dve.wait_ge(visit_done, t + 3)
                    dve.wait_ge(acc_done, t + 2)
                    if look or j == 0:
                        dve.wait_ge(x_acc, seen + 1)
                    accumulate(p, start, acc_done)
                    if look:
                        with dve.If(further > 0):
                            with dve.Fori(0, further) as k:
                                dve.wait_ge(acc_done, t + 3)
                                dve.wait_ge(x_acc, seen + k + 1)
                                dve.tensor_tensor(relx[:, 0:1], rel[:, col], wsteps[:, bass.ds(k, 1)], ALU.add).then_inc(x_rel, 1)
                                dve.wait_ge(x_rel, seen + k + 1)
                                dve.tensor_scalar(eq[p], iota32, relx[:, 0:1], None, ALU.is_equal).then_inc(x_eq, 1)
                                dve.wait_ge(x_done, seen + k + 1)
                                node = nc.s_assert_within(
                                    start + (k + 1) * W, 0, NODES - 1,
                                    skip_runtime_bounds_check_because="the last window starts at or before the largest receiver")
                                accumulate(p, node, x_acc)

                def turn(i, last, look):
                    for j in range(BODY):
                        if not (last and j == BODY - 1):
                            products(i + (j + 1) // BODY, (j + 1) % BODY)
                        settle(i, j, look)

                products(0, 0)
                with dve.Fori(0, TURNS - 1) as i:
                    either(dve, i, lambda look: turn(i, False, look))
                either(dve, TURNS - 1, lambda look: turn(TURNS - 1, True, look))

            @block.tensor
            def _(pe):
                pe.sem_inc(visit_done, 2)
                pe.wait_ge(w4_ld, 32)

                def weights(turn, j):
                    q = j % SLOTS
                    half = slice(q // 4 * HID, (q // 4 + 1) * HID)
                    pe.wait_ge(h_ld[q], (turn * (BODY // SLOTS) + j // SLOTS) * 16 + 16)
                    pe.matmul(bank[TP[j % 2]][0:P, :], hS[half, q % 4], W4[half, :], start=True, stop=True).then_inc(tpw_ready, 1)

                def visit(p, done):
                    msg, m = bank[MSG[p]], M[p]
                    sy = Sy[p].rearrange("p m w -> p (m w)")
                    pe.matmul(msg[:, 0:4 * W], m[:, 0], sy, start=True, stop=True)
                    pe.matmul(msg[:, W:4 * W], m[:, 1], sy[:, W:], start=True, stop=True)
                    for k in range(3):
                        pe.matmul(msg[:, (4 + k) * W:(8 + k) * W], m[:, 2 + k], sy, start=True, stop=True)
                    for k in range(3):
                        pe.matmul(msg[:, 7 * W:(10 - k) * W], m[:, 5 + k], sy[:, (1 + k) * W:], start=(k == 0), stop=(k == 2))
                    for c in range(NT):
                        b, o = bank[BLD[p] + c // 5], c % 5 * 3 * W
                        s = Ss[p][:, c * NP:(c + 1) * NP]
                        pe.matmul(b[:, o:o + 3 * W], s, Sw[p][:, 2 * W:5 * W], start=True, stop=False)
                        pe.matmul(b[:, o:o + W], s, Sw[p][:, 0:W], start=False, stop=False)
                        last = pe.matmul(b[:, o:o + W], s, Sw[p][:, W:2 * W], start=False, stop=True)
                    last.then_inc(done, 1)

                def turn(i, last, look):
                    for j in range(BODY):
                        t = i * BODY + j
                        if not (last and j == BODY - 1):
                            pe.wait_ge(prod_done, t + 1)
                            weights(i + (j + 1) // BODY, (j + 1) % BODY)
                        pe.wait_ge(prod_done, t + 2)
                        pe.wait_ge(send_ready, t + 1)
                        pe.wait_ge(recv_ready, t * 3 + 3)
                        pe.wait_ge(acc_done, t + 1)
                        visit(j % 2, visit_done)
                        if look:
                            further, seen = tile_numbers(pe, t)
                            with pe.If(further > 0):
                                with pe.Fori(0, further) as k:
                                    pe.wait_ge(x_ready, (seen + k) * 3 + 3)
                                    visit(j % 2, x_done)
                weights(0, 0)
                with pe.Fori(0, TURNS - 1) as i:
                    either(pe, i, lambda look: turn(i, False, look))
                either(pe, TURNS - 1, lambda look: turn(TURNS - 1, True, look))

        xs = at(R3 + 8 * WPAD, NT * D).rearrange("p (n f) -> p n f", n=NT)
        ph = Region(R3 + 8 * WPAD + NT * D, WORDS)
        wout = ph.take(4 * 128).rearrange("p (q n) -> p q n", q=4)
        xT1 = ph.take(FC * NALL).rearrange("p (c n) -> p c n", c=FC)
        wg = ph.take(FC * 128).rearrange("p (c n) -> p c n", c=FC)
        wf = ph.take(FC * 128).rearrange("p (c n) -> p c n", c=FC)
        wfT = ph.take(D)
        xw = ph.take(NT * 128).rearrange("p (n f) -> p n f", n=NT)
        hT = ph.take(NALL)
        o_z = sem("o_z"); o_wld = sem("o_wld"); o_ld = [sem(f"o_ld{g}") for g in range(NT // 2)]; o_w = sem("o_w"); o_mm = sem("o_mm"); o_h = sem("o_h")
        g_ld = sem("g_ld")
        with nc.Block() as block:
            @block.sync
            def _(sp):
                sp.dma_start(wout[:, 0:2], A["L0_gnn_W_out0"].rearrange("(q p) n -> p q n", q=2)).then_inc(o_wld, 16)
                sp.dma_start(wout[:, 2:4], A["L0_gnn_W_out1"].rearrange("(q p) n -> p q n", q=2)).then_inc(o_wld, 16)
                for g in range(NT // 2):
                    for n in (2 * g, 2 * g + 1):
                        rows = min(NP, NODES - n * NP)
                        if n == NT - 1:
                            sp.wait_ge(o_z, 1)
                        sp.dma_start(xs[0:rows, n], A["x"][n * NP:n * NP + rows]).then_inc(o_ld[g], 16)
                sp.dma_start(wg, A["L1_gnn_W_gcn"].rearrange("(c p) n -> p c n", c=FC)).then_inc(g_ld, 16)
                sp.dma_start(wf, A["L1_gnn_W_fc"].rearrange("(c p) n -> p c n", c=FC)).then_inc(g_ld, 16)
                sp.dma_start(bgcn, A["L1_gnn_b_gcn"].rearrange("(p a) -> p a", a=1)).then_inc(g_ld, 16)
                sp.dma_start(brow, A["L1_gnn_b_fc"].rearrange("(a n) -> a n", a=1)).then_inc(g_ld, 16)

            @block.gpsimd
            def _(pool):
                pool.memset(xs[:, NT - 1], 0.0).then_inc(o_z, 1)

            @block.tensor
            def _(pe):
                pe.wait_ge(o_w, 1)

                def tile(n):
                    if n >= 2:
                        pe.wait_ge(f_rows, n - 1)
                    ns = slice(n * NP, (n + 1) * NP)
                    for q in range(4):
                        first, second = (0, 7) if q == 0 else (q, 3 + q)
                        o = bank[n % 2][:, q * 128:(q + 1) * 128]
                        pe.matmul(o, accT[:, first, ns], wout[:, 0 if q == 0 else 2], start=True, stop=False)
                        last = pe.matmul(o, accT[:, second, ns], wout[:, 1 if q == 0 else 3], start=False, stop=True)
                    last.then_inc(o_mm, 1)
                norm_tensor(pe, 0, xs, 2, tile)

            @block.scalar
            def _(act):
                norm_scalar(act, 0, xT1, 2)

            @block.vector
            def _(dve):
                dve.wait_ge(o_wld, 32)
                dve.tensor_scalar(wout[:, 1], wout[:, 1], 1.0 / math.sqrt(3.0), None, ALU.mult).then_inc(o_w, 1)
                c = SILU_2MOM / math.sqrt(HID) / math.sqrt(2 * MUL) / 10.0

                def rows(n):
                    dve.wait_ge(o_mm, n + 1)
                    dve.wait_ge(o_ld[n // 2], 32)
                    b = bank[n % 2][:, :]
                    dve.scalar_tensor_tensor(xs[:, n, 0:MUL], b[:, 0:MUL], c, xs[:, n, 0:MUL],
                                             ALU.mult, ALU.add).then_inc(o_h, 1)
                    dve.wait_ge(o_h, n + 1)
                    v = xs[:, n, MUL:].rearrange("p (u m) -> p m u", m=3)
                    dve.scalar_tensor_tensor(v, b[:, MUL:].rearrange("p (m u) -> p m u", m=3), c, v,
                                             ALU.mult, ALU.add).then_inc(f_rows, 1)
                norm_vector(dve, 0, xs, rows)

        xT = at(R3, FC * NALL).rearrange("p (c n) -> p c n", c=FC)
        xnT = at(R3 + FC * NALL, FC * NALL).rearrange("p (c n) -> p c n", c=FC)
        bias_rows = at(R3 + FC * NALL + 2 * FC * D, D)
        raw = [at(R3 + FC * NALL + w * FC * D, FC * D).rearrange("p (c n) -> p c n", c=FC) for w in range(2)]
        g_wt = sem("g_wt"); g_mm = sem("g_mm"); g_ev = sem("g_ev")
        g_hm = sem("g_hm"); g_he = sem("g_he"); g_o = sem("g_o")
        g_b = sem("g_b"); g_bt = sem("g_bt"); g_r = sem("g_r"); s_ld = sem("s_ld"); s_b = sem("s_b")
        with nc.Block() as block:
            @block.sync
            def _(sp):
                sp.dma_start(raw[0], A["L2_gnn_W_neigh"].rearrange("(c p) n -> p c n", c=FC)).then_inc(s_ld, 16)
                sp.dma_start(raw[1], A["L2_gnn_W_self"].rearrange("(c p) n -> p c n", c=FC)).then_inc(s_ld, 16)

            @block.gpsimd
            def _(pool):
                pool.wait_ge(g_bt, 1)
                for n in range(NT):
                    pool.tensor_tensor(xs[:, n], xs[:, n], bias_rows, ALU.add).then_inc(g_r, 1)

            @block.tensor
            def _(pe):
                pe.wait_ge(g_ld, 64)
                for c in range(FC):
                    last = pe.transpose(bank[7][:, c * 128:(c + 1) * 128], wf[:, c], ident)
                last.then_inc(g_wt, 1)
                pe.matmul(bank[6][:, :], onesM[0:1, :], brow, start=True, stop=True).then_inc(g_b, 1)
                for n in range(NT):
                    if n >= 2:
                        pe.wait_ge(g_ev, n - 1)
                    for c in range(FC):
                        last = pe.matmul(bank[n % 2][:, 0:128], xT1[:, c, n * NP:(n + 1) * NP], wg[:, c],
                                         start=(c == 0), stop=(c == FC - 1))
                    last.then_inc(g_mm, 1)
                pe.wait_ge(g_ev, NT)
                for k, (lo, hi) in enumerate(SPANS):
                    for s in range(NT):
                        last = pe.matmul(bank[2 + k][:, 0:hi - lo], xw[:, s], AT[:, s, lo:hi],
                                         start=(s == 0), stop=(s == NT - 1))
                    last.then_inc(g_hm, 1)
                pe.wait_ge(g_he, 3)
                pe.wait_ge(g_wt, 2)

                def tile(n):
                    if n >= 2:
                        pe.wait_ge(f_rows, 1 * NT + n - 1)
                    pe.matmul(bank[n % 2][:, :], hT[:, n * NP:(n + 1) * NP], wfT, start=True, stop=True).then_inc(g_o, 1)
                norm_tensor(pe, 1, xs, 2, tile)

            @block.scalar
            def _(act):
                act.wait_ge(g_wt, 1)
                act.activation(wfT, bank[7][:, :], ACT.Copy).then_inc(g_wt, 1)
                act.wait_ge(g_b, 1)
                act.activation(bias_rows, bank[6][:, :], ACT.Copy).then_inc(g_bt, 1)
                for k, (lo, hi) in enumerate(SPANS):
                    act.wait_ge(g_hm, k + 1)
                    act.activation(hT[:, lo:hi], bank[2 + k][:, 0:hi - lo], ACT.Identity, bias=bgcn).then_inc(g_he, 1)
                norm_scalar(act, 1, xT, 2)

            @block.vector
            def _(dve):
                for n in range(NT):
                    dve.wait_ge(g_mm, n + 1)
                    dve.tensor_copy(xw[:, n], bank[n % 2][:, 0:128]).then_inc(g_ev, 1)

                def rows(n):
                    dve.wait_ge(g_o, n + 1)
                    dve.wait_ge(g_r, n + 1)
                    dve.tensor_tensor(xs[:, n], bank[n % 2][:, :], xs[:, n], ALU.add).then_inc(f_rows, 1)
                norm_vector(dve, 1, xs, rows)

        ph = Region(R3 + 8 * WPAD + NT * D, WORDS)
        wT = [ph.take(FC * D).rearrange("p (c n) -> p c n", c=FC) for _ in range(2)]
        HALF = NALL // 2
        degp = ph.take(HALF)
        bias2 = ph.take(D)
        stage2 = [ph.take(D), at(R3 + 8 * WPAD + NT * D + 2 * FC * D, D)]
        ALONE = 8

        def slot(k):
            return 0 if k < ALONE else k % 2

        def uses(q, k):
            return sum(slot(j) == q for j in range(k))
        bas2 = [ph.take(4 * D, 4 * BASES) for _ in range(2)]
        STEPS2 = 128 // 4
        s_tr = sem("s_tr"); s_te = sem("s_te"); s_nm = sem("s_nm"); s_ne = sem("s_ne")
        s_o = sem("s_o"); s_x = sem("s_x"); s_dp = sem("s_dp"); s_dg = sem("s_dg"); s_di = sem("s_di")
        s_b1 = sem("s_b1"); s_bm = sem("s_bm"); s_bt = sem("s_bt"); s_r = sem("s_r")
        s_cm = sem("s_cm"); s_ct = sem("s_ct")
        d_ld = [sem("d_ld0"), sem("d_ld1")]
        d_mm = sem("d_mm"); d_ev = sem("d_ev"); d_st = [sem("d_st0"), sem("d_st1")]
        NEIGH = (2, 3, 4, 5)
        with nc.Block() as block:
            @block.sync
            def _(sp):
                sp.dma_start(brow, A["L2_gnn_b_self"].rearrange("(a n) -> a n", a=1)).then_inc(s_b, 16)
                sp.dma_start(brow2, A["L2_gnn_b_neigh"].rearrange("(a n) -> a n", a=1)).then_inc(s_b, 16)
                v = A["L3_gnn_basis2"].rearrange("b (q i) o -> (b q) (i o)", q=4)
                for k in range(STEPS2 + 2):
                    if k < STEPS2:
                        if k >= 2:
                            sp.wait_ge(d_mm, k - 1)
                        sp.dma_start(bas2[k % 2], v[:, k * 4 * D:(k + 1) * 4 * D]).then_inc(d_ld[k % 2], 16)
                    if k >= 2:
                        e = k - 2
                        sp.wait_ge(d_ev, e + 1)
                        for s in range(4):
                            sp.dma_start(wD[1].rearrange("m (k s) o -> s m k o", s=4)[s, :, e],
                                         stage2[slot(e)][32 * s:32 * s + 8]).then_inc(d_st[slot(e)], 16)
                for q in range(2):
                    sp.wait_ge(d_st[q], 64 * uses(q, STEPS2))
                for n in range(NT):
                    sp.wait_ge(f_normed, 2 * NT + n + 1)
                    sp.dma_start(x3D[:, n * D:(n + 1) * D], xs[:, n]).then_inc(x_sv, 16)

            @block.gpsimd
            def _(pool):
                pool.wait_ge(s_b, 32)
                pool.tensor_tensor(brow, brow, brow2, ALU.add).then_inc(s_b1, 1)
                pool.wait_ge(s_bt, 1)
                pool.wait_ge(s_nm, FC * 3)
                for n in range(NT):
                    pool.tensor_tensor(xs[:, n], xs[:, n], bias2, ALU.add).then_inc(s_r, 1)

            @block.tensor
            def _(pe):
                def bases(lo, hi):
                    for k in range(lo, hi):
                        pe.wait_ge(d_ld[k % 2], 16 * (k // 2 + 1))
                        if k >= 2:
                            pe.wait_ge(d_ev, k - 1)
                        for s in range(4):
                            last = pe.matmul(bank[6 + k % 2][32 * s:32 * s + 32, :], attL[:, 1],
                                             bas2[k % 2][:, s * D:(s + 1) * D], start=True, stop=True)
                        last.then_inc(d_mm, 1)
                pe.wait_ge(s_ld, 32)
                for w in range(2):
                    for ic in range(FC):
                        k = w * FC + ic
                        if k >= 2:
                            pe.wait_ge(s_te, k - 1)
                        for oc in range(FC):
                            last = pe.transpose(bank[k % 2][:, oc * 128:(oc + 1) * 128],
                                                raw[w][:, oc, ic * 128:(ic + 1) * 128], ident)
                        last.then_inc(s_tr, 1)
                pe.wait_ge(s_te, 2 * FC)
                for g in range(FC * 3):
                    c, (lo, hi) = g // 3, SPANS[g % 3]
                    if g >= 4:
                        pe.wait_ge(s_ne, g - 3)
                    for s in range(NT):
                        last = pe.matmul(bank[NEIGH[g % 4]][:, 0:hi - lo], xs[:, s, c * 128:(c + 1) * 128], AT[:, s, lo:hi],
                                         start=(s == 0), stop=(s == NT - 1))
                        if s == NT - 1:
                            last.then_inc(s_nm, 1)
                        m = g * NT + s
                        bases(m * STEPS2 // (FC * 3 * NT), (m + 1) * STEPS2 // (FC * 3 * NT))
                    if g < 2:
                        pe.wait_ge(s_dp, g + 1)
                        for n in range(NT // 2):
                            last = pe.matmul(bank[0][:, g * NT // 2 + n:g * NT // 2 + n + 1], degp[:, n * NP:(n + 1) * NP],
                                             onesM[:, 0:1], start=True, stop=True)
                        last.then_inc(s_dg, 1)
                    if g == 2:
                        pe.wait_ge(s_b1, 1)
                        pe.matmul(bank[1][:, :], onesM[0:1, :], brow, start=True, stop=True).then_inc(s_bm, 1)
                pe.wait_ge(s_cm, 1)
                pe.wait_ge(s_di, 2)
                pe.transpose(bank[0][0:1, 0:128], cmax, ident).then_inc(s_ct, 1)
                pe.wait_ge(s_cm, 2)
                pe.wait_ge(s_bt, 1)
                pe.wait_ge(s_ne, FC * 3)

                def tile(n):
                    if n >= 2:
                        pe.wait_ge(f_rows, 2 * NT + n - 1)
                    a, b = bank[n % 2][:, :], bank[2 + n % 2][:, :]
                    for c in range(FC):
                        pe.matmul(a, xnT[:, c, n * NP:(n + 1) * NP], wT[0][:, c], start=(c == 0), stop=(c == FC - 1))
                    for c in range(FC):
                        last = pe.matmul(b, xT[:, c, n * NP:(n + 1) * NP], wT[1][:, c], start=(c == 0), stop=(c == FC - 1))
                    last.then_inc(s_o, 1)
                norm_tensor(pe, 2, xs, 4, tile)

            @block.scalar
            def _(act):
                for k in range(2 * FC):
                    act.wait_ge(s_tr, k + 1)
                    act.activation(wT[k // FC][:, k % FC], bank[k % 2][:, :], ACT.Copy).then_inc(s_te, 1)
                for k in range(STEPS2):
                    act.wait_ge(d_mm, k + 1)
                    q = slot(k)
                    if uses(q, k):
                        act.wait_ge(d_st[q], 64 * uses(q, k))
                    elif q == 1:
                        act.wait_ge(s_dg, 2)
                    act.activation(stage2[q], bank[6 + k % 2][:, :], ACT.Copy).then_inc(d_ev, 1)
                    if k == STEPS2 // 2:
                        act.wait_ge(s_bm, 1)
                        act.activation(bias2, bank[1][:, :], ACT.Copy).then_inc(s_bt, 1)
                norm_scalar(act, 2, xT, 4)

            @block.vector
            def _(dve):
                def part(h):
                    if h:
                        dve.wait_ge(s_dg, h)
                    dve.tensor_reduce(degp, AT[:, :, h * HALF:(h + 1) * HALF].rearrange("p c n -> p n c"),
                                      AX.X, ALU.add).then_inc(s_dp, 1)
                part(0)
                for g in range(FC * 3):
                    c, (lo, hi) = g // 3, SPANS[g % 3]
                    dve.wait_ge(s_nm, g + 1)
                    dve.tensor_copy(xnT[:, c, lo:hi], bank[NEIGH[g % 4]][:, 0:hi - lo]).then_inc(s_ne, 1)
                    if g == 0:
                        part(1)
                    if g == 3:
                        dve.wait_ge(s_dg, 2)
                        dve.tensor_scalar(nt1, bank[0][:, 0:NT], 1.0, None, ALU.max).then_inc(s_di, 1)
                        dve.wait_ge(s_di, 1)
                        dve.reciprocal(invdeg, nt1).then_inc(s_di, 1)
                        dve.tensor_reduce(cmax, CNT.rearrange("p c n -> p (c n)"), AX.X, ALU.max).then_inc(s_cm, 1)
                dve.wait_ge(s_ct, 1)
                dve.tensor_reduce(cmax1, bank[0][0:1, 0:128], AX.X, ALU.max).then_inc(s_cm, 1)
                dve.wait_ge(s_cm, 2)
                dve.tensor_scalar(large, cmax1, 4096.0, None, ALU.is_gt).then_inc(s_cm, 1)
                dve.wait_ge(s_di, 2)

                def rows(n):
                    dve.wait_ge(s_o, n + 1)
                    dve.wait_ge(s_r, n + 1)
                    dve.scalar_tensor_tensor(xs[:, n], bank[n % 2][:, :], invdeg[:, n:n + 1], xs[:, n],
                                             ALU.mult, ALU.add).then_inc(s_x, 1)
                    dve.wait_ge(s_x, n + 1)
                    dve.tensor_tensor(xs[:, n], xs[:, n], bank[2 + n % 2][:, :], ALU.add).then_inc(f_rows, 1)
                norm_vector(dve, 2, xs, rows)

        R6 = R3 + FC * NALL
        BT_AT = [R1, (WORDS - NT * NALL) // 8 * 8]
        xTa = at(R3, FC * NALL).rearrange("p (c n) -> p c n", c=FC)
        xTb = at(R2, FC * NALL).rearrange("p (c n) -> p c n", c=FC)
        BTr = [nc.alloc_sbuf_tensor_at(f"counts_r{r}", [128, NT * NALL], F32R, offset=ARENA + 4 * BT_AT[r])[:, :]
               .rearrange("p (c n) -> p c n", c=NT) for r in range(REL)]
        BTw = [at(BT_AT[r], NT * NALL).rearrange("p (c n) -> p c n", c=NT) for r in range(REL)]
        RINGS = 3
        Z_AT = -(-(R2 + FC * NALL + 3 * FC * D) // 8) * 8
        assert Z_AT + RINGS * 4 * 128 <= R3
        Zr = nc.alloc_sbuf_tensor_at("z_parts", [128, RINGS * 4 * 128], F32R, offset=ARENA + 4 * Z_AT)[:, :] \
            .rearrange("p (q r h f) -> p q r h f", q=RINGS, r=REL, h=2)
        Zw = at(Z_AT, RINGS * 4 * 128).rearrange("p (q r h f) -> p q r h f", q=RINGS, r=REL, h=2)
        ph = Region(R6, BT_AT[1])
        cf = [ph.take(2 * NP).rearrange("p (n r) -> p n r", r=2) for _ in range(4)]
        gw = [ph.take(FC * REL).rearrange("p (c r) -> p c r", c=FC) for _ in range(2)]
        bT = [ph.take(FC) for _ in range(2)]
        gate = ph.take(NT * REL).rearrange("p (n r) -> p n r", n=NT)
        w_at = [ph.at, R2 + FC * NALL]
        wrel = [at(w, 2 * FC * D).rearrange("p (r c n) -> p r c n", r=REL, c=FC) for w in w_at]
        root = [at(w + 2 * FC * D, FC * D).rearrange("p (c n) -> p c n", c=FC) for w in w_at]
        assert w_at[0] + 3 * FC * D <= BT_AT[1]
        x3 = at(w_at[0], NT * D).rearrange("p (n f) -> p n f", n=NT)
        x_bk = sem("x_bk")
        w_ld = [sem("w_ld0"), sem("w_ld1")]
        c_cv = [sem(f"c_cv{k}") for k in range(4)]; c_tr = sem("c_tr"); c_ev = [sem("c_ev0"), sem("c_ev1")]

        def by_size(eng, program):
            over = eng.value_load(large, min_val=0, max_val=1)
            with eng.If(over > 0):
                program(True)
            with eng.Else():
                program(False)

        def load_layer(sp, layer):
            sp.dma_start(gw[layer], A[f"gate_w{layer + 1}"]).then_inc(w_ld[layer], 16)
            sp.dma_start(bT[layer], A[f"bias{layer + 1}_cols"]).then_inc(w_ld[layer], 16)
            for r in range(REL):
                sp.dma_start(wrel[layer][:, r], wD[layer, 4 * r:4 * r + 4].rearrange("q i o -> i q o")).then_inc(w_ld[layer], 16)
            sp.dma_start(root[layer], A[f"L3_gnn_root{layer + 1}"].rearrange("(c p) n -> p c n", c=FC)).then_inc(w_ld[layer], 16)

        with nc.Block() as block:
            @block.sync
            def _(sp):
                load_layer(sp, 0)

            def convert(copy, eng, k):
                s, d = k % NT, k // NT
                if k >= 4:
                    eng.wait_ge(c_tr, k - 3)
                copy(cf[k % 4], CNT[:, s, 2 * d * NP:2 * (d + 1) * NP]
                     .rearrange("p (n r) -> p n r", r=2)).then_inc(c_cv[k % 4], 1)

            @block.gpsimd
            def _(pool):
                for k in range(0, NT * NT, 4):
                    convert(pool.tensor_copy, pool, k)

            @block.tensor
            def _(pe):
                for k in range(NT * NT):
                    pe.wait_ge(c_cv[k % 4], k // 4 + 1)
                    if k >= 8:
                        pe.wait_ge(c_ev[k % 2], (k - 8) // 2 + 1)
                    for r in range(REL):
                        last = pe.transpose(bank[k % 8][:, r * NP:(r + 1) * NP], cf[k % 4][:, :, r], ident)
                    last.then_inc(c_tr, 1)

            def counts(copy, eng, first, wide):
                for k in range(NT * NT + 4):
                    if k < NT * NT and ((k % 4 == 2 - first) or (k % 4 == 3 and k // 4 % 2 == first)):
                        convert(copy, eng, k)
                    e = k - 4
                    if e >= 0 and e % 2 == first:
                        s, d = e % NT, e // NT
                        eng.wait_ge(c_tr, e + 1)
                        for r in range(REL):
                            dst = (BTw if wide else BTr)[r][:, d, s * NP:(s + 1) * NP]
                            last = copy(dst, bank[e % 8][:, r * NP:(r + 1) * NP])
                        last.then_inc(c_ev[first], 1)

            @block.vector
            def _(dve):
                dve.wait_ge(x_sv, 16 * NT)
                by_size(dve, lambda wide: counts(dve.tensor_copy, dve, 0, wide))

            @block.scalar
            def _(act):
                act.wait_ge(x_sv, 16 * NT)
                by_size(act, lambda wide: counts(lambda dst, src: act.activation(dst, src, ACT.Copy), act, 1, wide))

        for layer in range(2):
            tag = f"r{layer}"
            xin, xout = (xTa, xTb) if layer == 0 else (xTb, xTa)
            g_mm = sem(tag + "_gates"); g_sg = sem(tag + "_sigmoid")
            z_mm = sem(tag + "_z_ready"); z_hi = sem(tag + "_z_high"); z_lo = sem(tag + "_z_low")
            z_us = sem(tag + "_z_used"); o_mm = sem(tag + "_sums_ready"); o_ev = sem(tag + "_sums_out")
            ITEMS = FC * NT
            with nc.Block() as block:
                @block.sync
                def _(sp):
                    if layer == 0:
                        load_layer(sp, 1)
                    else:
                        sp.dma_start(at(w_at[0], NT * D), x3D).then_inc(x_bk, 16)

                @block.tensor
                def _(pe):
                    pe.wait_ge(w_ld[layer], 80)
                    for n in range(NT):
                        for c in range(FC):
                            last = pe.matmul(bank[7][:, 2 * n:2 * n + 2], xin[:, c, n * NP:(n + 1) * NP], gw[layer][:, c],
                                             start=(c == 0), stop=(c == FC - 1))
                    last.then_inc(g_mm, 1)

                    def transformed(i):
                        c, n = i // NT, i % NT
                        if i == 1:
                            pe.wait_ge(g_sg, 1)
                        if i >= 2:
                            pe.wait_ge(z_lo, i - 1)
                        for k in range(FC):
                            last = pe.matmul(bank[6 + i % 2][:, 0:2 * 128], xin[:, k, n * NP:(n + 1) * NP],
                                             wrel[layer][:, :, k, c * 128:(c + 1) * 128],
                                             start=(k == 0), stop=(k == FC - 1))
                        last.then_inc(z_mm, 1)

                    def program(wide):
                        transformed(0)
                        for i in range(ITEMS):
                            c, n = i // NT, i % NT
                            if i + 1 < ITEMS:
                                transformed(i + 1)
                            sums = bank[3 * (c % 2):3 * (c % 2) + 3]
                            if n == 0:
                                if c >= 2:
                                    pe.wait_ge(o_ev, 3 * (c - 1))
                                for k in range(FC):
                                    for o, (lo, hi) in zip(sums, SPANS):
                                        pe.matmul(o[:, 0:hi - lo], root[layer][:, k, c * 128:(c + 1) * 128],
                                                  xin[:, k, lo:hi], start=(k == 0), stop=False)
                            pe.wait_ge(z_lo, i + 1)
                            for r in range(REL):
                                for h in range(1 if wide else 2):
                                    z = (Zw if wide else Zr)[:, i % RINGS, r, h]
                                    end = n == NT - 1 and r == REL - 1 and (wide or h == 1)
                                    for o, (lo, hi) in zip(sums, SPANS):
                                        last = pe.matmul(o[:, 0:hi - lo], z, (BTw if wide else BTr)[r][:, n, lo:hi],
                                                         start=False, stop=end)
                            last.then_inc(z_us, 1)
                            if n == NT - 1:
                                pe.wait_ge(z_us, i + 1)
                                pe.sem_inc(o_mm, 1)
                    by_size(pe, program)

                @block.scalar
                def _(act):
                    act.wait_ge(w_ld[layer], 80)
                    act.wait_ge(g_mm, 1)
                    act.activation(gate.rearrange("p n r -> p (n r)"), bank[7][:, 0:REL * NT], ACT.Sigmoid).then_inc(g_sg, 1)
                    act.wait_ge(g_sg, 1)

                    def program(wide):
                        for i in range(ITEMS + 1):
                            if i < ITEMS:
                                act.wait_ge(z_mm, i + 1)
                                if i >= RINGS:
                                    act.wait_ge(z_us, i - RINGS + 1)
                                for r in range(REL):
                                    act.activation((Zw if wide else Zr)[:, i % RINGS, r, 0],
                                                   bank[6 + i % 2][:, r * 128:(r + 1) * 128], ACT.Copy,
                                                   scale=gate[:, i % NT, r:r + 1]).then_inc(z_hi, 1)
                            if i and i % NT == 0:
                                c = i // NT - 1
                                act.wait_ge(o_mm, c + 1)
                                for o, (lo, hi) in zip(bank[3 * (c % 2):3 * (c % 2) + 3], SPANS):
                                    act.activation(xout[:, c, lo:hi], o[:, 0:hi - lo],
                                                   ACT.Relu if layer == 0 else ACT.Identity,
                                                   bias=bT[layer][:, c:c + 1]).then_inc(o_ev, 1)
                    by_size(act, program)

                @block.vector
                def _(dve):
                    dve.wait_ge(g_sg, 1)

                    def program(wide):
                        for i in range(ITEMS):
                            dve.wait_ge(z_hi, 2 * i + 2)
                            if wide:
                                dve.sem_inc(z_lo, 1)
                                continue
                            for r in range(REL):
                                last = dve.scalar_tensor_tensor(Zr[:, i % RINGS, r, 1], bank[6 + i % 2][:, r * 128:(r + 1) * 128],
                                                                gate[:, i % NT, r:r + 1], Zr[:, i % RINGS, r, 0].bitcast(F32),
                                                                ALU.mult, ALU.subtract)
                            last.then_inc(z_lo, 1)
                    by_size(dve, program)

        l_tr = sem("l_tr"); f_st = sem("f_st")
        with nc.Block() as block:
            @block.sync
            def _(sp):
                for g in range(NT // 2):
                    sp.wait_ge(f_normed, 3 * NT + 2 * g + 2)
                    for n in (2 * g, 2 * g + 1):
                        rows = min(NP, NODES - n * NP)
                        sp.dma_start(out[n * NP:n * NP + rows], x3[0:rows, n]).then_inc(f_st, 16)
                sp.wait_ge(f_st, 16 * NT)

            @block.tensor
            def _(pe):
                for n in range(NT):
                    if n >= 4:
                        pe.wait_ge(f_rows, 3 * NT + n - 3)
                    for c in range(FC):
                        last = pe.transpose(bank[n % 4][:, c * 128:(c + 1) * 128], xTa[:, c, n * NP:(n + 1) * NP], ident)
                    last.then_inc(l_tr, 1)

            @block.scalar
            def _(act):
                norm_scalar(act, 3)

            @block.vector
            def _(dve):
                dve.wait_ge(x_bk, 16)

                def rows(n):
                    dve.wait_ge(l_tr, n + 1)
                    dve.tensor_tensor(x3[:, n], bank[n % 4][:, :], x3[:, n], ALU.add).then_inc(f_rows, 1)
                norm_vector(dve, 3, x3, rows)


_NAMES = ["x", "src", "dst", "edge_attr_4", "edge_attr_8", "edge_type_2", "edge_weight",
          "L0_gnn_W_up0", "L0_gnn_W_up1", "L0_gnn_W_mlp1", "L0_gnn_W_mlp2", "L0_gnn_W_mlp3", "L0_gnn_W_mlp4",
          "L0_gnn_W_out0", "L0_gnn_W_out1", "L1_gnn_W_gcn", "L1_gnn_b_gcn", "L1_gnn_W_fc", "L1_gnn_b_fc",
          "L2_gnn_W_self", "L2_gnn_b_self", "L2_gnn_W_neigh", "L2_gnn_b_neigh",
          "L3_gnn_basis1", "L3_gnn_root1", "L3_gnn_basis2", "L3_gnn_root2"]


def kernel(**inputs):
    import numpy as np
    import concourse.bacc as bacc
    from concourse.bass_utils import run_bass_kernel_spmd

    nc = bacc.Bacc("TRN2", target_bir_lowering=False, num_devices=1)
    host = {name: np.ascontiguousarray(inputs[name]) for name in _NAMES}
    for k in (1, 2):
        host[f"att{k}_rep"] = np.ascontiguousarray(np.repeat(np.asarray(inputs[f"L3_gnn_att{k}"]).T, 4, axis=0))
        gate = np.asarray(inputs[f"L3_gnn_gate_w{k}"]).reshape(REL, FC, 128)
        host[f"bias{k}_cols"] = np.ascontiguousarray(np.asarray(inputs[f"L3_gnn_bias{k}"]).reshape(FC, 128).T)
        host[f"gate_w{k}"] = np.ascontiguousarray(gate.transpose(2, 1, 0))
    host["ident"] = np.eye(128, dtype=np.float32)
    host["mask4"] = np.tile(np.tile(np.eye(4, dtype=np.float32), (BASES, 1)), (1, REL))
    aps = {}
    arrays = {}
    for name, a in host.items():
        arrays["in_" + name] = a
        aps[name] = nc.dram_tensor("in_" + name, a.shape, mybir.dt.from_np(a.dtype), kind="ExternalInput").ap()
    out = nc.dram_tensor("out_0", (NODES, D), F32, kind="ExternalOutput").ap()
    gnn_program(nc, aps, out)
    r = run_bass_kernel_spmd(nc, [arrays], core_ids=[0])
    return r.results[0]["out_0"]
```
